# Optimizing a Trainium2 kernel written in Bass

```python
import numpy as np
import jax
import jax.numpy as jnp

def _softmax(x, axis=-1):
    return jax.nn.softmax(x, axis=axis)
def _gelu(x):
    return jax.nn.gelu(x, approximate=True)
def _silu(x):
    return jax.nn.silu(x)
def _sigmoid(x):
    return jax.nn.sigmoid(x)
def _layernorm(x, axis=-1, eps=1e-5):
    m = jnp.mean(x, axis=axis, keepdims=True)
    v = jnp.var(x, axis=axis, keepdims=True)
    return (x - m) / jnp.sqrt(v + eps)
def _scatter_add(tgt, idx, src, axis=0):
    return tgt.at[idx].add(src)
def _segment_sum(src, seg, n):
    return jax.ops.segment_sum(src, seg, n)

kernel_name = 'mk_conv_preact_d2_conv_nchw256_f6e5a5'

def setup_inputs(seed: int = 0):
    np.random.seed(seed)
    _w = jnp.asarray
    def _rec_inputs():
        import jax
        import jax.numpy as jnp
        _gk = jax.random.key(seed)
        x = -0.0006537 + 1.001 * jax.random.normal(jax.random.fold_in(_gk, 1), (1, 256, 96, 96), jnp.float32)
        return x
    x = _rec_inputs()
    def _L0_conv_setup():
        import jax, jax.numpy as jnp
        import numpy as np
        CUTOFF = 0.05

        def _freq_filter(x_chw, filter_type):
            x = jax.lax.stop_gradient(x_chw)
            C, H, W = x.shape
            a = jnp.abs(x)
            mn = a.min(axis=(1, 2), keepdims=True)
            ptp = a.max(axis=(1, 2), keepdims=True) - mn
            q = jnp.floor(255.0 * (a - mn) / ptp)
            f = jnp.fft.fftshift(jnp.fft.fft2(q), axes=(-2, -1))
            crow, ccol = (H // 2, W // 2)
            dr, dc = (int(CUTOFF * crow), int(CUTOFF * ccol))
            m = jnp.zeros((H, W), dtype=q.dtype)
            m = m.at[crow - dr:crow + dr, ccol - dc:ccol + dc].set(1.0)
            if filter_type == 'low_pass':
                m = 1.0 - m
            out = jnp.abs(jnp.fft.ifft2(jnp.fft.ifftshift(f * m, axes=(-2, -1))))
            return out.astype(x_chw.dtype)

        def _conv1x1(x, w, b):
            return jnp.einsum('oc,bchw->bohw', w, x) + b[None, :, None, None]
        key = jax.random.key(seed)
        ks = jax.random.split(key, 7)
        B, C, H, W = (1, 256, 96, 96)
        fuse = jax.random.normal(ks[0], (B, C, H, W), dtype=jnp.float32)
        s = 1.0 / np.sqrt(C)
        Wq = jax.random.normal(ks[1], (C, C), dtype=jnp.float32) * s
        bq = jax.random.normal(ks[2], (C,), dtype=jnp.float32) * 0.01
        Wk = jax.random.normal(ks[3], (C, C), dtype=jnp.float32) * s
        bk = jax.random.normal(ks[4], (C,), dtype=jnp.float32) * 0.01
        Wv = jax.random.normal(ks[5], (C, C), dtype=jnp.float32) * s
        bv = jax.random.normal(ks[6], (C,), dtype=jnp.float32) * 0.01
        return {'fuse': fuse, 'Wq': Wq, 'bq': bq, 'Wk': Wk, 'bk': bk, 'Wv': Wv, 'bv': bv}
    _L0_conv_all = _L0_conv_setup()
    _L0_conv_in = {k: v for k, v in _L0_conv_all.items() if k in ('Wq', 'bq', 'Wk', 'bk', 'Wv', 'bv', )}
    del _L0_conv_all

    def _L1_conv_setup():
        import jax, jax.numpy as jnp
        import numpy as np
        K = 4

        def grid_sample_bilinear_zeros(img, grid):
            b, c, H, W = img.shape
            h, w = (grid.shape[1], grid.shape[2])
            ix = (grid[..., 0] + 1.0) * (W * 0.5) - 0.5
            iy = (grid[..., 1] + 1.0) * (H * 0.5) - 0.5
            x0 = jnp.floor(ix)
            y0 = jnp.floor(iy)
            wx1 = ix - x0
            wx0 = 1.0 - wx1
            wy1 = iy - y0
            wy0 = 1.0 - wy1
            x0i = x0.astype(jnp.int32)
            y0i = y0.astype(jnp.int32)
            x1i = x0i + 1
            y1i = y0i + 1
            imgf = img.reshape(b, c, H * W)
            N = h * w

            def gather(xi, yi, wgt):
                valid = (xi >= 0) & (xi < W) & (yi >= 0) & (yi < H)
                xc = jnp.clip(xi, 0, W - 1)
                yc = jnp.clip(yi, 0, H - 1)
                idx = (yc * W + xc).reshape(b, 1, N)
                g = jnp.take_along_axis(imgf, jnp.broadcast_to(idx, (b, c, N)), axis=2)
                wv = (wgt * valid.astype(img.dtype)).reshape(b, 1, N)
                return g * wv
            out = gather(x0i, y0i, wx0 * wy0) + gather(x1i, y0i, wx1 * wy0) + gather(x0i, y1i, wx0 * wy1) + gather(x1i, y1i, wx1 * wy1)
            return out.reshape(b, c, h, w)
        key = jax.random.key(seed)
        ks = jax.random.split(key, 8)
        b, c, h, w = (8, 256, 96, 96)
        out_ch = 256
        x = jax.random.normal(ks[0], (b, c, h, w), dtype=jnp.float32)
        Wc = jax.random.normal(ks[1], (out_ch, c), dtype=jnp.float32) * 0.02
        bc = jax.random.normal(ks[2], (out_ch,), dtype=jnp.float32) * 0.02
        Woff = jax.random.normal(ks[3], (K, 2, c), dtype=jnp.float32) * 0.02
        boff = jax.random.normal(ks[4], (K, 2), dtype=jnp.float32) * 0.02
        Wwt = jax.random.normal(ks[5], (K, c), dtype=jnp.float32) * 0.02
        bwt = jax.random.normal(ks[6], (K,), dtype=jnp.float32) * 0.02
        return {'x': x, 'Wc': Wc, 'bc': bc, 'Woff': Woff, 'boff': boff, 'Wwt': Wwt, 'bwt': bwt}
    _L1_conv_all = _L1_conv_setup()
    _L1_conv_in = {k: v for k, v in _L1_conv_all.items() if k in ('Wc', 'bc', 'Woff', 'boff', 'Wwt', 'bwt', )}
    del _L1_conv_all

    return {
        "x": x,
        "L0_conv_Wq": _L0_conv_in["Wq"],
        "L0_conv_bq": _L0_conv_in["bq"],
        "L0_conv_Wk": _L0_conv_in["Wk"],
        "L0_conv_bk": _L0_conv_in["bk"],
        "L0_conv_Wv": _L0_conv_in["Wv"],
        "L0_conv_bv": _L0_conv_in["bv"],
        "L1_conv_Wc": _L1_conv_in["Wc"],
        "L1_conv_bc": _L1_conv_in["bc"],
        "L1_conv_Woff": _L1_conv_in["Woff"],
        "L1_conv_boff": _L1_conv_in["boff"],
        "L1_conv_Wwt": _L1_conv_in["Wwt"],
        "L1_conv_bwt": _L1_conv_in["bwt"],
    }

def reference(x, L0_conv_Wq, L0_conv_bq, L0_conv_Wk, L0_conv_bk, L0_conv_Wv, L0_conv_bv, L1_conv_Wc, L1_conv_bc, L1_conv_Woff, L1_conv_boff, L1_conv_Wwt, L1_conv_bwt):
    import jax
    import jax.numpy as jnp
    def _L0_conv_ref(fuse, Wq, bq, Wk, bk, Wv, bv):
        import jax, jax.numpy as jnp
        import numpy as np
        CUTOFF = 0.05

        def _freq_filter(x_chw, filter_type):
            x = jax.lax.stop_gradient(x_chw)
            C, H, W = x.shape
            a = jnp.abs(x)
            mn = a.min(axis=(1, 2), keepdims=True)
            ptp = a.max(axis=(1, 2), keepdims=True) - mn
            q = jnp.floor(255.0 * (a - mn) / ptp)
            f = jnp.fft.fftshift(jnp.fft.fft2(q), axes=(-2, -1))
            crow, ccol = (H // 2, W // 2)
            dr, dc = (int(CUTOFF * crow), int(CUTOFF * ccol))
            m = jnp.zeros((H, W), dtype=q.dtype)
            m = m.at[crow - dr:crow + dr, ccol - dc:ccol + dc].set(1.0)
            if filter_type == 'low_pass':
                m = 1.0 - m
            out = jnp.abs(jnp.fft.ifft2(jnp.fft.ifftshift(f * m, axes=(-2, -1))))
            return out.astype(x_chw.dtype)

        def _conv1x1(x, w, b):
            return jnp.einsum('oc,bchw->bohw', w, x) + b[None, :, None, None]
        B, C, H, W = fuse.shape
        scale = 1.0 / C ** 0.5
        FQ = jnp.broadcast_to(_freq_filter(fuse[0], 'high_pass'), fuse.shape)
        FK = jnp.broadcast_to(_freq_filter(fuse[0], 'low_pass'), fuse.shape)
        fuse_Query = _conv1x1(FQ, Wq, bq).reshape(B, C, H * W)
        fuse_Q_mask = fuse_Query.reshape(B * H, C * W)
        fuse_Query_t = jnp.transpose(fuse_Query, (0, 2, 1))
        fuse_Key = _conv1x1(FK, Wk, bk).reshape(B, C, H * W)
        Fuse_Q_mask = jnp.max(fuse_Q_mask, axis=0, keepdims=True)
        mask_KQ = jnp.einsum('bnc,bcm->bnm', fuse_Query_t, fuse_Key) * scale
        mask_KQ = jax.nn.softmax(mask_KQ, axis=0)
        mask_KQ = jnp.max(mask_KQ, axis=1)
        mask_KQ = mask_KQ.reshape(-1, W)
        mask_KQ = jnp.max(mask_KQ, axis=-1, keepdims=True)
        mask = (mask_KQ @ Fuse_Q_mask).reshape(B, C, H, W)
        fuse_Value = _conv1x1(fuse, Wv, bv)
        return fuse_Value + fuse_Value * mask

    def _L1_conv_ref(x, Wc, bc, Woff, boff, Wwt, bwt):
        import jax, jax.numpy as jnp
        import numpy as np
        K = 4

        def grid_sample_bilinear_zeros(img, grid):
            b, c, H, W = img.shape
            h, w = (grid.shape[1], grid.shape[2])
            ix = (grid[..., 0] + 1.0) * (W * 0.5) - 0.5
            iy = (grid[..., 1] + 1.0) * (H * 0.5) - 0.5
            x0 = jnp.floor(ix)
            y0 = jnp.floor(iy)
            wx1 = ix - x0
            wx0 = 1.0 - wx1
            wy1 = iy - y0
            wy0 = 1.0 - wy1
            x0i = x0.astype(jnp.int32)
            y0i = y0.astype(jnp.int32)
            x1i = x0i + 1
            y1i = y0i + 1
            imgf = img.reshape(b, c, H * W)
            N = h * w

            def gather(xi, yi, wgt):
                valid = (xi >= 0) & (xi < W) & (yi >= 0) & (yi < H)
                xc = jnp.clip(xi, 0, W - 1)
                yc = jnp.clip(yi, 0, H - 1)
                idx = (yc * W + xc).reshape(b, 1, N)
                g = jnp.take_along_axis(imgf, jnp.broadcast_to(idx, (b, c, N)), axis=2)
                wv = (wgt * valid.astype(img.dtype)).reshape(b, 1, N)
                return g * wv
            out = gather(x0i, y0i, wx0 * wy0) + gather(x1i, y0i, wx1 * wy0) + gather(x0i, y1i, wx0 * wy1) + gather(x1i, y1i, wx1 * wy1)
            return out.reshape(b, c, h, w)
        b, c, h, w = x.shape
        proj = jnp.einsum('bchw,oc->bohw', x, Wc) + bc[None, :, None, None]
        flows = jnp.einsum('bchw,koc->kbohw', x, Woff) + boff[:, None, :, None, None]
        flows = jnp.transpose(flows, (0, 1, 3, 4, 2))
        logits = jnp.einsum('bchw,kc->bkhw', x, Wwt) + bwt[None, :, None, None]
        weights = jax.nn.softmax(logits, axis=1)
        gy, gx = jnp.meshgrid(jnp.arange(h, dtype=x.dtype), jnp.arange(w, dtype=x.dtype), indexing='ij')
        base = jnp.stack((gx, gy), axis=-1)
        vgrid = base[None, None] + flows
        vx = 2.0 * vgrid[..., 0] / max(w - 1, 1) - 1.0
        vy = 2.0 * vgrid[..., 1] / max(h - 1, 1) - 1.0
        vgrid_scaled = jnp.stack((vx, vy), axis=-1)
        feats = jax.vmap(lambda g: grid_sample_bilinear_zeros(proj, g))(vgrid_scaled)
        out = jnp.einsum('kbohw,bkhw->bohw', feats, weights)
        return out

    def _gn(v, G=32, eps=1e-5):
        B_, C_, H_, W_ = v.shape
        g = v.reshape(B_, G, C_ // G, H_, W_)
        m = jnp.mean(g, axis=(2, 3, 4), keepdims=True)
        s = jnp.var(g, axis=(2, 3, 4), keepdims=True)
        return ((g - m) / jnp.sqrt(s + eps)).reshape(v.shape)

    def _ln_c(v, eps=1e-6):
        m = jnp.mean(v, axis=1, keepdims=True)
        s = jnp.var(v, axis=1, keepdims=True)
        return (v - m) / jnp.sqrt(s + eps)

    def _ln_t(v, eps=1e-5):
        m = jnp.mean(v, axis=-1, keepdims=True)
        s = jnp.var(v, axis=-1, keepdims=True)
        return (v - m) / jnp.sqrt(s + eps)

    def _to_tokens(v):
        B_, C_, H_, W_ = v.shape
        return v.reshape(B_, C_, H_ * W_).transpose(0, 2, 1)
    def _from_tokens(t, like):
        B_, C_, H_, W_ = like.shape
        return t.transpose(0, 2, 1).reshape(B_, C_, H_, W_)

    x = x + _L0_conv_ref(_gn(x), L0_conv_Wq, L0_conv_bq, L0_conv_Wk, L0_conv_bk, L0_conv_Wv, L0_conv_bv)
    x = x + _L1_conv_ref(_gn(x), L1_conv_Wc, L1_conv_bc, L1_conv_Woff, L1_conv_boff, L1_conv_Wwt, L1_conv_bwt)
    return x


_drawn_inputs = setup_inputs


def setup_inputs(seed=0):
    import zlib

    import numpy as np

    out = dict(_drawn_inputs(seed))
    spreads = {}
    factors = {'L0_conv_bq': 200.0,
     'L0_conv_bv': 5.404,
     'L1_conv_Wc': 37.951,
     'L1_conv_bc': 200.0,
     'L1_conv_Woff': 38.835,
     'L1_conv_boff': 64.0,
     'L1_conv_Wwt': 49.393,
     'L1_conv_bwt': 200.0}
    for name, (base, spread) in spreads.items():
        noise = np.random.default_rng([zlib.crc32(name.encode()), seed]).standard_normal(out[name].shape)
        drawn = base * np.exp(spread * noise) if base else spread * noise
        out[name] = jnp.asarray(drawn.astype(out[name].dtype))
    for name, factor in factors.items():
        out[name] = (out[name] * factor).astype(out[name].dtype)
    return out
```

```python
from contextlib import ExitStack

import numpy as np

import concourse.bass as bass
from concourse import mybir

F32 = mybir.dt.float32
BF16 = mybir.dt.bfloat16
U32 = mybir.dt.uint32
ALU = mybir.AluOpType
ACT = mybir.ActivationFunctionType
AX_X = mybir.AxisListType.X
ds = bass.ds

P = 128
C, H, W = 256, 96, 96
HW = H * W
CB = C // P
NT = HW // P
GROUPS = 32
PER_GROUP = C // GROUPS
EPS = 1e-5
HEADS = 4
NFLOW = 3 * HEADS
NPROJ = C + NFLOW
LEVELS = 255.0
ROUND = 1.5 * 2.0 ** 23
CHUNK = 512
NCH = HW // CHUNK
QCH = 768
NQ = HW // QCH
QT = QCH // P
CUT = int(0.05 * (H // 2))
SPLITS = 3
ROWS = 32
STACK = SPLITS * ROWS
BLOCKS = 8
THIRD = HW // 3
THIRD_TILES = THIRD // P


def bf16_bits(a):
    u = np.ascontiguousarray(a, np.float32).view(np.uint32).astype(np.uint64)
    return ((u + 0x7FFF + ((u >> 16) & 1)) >> 16).astype(np.uint16)


def from_bits(b):
    return (b.astype(np.uint32) << 16).view(np.float32)


def split3(a):
    out = []
    for _ in range(SPLITS):
        out.append(bf16_bits(a.astype(np.float32)))
        a = a - from_bits(out[-1])
    return out


def shape_constants():
    freqs = range(-CUT, CUT)
    alone = [(a, b) for a in freqs for b in freqs if -CUT in (a, b)]
    pairs = [(a, b) for a in range(CUT) for b in range(-CUT + 1, CUT) if a > 0 or b > 0]
    yy, xx = np.divmod(np.arange(HW), W)
    n_a, n_p = len(alone), len(pairs)

    def phase(ab):
        return 2 * np.pi * ((ab[0] * yy + ab[1] * xx) % W) / W

    fns = [np.cos(phase(f)) for f in alone] + [np.sin(phase(f)) for f in alone]
    fns += [np.cos(phase(f)) for f in pairs] + [np.sin(phase(f)) for f in pairs] + [np.ones(HW)]
    n = len(fns)
    assert n <= ROWS
    basis = np.zeros((ROWS, HW))
    basis[:n] = fns
    b1, b2, b3 = split3(basis)
    ana = np.zeros((P, NT, P), np.uint16)
    ana[:, :, :STACK] = np.stack([b1, b2, b3], 0).reshape(STACK, NT, P).transpose(2, 1, 0)
    syn = np.stack([np.concatenate([b1, b1, b1]), np.concatenate([b2, b3, b2])], 1)
    sel = np.zeros((STACK, 2, STACK), np.float32)
    for s in range(SPLITS):
        for to in range(SPLITS):
            for j in range(n):
                sel[s * ROWS + j, 0, to * ROWS + j] = 2.0 if 2 * n_a <= j < 2 * n_a + 2 * n_p else 1.0
            for j in range(n_a):
                sel[s * ROWS + j, 1, to * ROWS + n_a + j] = 1.0
                sel[s * ROWS + n_a + j, 1, to * ROWS + j] = -1.0
    group = np.zeros((P, P), np.float32)
    for c in range(P):
        group[c, c // PER_GROUP * PER_GROUP:(c // PER_GROUP + 1) * PER_GROUP] = 1.0 / PER_GROUP
    pick = np.zeros((P, 3, C), np.float32)
    for s in range(SPLITS):
        for t in range(3):
            for c in range(C):
                pick[s * BLOCKS + 3 * (3 * c + t) % BLOCKS, t, c] = 1.0
    grid = np.zeros((P, NT, HEADS, 2), np.float32)
    gx, gy = xx.reshape(NT, P).T, yy.reshape(NT, P).T
    grid[..., 0] = (gx * (W / (W - 1.0)) - 0.5)[:, :, None]
    grid[..., 1] = (gy * (H / (H - 1.0)) - 0.5)[:, :, None]
    return {
        "ana": ana, "syn": np.ascontiguousarray(syn), "sel": sel, "group": group,
        "pick": bf16_bits(pick), "grid": grid.reshape(P, NT, 2 * HEADS),
        "ident": np.eye(P, dtype=np.float32), "identb": bf16_bits(np.eye(P)),
    }


def build(nc, x, WqT, bq, WvT, bv, WpT, bp, out):
    const = shape_constants()
    k_ = {n: nc.inline_tensor(a, name="const_" + n).ap() for n, a in const.items()}
    x_c = x.rearrange("a (t p) h w -> t p (a h w)", p=P)
    out_c = out.rearrange("a (t p) h w -> p (a t) (h w)", p=P)
    table = nc.dram_tensor("table", (HW + W, 2 * C), F32, kind="Internal").ap()

    with ExitStack() as ctx:
        def sb(name, shape, dt=F32):
            return ctx.enter_context(nc.sbuf_tensor(name, shape, dt))

        def sem(name):
            return ctx.enter_context(nc.semaphore(name))

        ps = ctx.enter_context(nc.psum_tensor("ps", [P, 8, CHUNK], F32))
        xs = sb("xs", [P, CB, HW])
        ident = sb("ident", [P, P])
        identb = sb("identb", [P, P], BF16)
        group = sb("group", [P, P])
        small = sb("small", [P, 256])
        wp = sb("wp", [P, CB, NPROJ])
        link_sem = sem("link_sem")
        linked = [0]

        def link(eng, ins):
            linked[0] += 1
            ins.then_inc(link_sem, 1)
            eng.wait_ge(link_sem, linked[0])

        col = {}

        def column(name, n=1):
            if name not in col:
                col[name] = (sum(w for _, w in col.values()), n)
            a, w = col[name]
            return small[:, a:a + w]

        for nme in ("mean", "var", "rstd", "nmr", "mg", "mn", "sc", "bvp", "mean1", "var1", "rstd1", "nmr1"):
            column(nme, CB)
        for nme in ("d", "e", "mx_", "ptp", "rp"):
            column(nme, CB)
        column("mv", 2 * CB)
        column("minus_round", 1)
        column("minus_one", 1)
        column("one", 1)
        column("eye3", 3)

        with ExitStack() as c0:
            def sb0(name, shape, dt=F32):
                return c0.enter_context(nc.sbuf_tensor(name, shape, dt))

            v = sb0("v", [P, CB, HW])
            wq = sb0("wq", [P, CB, C])
            bq3 = sb0("bq3", [3, C])
            bqs = sb0("bqs", [P, C], BF16)
            ones = sb0("ones", [P, P], BF16)
            pick = sb0("pick", [P, 3, C], BF16)
            coef = sb0("coef", [STACK, CB * P])
            mask = sb0("mask", [P, THIRD], BF16)

            with ExitStack() as c1:
                def sb1(name, shape, dt=F32):
                    return c1.enter_context(nc.sbuf_tensor(name, shape, dt))

                ana = sb1("ana", [P, NT, P], BF16)
                wv = sb1("wv", [P, CB, C])
                wvs = sb1("wvs", [P, CB, C])
                stats = sb1("stats", [P, CB, NCH, 6])
                mxs = sb1("mxs", [P, CB, NQ])
                mns = sb1("mns", [P, CB, NQ])
                a_ring = [sb1(f"a_ring{i}", [P, QCH]) for i in range(2)]
                t_ring = [sb1(f"t_ring{i}", [P, QCH]) for i in range(2)]
                u_ring = [sb1(f"u_ring{i}", [P, QCH]) for i in range(2)]
                qt_ring = [sb1(f"qt_ring{i}", [P, QT, P], BF16) for i in range(2)]

                PIECES = 3
                x_landed = [[sem(f"x_landed{t}{i}") for i in range(PIECES)] for t in range(CB)]
                w_landed = sem("w_landed")
                ana_landed = sem("ana_landed")
                c_landed = sem("c_landed")
                bq_landed = sem("bq_landed")
                stats_done = sem("stats_done")
                mean_in = sem("mean_in")
                mean_out = sem("mean_out")
                var_in = sem("var_in")
                var_out = sem("var_out")
                std_in = sem("std_in")
                std_out = sem("std_out")
                norm_ready = sem("norm_ready")
                wvs_ready = sem("wvs_ready")
                bvp_out = sem("bvp_out")
                bvp_ready = sem("bvp_ready")
                abs_ready = sem("abs_ready")
                abs_free = sem("abs_free")
                minmax_done = sem("minmax_done")
                t_done = sem("t_done")
                u_ready = sem("u_ready")
                transposed = sem("transposed")
                qt_ready = sem("qt_ready")
                qt_free = sem("qt_free")
                v_psum = sem("v_psum")
                v_free = sem("v_free")
                cst_ready = sem("cst_ready")

                def q_psum(slot):
                    return ps[:, 2 * slot:2 * slot + 2, :].rearrange("p b n -> p (b n)")[:, 0:QCH]

                PRE = CB * NQ

                with nc.Block(no_gpsimd_drain=True) as block:
                    @block.sync
                    def _(sp):
                        n = HW // PIECES
                        for t in range(CB):
                            for i in range(PIECES):
                                sp.dma_start(xs[:, t, i * n:(i + 1) * n], x_c[t][:, i * n:(i + 1) * n]) \
                                    .then_inc(x_landed[t][i], 16)
                                if t == 0 and i == 0:
                                    sp.dma_start(group[:, :], k_["group"]).then_inc(c_landed, 16)
                                    sp.dma_start(ident[:, :], k_["ident"]).then_inc(c_landed, 16)
                        sp.dma_start(wv[:, :, :], WvT.rearrange("(t p) n -> p t n", p=P)).then_inc(w_landed, 16)
                        sp.dma_start(column("bvp"), bv).then_inc(w_landed, 16)
                        sp.dma_start(ana[:, :, :], k_["ana"].bitcast(BF16)).then_inc(ana_landed, 16)
                        sp.dma_start(identb[:, :], k_["identb"].bitcast(BF16)).then_inc(bq_landed, 16)
                        sp.dma_start(wq[:, :, :], WqT.rearrange("(t p) n -> p t n", p=P)).then_inc(bq_landed, 16)
                        sp.dma_start(wp[:, :, :], WpT.rearrange("(t p) n -> p t n", p=P)).then_inc(bq_landed, 16)
                        sp.dma_start(pick[:, :, :], k_["pick"].bitcast(BF16)).then_inc(bq_landed, 16)
                        for r in range(3):
                            sp.dma_start(bq3[r:r + 1, :], bq.rearrange("(a n) -> a n", a=1)).then_inc(bq_landed, 16)
                        sp.dma_start(column("eye3")[0:3, :], k_["ident"][0:3, 0:3]).then_inc(bq_landed, 16)
                        sp.wait_ge(bq_landed, 16 * 8)
                        sp.wait_ge(ana_landed, 16)

                    @block.vector
                    def _(dve):
                        V = nc.vector
                        V.memset(column("minus_round"), -ROUND).then_inc(cst_ready, 1)
                        V.memset(column("minus_one"), -1.0).then_inc(cst_ready, 1)
                        V.memset(column("one"), 1.0).then_inc(cst_ready, 1)
                        V.memset(ones[:, :], 1.0).then_inc(cst_ready, 1)
                        V.memset(bqs[:, :], 0.0).then_inc(cst_ready, 1)
                        V.memset(mask[:, :], 0.0).then_inc(cst_ready, 1)
                        for t in range(CB):
                            per = NCH // PIECES
                            for i in range(PIECES):
                                dve.wait_ge(x_landed[t][i], 16)
                                with dve.Fori(0, per) as j:
                                    V.bn_stats(stats[:, t, ds(j + i * per, 1), :],
                                               xs[:, t, ds(j * CHUNK + i * per * CHUNK, CHUNK)]).then_inc(stats_done, 1)
                            dve.wait_ge(stats_done, NCH * (t + 1))
                            mean, var = column("mv")[:, 2 * t:2 * t + 1], column("mv")[:, 2 * t + 1:2 * t + 2]
                            V.bn_aggr(column("mv")[:, 2 * t:2 * t + 2],
                                      stats[:, t, :, :].rearrange("p a b -> p (a b)")).then_inc(mean_in, 1)
                            dve.wait_ge(mean_in, t + 1)
                            dve.wait_ge(mean_out, t + 1)
                            link(dve, V.tensor_copy(column("mg")[:, t:t + 1], ps[:, 7, 0:1]))
                            link(dve, V.tensor_tensor(column("d")[:, t:t + 1], mean, column("mg")[:, t:t + 1], ALU.subtract))
                            link(dve, V.tensor_tensor(column("d")[:, t:t + 1], column("d")[:, t:t + 1],
                                                      column("d")[:, t:t + 1], ALU.mult))
                            V.tensor_tensor(column("e")[:, t:t + 1], column("d")[:, t:t + 1], var, ALU.add).then_inc(var_in, 1)
                            dve.wait_ge(var_out, t + 1)
                            V.tensor_scalar(column("var")[:, t:t + 1], ps[:, 7, 1:2], EPS, None, ALU.add).then_inc(std_in, 1)
                            dve.wait_ge(std_out, t + 1)
                            link(dve, V.reciprocal(column("rstd")[:, t:t + 1], column("e")[:, t:t + 1]))
                            V.scalar_tensor_tensor(column("nmr")[:, t:t + 1], column("mg")[:, t:t + 1], -1.0,
                                                   column("rstd")[:, t:t + 1], ALU.mult, ALU.mult).then_inc(norm_ready, 1)
                        dve.wait_ge(w_landed, 32)
                        for t in range(CB):
                            V.tensor_scalar(wvs[:, t, :], wv[:, t, :], column("rstd")[:, t:t + 1], None,
                                            ALU.mult).then_inc(wvs_ready, 1)
                        dve.wait_ge(norm_ready, CB)
                        dve.wait_ge(bvp_out, 1)
                        V.tensor_tensor(column("bvp"), column("bvp"), ps[:, 7, 2:4], ALU.add).then_inc(bvp_ready, 1)
                        for t in range(CB):
                            with dve.Fori(0, NQ // 2) as j:
                                for u in range(2):
                                    dve.wait_ge(abs_ready, j * 2 + (t * NQ + u + 1))
                                    V.tensor_reduce(mxs[:, t, ds(j * 2 + u, 1)], a_ring[u][:, :], AX_X, ALU.max).then_inc(minmax_done, 1)
                                    V.tensor_reduce(mns[:, t, ds(j * 2 + u, 1)], a_ring[u][:, :], AX_X, ALU.min).then_inc(abs_free, 1)
                            dve.wait_ge(minmax_done, NQ * (t + 1))
                            dve.wait_ge(abs_free, NQ * (t + 1))
                            one = slice(t, t + 1)
                            link(dve, V.tensor_reduce(column("mx_")[:, one], mxs[:, t, :], AX_X, ALU.max))
                            link(dve, V.tensor_reduce(column("mn")[:, one], mns[:, t, :], AX_X, ALU.min))
                            link(dve, V.tensor_tensor(column("ptp")[:, one], column("mx_")[:, one], column("mn")[:, one],
                                                      ALU.subtract))
                            link(dve, V.reciprocal(column("rp")[:, one], column("ptp")[:, one]))
                            link(dve, V.tensor_scalar(column("sc")[:, one], column("rp")[:, one],
                                                      LEVELS * (1 + 2.0 ** -22), None, ALU.mult))
                        for t in range(CB):
                            with dve.Fori(0, NQ // 2) as j:
                                for u in range(2):
                                    n = j * 2 + (t * NQ + u + 1)
                                    dve.wait_ge(abs_ready, n + CB * NQ)
                                    dve.wait_ge(transposed, n)
                                    V.tensor_scalar(t_ring[u][:, :], a_ring[u][:, :], column("mn")[:, t:t + 1],
                                                    column("sc")[:, t:t + 1], ALU.subtract, ALU.mult).then_inc(abs_free, 1)
                                    dve.wait_ge(abs_free, n + CB * NQ)
                                    V.tensor_scalar(u_ring[u][:, :], t_ring[u][:, :], -0.5 + 2.0 ** -16, ROUND,
                                                    ALU.add, ALU.add).then_inc(u_ready, 1)

                    @block.scalar
                    def _(act):
                        S = nc.scalar
                        for t in range(CB):
                            act.wait_ge(std_in, t + 1)
                            S.activation(column("e")[:, t:t + 1], column("var")[:, t:t + 1], ACT.Sqrt).then_inc(std_out, 1)

                        def absolute(t, j, u):
                            S.activation(a_ring[u][:, :], xs[:, t, ds(j * (2 * QCH) + u * QCH, QCH)], ACT.Abs,
                                         scale=column("rstd")[:, t:t + 1], bias=column("nmr")[:, t:t + 1]).then_inc(abs_ready, 1)

                        def v_out(n, chunk, ob, slot):
                            act.wait_ge(v_psum, n + 1)
                            S.activation(v[:, ob, ds(chunk * CHUNK, CHUNK)], ps[:, 4 + slot, :], ACT.Identity,
                                         bias=column("bvp")[:, ob:ob + 1]).then_inc(v_free, 1)

                        half = NQ // 2
                        act.wait_ge(norm_ready, 1)
                        absolute(0, 0, 0)
                        absolute(0, 0, 1)
                        act.wait_ge(norm_ready, CB)
                        act.wait_ge(bvp_ready, 1)
                        for t in range(CB):
                            with act.Fori(0, half - 1) as j:
                                for u in range(2):
                                    n = j * 2 + (t * NQ + u)
                                    act.wait_ge(abs_free, n + 1)
                                    absolute(t, j + 1, u)
                                    v_out(n, j + t * half, u, u)
                            for u in range(2):
                                n = (t + 1) * NQ - 2 + u
                                act.wait_ge(abs_free, n + 1)
                                absolute((t + 1) % CB, 0, u)
                                v_out(n, n // 2, u, u)
                        act.wait_ge(cst_ready, 4)

                        def q_out(t, j, u, nxt):
                            n = j * 2 + (t * NQ + u)
                            if nxt is not None:
                                act.wait_ge(abs_free, n + (CB * NQ + 1))
                                absolute(nxt[0], nxt[1], u)
                            act.wait_ge(transposed, n + 3)
                            act.wait_ge(qt_free, n + 1)
                            S.activation(qt_ring[u][:, :, :].rearrange("p a b -> p (a b)"), q_psum(u), ACT.Identity,
                                         bias=column("minus_round")).then_inc(qt_ready, 1)
                            before = isinstance(j, int) and (t, j, u) == (0, 0, 0)
                            after = isinstance(j, int) and (t, j, u) > (1, 0, 0) or t > 0 and not isinstance(j, int)
                            if not before and not after:
                                v_out(n + (PRE - 1), j + ((PRE + t * NQ) // 2 + u - 1), 1 - u, 1 - u)

                        for t in range(CB):
                            for u in range(2):
                                q_out(t, 0, u, (t, 1))
                            with act.Fori(1, half - 1) as j:
                                for u in range(2):
                                    q_out(t, j, u, (t, j + 1))
                            for u in range(2):
                                q_out(t, half - 1, u, (t + 1, 0) if t + 1 < CB else None)

                    @block.tensor
                    def _(pe):
                        T = nc.tensor
                        pe.wait_ge(c_landed, 32)
                        for t in range(CB):
                            pe.wait_ge(mean_in, t + 1)
                            T.matmul(ps[:, 7, 0:1], group[:, :], column("mv")[:, 2 * t:2 * t + 1],
                                     start=True, stop=True).then_inc(mean_out, 1)
                            pe.wait_ge(var_in, t + 1)
                            T.matmul(ps[:, 7, 1:2], group[:, :], column("e")[:, t:t + 1],
                                     start=True, stop=True).then_inc(var_out, 1)
                        pe.wait_ge(norm_ready, CB)
                        pe.wait_ge(w_landed, 32)
                        for ob in range(CB):
                            for kb in range(CB):
                                m = T.matmul(ps[:, 7, 2 + ob:3 + ob], wv[:, kb, ob * P:(ob + 1) * P],
                                             column("nmr")[:, kb:kb + 1], start=kb == 0, stop=kb == CB - 1)
                        m.then_inc(bvp_out, 1)
                        pe.wait_ge(wvs_ready, CB)
                        pe.sem_inc(v_free, 2)
                        pe.sem_inc(transposed, 2)
                        pe.sem_inc(qt_free, 2)

                        def v_unit(n, chunk, ob):
                            pe.wait_ge(v_free, n + 1)
                            for kb in range(CB):
                                m = T.matmul(ps[:, 4 + ob, :], wvs[:, kb, ob * P:(ob + 1) * P],
                                             xs[:, kb, ds(chunk * CHUNK, CHUNK)], start=kb == 0, stop=kb == CB - 1)
                            m.then_inc(v_psum, 1)

                        with pe.Fori(0, PRE // 2) as j:
                            for u in range(2):
                                v_unit(j * 2 + u, j, u)
                        pe.wait_ge(ana_landed, 16)

                        def turn(n, u):
                            pe.wait_ge(u_ready, n + 1)
                            for i in range(QT):
                                m = T.transpose(q_psum(u)[:, i * P:(i + 1) * P], u_ring[u][:, i * P:(i + 1) * P], ident[:, :])
                            m.then_inc(transposed, 1)

                        def q_step(t, j, first=False, last=False):
                            for u in range(2):
                                n = j * 2 + (t * NQ + u)
                                if not (last and u == 1 and t == CB - 1):
                                    turn(n + 1, 1 - u)
                                if t == 0:
                                    v_unit(n + PRE, j + PRE // 2, u)
                                pe.wait_ge(qt_ready, n + 1)
                                for i in range(QT):
                                    m = T.matmul(ps[:, 6, t * P:(t + 1) * P],
                                                 ana[:, ds(j * (2 * QT) + (u * QT + i), 1), :].rearrange("p a n -> p (a n)"),
                                                 qt_ring[u][:, i, :], start=first and u == 0 and i == 0,
                                                 stop=last and u == 1 and i == QT - 1, skip_group_check=True)
                                m.then_inc(qt_free, 1)

                        turn(0, 0)
                        for t in range(CB):
                            q_step(t, 0, first=True)
                            with pe.Fori(1, NQ // 2 - 1) as j:
                                q_step(t, j)
                            q_step(t, NQ // 2 - 1, last=True)

            with ExitStack() as c2:
                def sb2(name, shape, dt=F32):
                    return c2.enter_context(nc.sbuf_tensor(name, shape, dt))

                sel = sb2("sel", [STACK, 2, STACK])
                f_all = sb2("f_all", [STACK, 2, C])
                rest1 = sb2("rest1", [STACK, 2, C])
                rest2 = sb2("rest2", [STACK, 2, C])
                part = [sb2(f"part{i}", [STACK, 2, C], BF16) for i in range(SPLITS)]
                stack_a = sb2("stack_a", [STACK, 2, C], BF16)
                stack_b = sb2("stack_b", [STACK, 2, C], BF16)
                syn_ring = [sb2(f"syn_ring{i}", [STACK, 2, CHUNK], BF16) for i in range(2)]
                sq_ring = [sb2(f"sq_ring{i}", [P, 2, CHUNK]) for i in range(2)]
                s2_ring = [sb2(f"s2_ring{i}", [P, CHUNK]) for i in range(2)]
                fq_ring = [sb2(f"fq_ring{i}", [P, CB, CHUNK]) for i in range(2)]
                bqf = [sb2(f"bqf{i}", [3, C]) for i in range(2)]
                bqp = [sb2(f"bqp{i}", [3, C], BF16) for i in range(3)]
                bqm = [sb2(f"bqm{i}", [3, C]) for i in range(2)]
                row_max = sb2("row_max", [P, NT, BLOCKS])
                m_f = sb2("m_f", [P, THIRD_TILES, BLOCKS])
                m_r = sb2("m_r", [P, THIRD_TILES, BLOCKS])
                m_r2 = sb2("m_r2", [P, THIRD_TILES, BLOCKS])
                m_p = sb2("m_p", [P, THIRD_TILES, SPLITS, BLOCKS], BF16)

                TPC = CHUNK // P
                sel_landed = sem("sel_landed")
                syn_landed = [sem(f"syn_landed{i}") for i in range(2)]
                ri_ready = sem("ri_ready")
                sq_ready = sem("sq_ready")
                s2_ready = sem("s2_ready")
                fq_ready = sem("fq_ready")
                q_ready = sem("q_ready")
                q_free = sem("q_free")
                coef_ready = sem("coef_ready")
                summed = sem("summed")
                stacks_ready = sem("stacks_ready")
                m_ready = sem("m_ready")
                m_turned = sem("m_turned")

                with nc.Block(no_gpsimd_drain=True) as block:
                    @block.sync
                    def _(sp):
                        sp.dma_start(sel[:, :, :], k_["sel"]).then_inc(sel_landed, 16)

                        def load(j, u):
                            sp.dma_start(syn_ring[u][:, :, :], k_["syn"].bitcast(BF16)[:, :, ds(j * (2 * CHUNK) + u * CHUNK, CHUNK)]) \
                                .then_inc(syn_landed[u], 16)

                        load(0, 0)
                        load(0, 1)
                        with sp.Fori(1, NCH // 2) as j:
                            for u in range(2):
                                sp.wait_ge(ri_ready, j * 4 + (2 * u - 2))
                                load(j, u)

                    @block.vector
                    def _(dve):
                        V = nc.vector
                        V.tensor_copy(coef[:, :], ps[0:STACK, 6, 0:CB * P]).then_inc(coef_ready, 1)
                        link(dve, V.tensor_copy(bqp[0][:, :], bq3[:, :]))
                        link(dve, V.tensor_tensor(bqf[0][:, :], bq3[:, :], bqp[0][:, :], ALU.subtract))
                        link(dve, V.tensor_copy(bqp[1][:, :], bqf[0][:, :]))
                        link(dve, V.tensor_tensor(bqf[1][:, :], bqf[0][:, :], bqp[1][:, :], ALU.subtract))
                        link(dve, V.tensor_copy(bqp[2][:, :], bqf[1][:, :]))
                        eye = column("eye3")
                        link(dve, V.tensor_scalar(bqm[0][:, :], bqp[0][:, :], eye[0:3, 0:1], None, ALU.mult))
                        link(dve, V.scalar_tensor_tensor(bqm[1][:, :], bqp[1][:, :], eye[0:3, 1:2], bqm[0][:, :],
                                                         ALU.mult, ALU.add))
                        link(dve, V.scalar_tensor_tensor(bqs[0:3, :], bqp[2][:, :], eye[0:3, 2:3], bqm[1][:, :],
                                                         ALU.mult, ALU.add))
                        dve.wait_ge(summed, 1)
                        link(dve, V.tensor_copy(f_all[:, :, :], ps[0:STACK, 4, :].rearrange("p (a n) -> p a n", a=2)))
                        link(dve, V.tensor_copy(part[0][:, :, :], f_all[:, :, :]))
                        link(dve, V.tensor_tensor(rest1[:, :, :], f_all[:, :, :], part[0][:, :, :], ALU.subtract))
                        link(dve, V.tensor_copy(part[1][:, :, :], rest1[:, :, :]))
                        link(dve, V.tensor_tensor(rest2[:, :, :], rest1[:, :, :], part[1][:, :, :], ALU.subtract))
                        link(dve, V.tensor_copy(part[2][:, :, :], rest2[:, :, :]))
                        for s, (a, b) in enumerate(((0, 0), (1, 0), (2, 1))):
                            r = slice(s * ROWS, (s + 1) * ROWS)
                            V.tensor_copy(stack_a[r, :, :], part[a][r, :, :]).then_inc(stacks_ready, 1)
                            V.tensor_copy(stack_b[r, :, :], part[b][r, :, :]).then_inc(stacks_ready, 1)
                        dve.sem_inc(q_free, 2)

                        def squares(j, u):
                            for cb in range(CB):
                                n = j * 4 + (2 * u + cb)
                                dve.wait_ge(sq_ready, n + 3)
                                dve.wait_ge(fq_ready, n + 1)
                                V.tensor_tensor(s2_ring[cb][:, :], sq_ring[cb][:, 0, :], sq_ring[cb][:, 1, :],
                                                ALU.add).then_inc(s2_ready, 1)

                        def maxima(j, u):
                            dve.wait_ge(q_ready, j * 2 + (u + 3))
                            V.tensor_reduce(row_max[:, ds(j * (2 * TPC) + u * TPC, TPC), :],
                                            ps[:, 4 + 2 * u:6 + 2 * u, :].rearrange(
                                                "p b (t g r) -> p (b t) r g", t=2, r=BLOCKS), AX_X, ALU.max).then_inc(q_free, 1)

                        last = NCH // 2 - 1
                        squares(0, 0)
                        with dve.Fori(0, last) as j:
                            squares(j, 1)
                            maxima(j, 0)
                            squares(j + 1, 0)
                            maxima(j, 1)
                        squares(last, 1)
                        maxima(last, 0)
                        maxima(last, 1)
                        dve.wait_ge(q_free, NCH + 2)
                        third = [row_max[:, t * THIRD_TILES:(t + 1) * THIRD_TILES, :] for t in range(3)]
                        for t in range(1, 3):
                            so_far = third[0] if t == 1 else m_f[:, :, :]
                            cut = 3 * t % BLOCKS
                            V.tensor_tensor(m_f[:, :, cut:BLOCKS], so_far[:, :, cut:BLOCKS], third[t][:, :, 0:BLOCKS - cut],
                                            ALU.max)
                            link(dve, V.tensor_tensor(m_f[:, :, 0:cut], so_far[:, :, 0:cut], third[t][:, :, BLOCKS - cut:BLOCKS],
                                                      ALU.max))
                        link(dve, V.tensor_copy(m_p[:, :, 0, :], m_f[:, :, :]))
                        link(dve, V.tensor_tensor(m_r[:, :, :], m_f[:, :, :], m_p[:, :, 0, :], ALU.subtract))
                        link(dve, V.tensor_copy(m_p[:, :, 1, :], m_r[:, :, :]))
                        link(dve, V.tensor_tensor(m_r2[:, :, :], m_r[:, :, :], m_p[:, :, 1, :], ALU.subtract))
                        V.tensor_copy(m_p[:, :, 2, :], m_r2[:, :, :]).then_inc(m_ready, 1)
                        dve.wait_ge(m_turned, 1)
                        V.tensor_copy(mask[0:SPLITS * BLOCKS, :], ps[0:SPLITS * BLOCKS, 0:3, :].rearrange("p b n -> p (b n)")
                                      .bitcast(BF16)[:, 0:THIRD])

                    @block.scalar
                    def _(act):
                        S = nc.scalar
                        act.sem_inc(sq_ready, 2)
                        act.sem_inc(fq_ready, 2)
                        with act.Fori(0, NCH // 2) as j:
                            for u in range(2):
                                for cb in range(CB):
                                    n = j * 4 + (2 * u + cb)
                                    act.wait_ge(ri_ready, n + 1)
                                    S.activation(sq_ring[cb][:, :, :], ps[:, 2 * cb:2 * cb + 2, :], ACT.Square,
                                                 scale=1.0 / HW).then_inc(sq_ready, 1)
                                for cb in range(CB):
                                    n = j * 4 + (2 * u + cb)
                                    act.wait_ge(s2_ready, n + 1)
                                    if cb == 0:
                                        act.wait_ge(q_ready, j * 2 + (u + 1))
                                    S.activation(fq_ring[u][:, cb, :], s2_ring[cb][:, :], ACT.Sqrt).then_inc(fq_ready, 1)

                    @block.tensor
                    def _(pe):
                        T = nc.tensor
                        pe.wait_ge(sel_landed, 16)
                        pe.wait_ge(coef_ready, 1)
                        for i in range(2):
                            m = T.matmul(ps[0:STACK, 4, i * C:(i + 1) * C], sel[:, i, :], coef[:, :], start=True, stop=True)
                        m.then_inc(summed, 1)
                        pe.wait_ge(stacks_ready, 6)
                        pe.sem_inc(q_ready, 2)

                        def parts(j, u):
                            pe.wait_ge(syn_landed[u], j * 16 + 16)
                            for cb in range(CB):
                                n = j * 4 + (2 * u + cb)
                                pe.wait_ge(sq_ready, n + 1)
                                for i in range(2):
                                    T.matmul(ps[:, 2 * cb + i, :], stack_a[:, i, cb * P:(cb + 1) * P], syn_ring[u][:, 0, :],
                                             start=True, stop=False)
                                    m = T.matmul(ps[:, 2 * cb + i, :], stack_b[:, i, cb * P:(cb + 1) * P], syn_ring[u][:, 1, :],
                                                 start=False, stop=True)
                                m.then_inc(ri_ready, 1)

                        def queries(j, u):
                            pe.wait_ge(fq_ready, j * 4 + (2 * u + 4))
                            pe.wait_ge(q_free, j * 2 + (u + 1))
                            for i in range(TPC):
                                o = ps[:, 4 + 2 * u + i // 2, (i % 2) * C:(i % 2 + 1) * C]
                                T.matmul(o, ones[:, :], bqs[:, :], start=True, stop=False)
                                for kb in range(CB):
                                    m = T.matmul(o, fq_ring[u][:, kb, i * P:(i + 1) * P], wq[:, kb, :],
                                                 start=False, stop=kb == CB - 1)
                                    if i == TPC - 1 and kb == CB - 1:
                                        m.then_inc(q_ready, 1)

                        parts(0, 0)
                        with pe.Fori(0, NCH // 2 - 1) as j:
                            parts(j, 1)
                            queries(j, 0)
                            parts(j + 1, 0)
                            queries(j, 1)
                        last = NCH // 2 - 1
                        parts(last, 1)
                        queries(last, 0)
                        queries(last, 1)
                        pe.wait_ge(m_ready, 1)
                        for i in range(THIRD_TILES):
                            o = ps[0:SPLITS * BLOCKS, i * P // (2 * CHUNK), :].bitcast(BF16)
                            a = i * P % (2 * CHUNK)
                            m = T.transpose(o[:, a:a + P], m_p[:, i, :, :].rearrange("p s b -> p (s b)"), identb[:, :])
                        m.then_inc(m_turned, 1)

            with ExitStack() as c3:
                def sb3(name, shape, dt=F32):
                    return c3.enter_context(nc.sbuf_tensor(name, shape, dt))

                SLOTS = 3
                y_ring = [sb3(f"y_ring{i}", [P, CB, CHUNK]) for i in range(SLOTS)]
                stats = sb3("stats1", [P, CB, NCH, 6])
                mask_psum = sem("mask_psum")
                y_ready = sem("y_ready")
                y_seen = sem("y_seen")
                x1_ready = sem("x1_ready")
                stats1_done = sem("stats1_done")

                with nc.Block(no_gpsimd_drain=True) as block:
                    @block.tensor
                    def _(pe):
                        T = nc.tensor
                        pe.sem_inc(y_ready, SLOTS)
                        for t in range(3):
                            with pe.Fori(0, NCH // 3 // SLOTS) as j:
                                for u in range(SLOTS):
                                    n = j * SLOTS + (t * (NCH // 3) + u)
                                    pe.wait_ge(y_ready, n + 1)
                                    for cb in range(CB):
                                        m = T.matmul(ps[:, 2 * u + cb, :], pick[:, t, cb * P:(cb + 1) * P],
                                                     mask[:, ds(j * (SLOTS * CHUNK) + u * CHUNK, CHUNK)], start=True, stop=True)
                                    m.then_inc(mask_psum, 1)

                    @block.vector
                    def _(dve):
                        V = nc.vector
                        dve.sem_inc(x1_ready, SLOTS)

                        def stat(i):
                            dve.wait_ge(x1_ready, i + (SLOTS + 1))
                            for cb in range(CB):
                                V.bn_stats(stats[:, cb, ds(i, 1), :], xs[:, cb, ds(i * CHUNK, CHUNK)]).then_inc(stats1_done, 1)

                        def product(i, u):
                            dve.wait_ge(mask_psum, i + 1)
                            dve.wait_ge(x1_ready, i + 1)
                            V.scalar_tensor_tensor(y_ring[u][:, :, :], ps[:, 2 * u:2 * u + 2, :], 1.0,
                                                   v[:, :, ds(i * CHUNK, CHUNK)], ALU.add, ALU.mult).then_inc(y_ready, 1)

                        for u in range(SLOTS):
                            product(u, u)
                        with dve.Fori(1, NCH // SLOTS) as j:
                            for u in range(SLOTS):
                                stat(j * SLOTS + (u - SLOTS))
                                product(j * SLOTS + u, u)
                        for i in range(NCH - SLOTS, NCH):
                            stat(i)
                        dve.wait_ge(stats1_done, 2 * NCH)
                        for t in range(CB):
                            V.bn_aggr(column("mv")[:, 2 * t:2 * t + 2], stats[:, t, :, :].rearrange("p a b -> p (a b)"))

                    @block.gpsimd
                    def _(pool):
                        with pool.Fori(0, NCH // SLOTS) as j:
                            for u in range(SLOTS):
                                pool.wait_ge(y_ready, j * SLOTS + (u + SLOTS + 1))
                                pool.sem_inc(y_seen, 1)
                                here = xs[:, :, ds(j * (SLOTS * CHUNK) + u * CHUNK, CHUNK)]
                                nc.gpsimd.tensor_tensor(here, here, y_ring[u][:, :, :], ALU.add).then_inc(x1_ready, 1)

        with ExitStack() as c4:
            def sb4(name, shape, dt=F32):
                return c4.enter_context(nc.sbuf_tensor(name, shape, dt))

            NX = NT * HEADS
            weights = sb4("weights", [P, NT, HEADS, 4])
            index = sb4("index", [P, NT, HEADS], U32)
            with ExitStack() as c5:
                def sb5(name, shape, dt=F32):
                    return c5.enter_context(nc.sbuf_tensor(name, shape, dt))

                wps = sb5("wps", [P, CB, NPROJ])
                nmr_wide = sb5("nmr_wide", [P, CB, P])
                ones_row = sb5("ones_row", [P, P])
                bias_row = sb5("bias_row", [1, NPROJ])
                bias = sb5("bias", [P, NPROJ])
                SLOTS = 4
                x_ring = [sb5(f"x_ring{i}", [P, CB, P]) for i in range(SLOTS)]
                stage = [sb5(f"stage{i}", [P, C]) for i in range(SLOTS)]
                flow = sb5("flow", [P, NT, NFLOW])
                grid = sb5("grid", [P, NT, 2 * HEADS])
                pos = sb5("pos", [P, NT, 2 * HEADS])
                low = sb5("low", [P, NT, 2 * HEADS])
                base = sb5("base", [P, NT, 2 * HEADS])
                off = sb5("off", [P, NT, 2 * HEADS])
                tent = [sb5(f"tent{i}", [P, NT, 2 * HEADS]) for i in range(2)]
                row = sb5("row", [P, NX])
                top = sb5("top", [P, NT])
                expo = sb5("expo", [P, NT, HEADS])
                total = sb5("total", [P, NT])
                share = sb5("share", [P, NT])
                wy = [sb5(f"wy{i}", [P, NX]) for i in range(2)]

                zeros = sb5("zeros", [W, C])
                grid_landed = sem("grid_landed")
                zeros_ready = sem("zeros_ready")
                edges_stored = sem("edges_stored")
                mean1_out = sem("mean1_out")
                var1_in = sem("var1_in")
                var1_out = sem("var1_out")
                std1_in = sem("std1_in")
                std1_out = sem("std1_out")
                wide_ready = sem("wide_ready")
                wps_ready = sem("wps_ready")
                bias_out = sem("bias_out")
                x_ready = sem("x_ready")
                proj_ready = sem("proj_ready")
                stage_ready = sem("stage_ready")
                proj_free = sem("proj_free")
                stored = [sem(f"stored{i}") for i in range(SLOTS)]
                off_ready = sem("off_ready")
                tent_ready = sem("tent_ready")
                expo_in = sem("expo_in")
                expo_out = sem("expo_out")

                with nc.Block(no_gpsimd_drain=True) as block:
                    @block.sync
                    def _(sp):
                        sp.dma_start(bias_row[:, :], bp.rearrange("(a n) -> a n", a=1)).then_inc(grid_landed, 16)
                        sp.dma_start(grid[:, :, :], k_["grid"]).then_inc(grid_landed, 16)
                        sp.wait_ge(zeros_ready, 1)
                        sp.dma_start(table[0:W, 0:C], zeros[:, :]).then_inc(edges_stored, 16)
                        sp.dma_start(table[HW:HW + W, C:2 * C], zeros[:, :]).then_inc(edges_stored, 16)
                        with sp.Fori(0, NT // SLOTS) as j:
                            for u in range(SLOTS):
                                sp.wait_ge(stage_ready, j * SLOTS + (u + 1))
                                r = j * (SLOTS * P) + u * P
                                sp.dma_start(table[ds(r + W, P), 0:C], stage[u][:, :]).then_inc(stored[u], 16)
                                sp.dma_start(table[ds(r, P), C:2 * C], stage[u][:, :]).then_inc(stored[u], 16)
                        for u in range(SLOTS):
                            sp.wait_ge(stored[u], 32 * (NT // SLOTS))
                        sp.wait_ge(edges_stored, 32)

                    @block.gpsimd
                    def _(pool):
                        nc.gpsimd.memset(zeros[:, :], 0.0).then_inc(zeros_ready, 1)

                    @block.vector
                    def _(dve):
                        V = nc.vector
                        V.memset(ones_row[:, :], 1.0).then_inc(wide_ready, 1)
                        dve.wait_ge(mean1_out, 1)
                        mv = column("mv").rearrange("p (t k) -> p k t", k=2)
                        link(dve, V.tensor_copy(column("mg"), ps[:, 7, 0:2]))
                        link(dve, V.tensor_tensor(column("d"), mv[:, 0, :], column("mg"), ALU.subtract))
                        link(dve, V.tensor_tensor(column("mean"), column("d"), column("d"), ALU.mult))
                        V.tensor_tensor(column("e"), column("mean"), mv[:, 1, :], ALU.add).then_inc(var1_in, 1)
                        dve.wait_ge(var1_out, 1)
                        V.tensor_scalar(column("var1"), ps[:, 7, 2:4], EPS, None, ALU.add).then_inc(std1_in, 1)
                        dve.wait_ge(std1_out, 1)
                        link(dve, V.reciprocal(column("rstd1"), column("mean1")))
                        link(dve, V.scalar_tensor_tensor(column("nmr1"), column("mg"), -1.0, column("rstd1"), ALU.mult, ALU.mult))
                        dve.wait_ge(wide_ready, 1)
                        for t in range(CB):
                            V.tensor_scalar(nmr_wide[:, t, :], ones_row[:, :], column("nmr1")[:, t:t + 1], None,
                                            ALU.mult).then_inc(wide_ready, 1)
                        for t in range(CB):
                            V.tensor_scalar(wps[:, t, :], wp[:, t, :], column("rstd1")[:, t:t + 1], None,
                                            ALU.mult).then_inc(wps_ready, 1)
                        dve.wait_ge(bias_out, 1)
                        link(dve, V.tensor_copy(bias[:, :], ps[:, 6, 0:NPROJ]))
                        dve.sem_inc(proj_free, SLOTS)

                        def leave(j, u):
                            dve.wait_ge(proj_ready, j * SLOTS + (u + 1))
                            if not (isinstance(j, int) and j == 0):
                                dve.wait_ge(stored[u], j * 32)
                            V.tensor_tensor(stage[u][:, :], ps[:, u, 0:C], bias[:, 0:C], ALU.add).then_inc(stage_ready, 1)
                            V.tensor_tensor(flow[:, ds(j * SLOTS + u, 1), :].rearrange("p a n -> p (a n)"), ps[:, u, C:NPROJ],
                                            bias[:, C:NPROJ], ALU.add).then_inc(proj_free, 1)

                        for u in range(SLOTS):
                            leave(0, u)
                        with dve.Fori(1, NT // SLOTS) as j:
                            for u in range(SLOTS):
                                leave(j, u)
                        dve.wait_ge(proj_free, NT + SLOTS)
                        dve.wait_ge(grid_landed, 32)
                        both = flow[:, :, 0:2 * HEADS]
                        link(dve, V.scalar_tensor_tensor(pos[:, :, :], both, W / (W - 1.0), grid[:, :, :], ALU.mult, ALU.add))
                        link(dve, V.tensor_scalar(low[:, :, :], pos[:, :, :], -0.5, 0.0, ALU.add, ALU.max))
                        link(dve, V.tensor_scalar(base[:, :, :], low[:, :, :], W - 2.0, ROUND, ALU.min, ALU.add))
                        link(dve, V.tensor_scalar(low[:, :, :], base[:, :, :], -ROUND, None, ALU.add))
                        V.tensor_tensor(off[:, :, :], pos[:, :, :], low[:, :, :], ALU.subtract).then_inc(off_ready, 1)
                        corner = low[:, :, :].rearrange("p t (k c) -> p (t k) c", c=2)
                        link(dve, V.tensor_scalar(row[:, :], corner[:, :, 1], float(W), float(W), ALU.mult, ALU.add))
                        link(dve, V.tensor_tensor(index[:, :, :].rearrange("p t k -> p (t k)"), row[:, :], corner[:, :, 0], ALU.add))
                        logit = flow[:, :, 2 * HEADS:NFLOW]
                        link(dve, V.tensor_reduce(top[:, :], logit, AX_X, ALU.max))
                        V.tensor_tensor(expo[:, :, :], logit, top[:, :, None].broadcast_to([P, NT, HEADS]),
                                        ALU.subtract).then_inc(expo_in, 1)
                        dve.wait_ge(expo_out, 1)
                        link(dve, V.tensor_reduce(total[:, :], expo[:, :, :], AX_X, ALU.add))
                        link(dve, V.reciprocal(share[:, :], total[:, :]))
                        link(dve, V.tensor_tensor(expo[:, :, :], expo[:, :, :], share[:, :, None].broadcast_to([P, NT, HEADS]),
                                                  ALU.mult))
                        dve.wait_ge(tent_ready, 4)
                        side = [tent[i][:, :, :].rearrange("p t (k c) -> p (t k) c", c=2) for i in range(2)]
                        for i in range(2):
                            link(dve, V.tensor_tensor(wy[i][:, :], side[i][:, :, 1], expo[:, :, :].rearrange("p t k -> p (t k)"),
                                                      ALU.mult))
                        w4 = weights[:, :, :, :].rearrange("p t k q -> p (t k) q")
                        for i in range(2):
                            for k in range(2):
                                V.tensor_tensor(w4[:, :, 2 * i + k], side[i][:, :, 0], wy[k][:, :], ALU.mult)

                    @block.scalar
                    def _(act):
                        S = nc.scalar
                        act.wait_ge(std1_in, 1)
                        S.activation(column("mean1"), column("var1"), ACT.Sqrt).then_inc(std1_out, 1)
                        for u in range(SLOTS):
                            S.copy(x_ring[u][:, :, :], xs[:, :, u * P:(u + 1) * P]).then_inc(x_ready, 1)
                        with act.Fori(1, NT // SLOTS) as j:
                            for u in range(SLOTS):
                                act.wait_ge(proj_ready, j * SLOTS + (u + 1 - SLOTS))
                                S.copy(x_ring[u][:, :, :], xs[:, :, ds(j * (SLOTS * P) + u * P, P)]).then_inc(x_ready, 1)
                        act.wait_ge(off_ready, 1)
                        S.activation(pos[:, :, :], off[:, :, :], ACT.Abs).then_inc(tent_ready, 1)
                        S.activation(base[:, :, :], off[:, :, :], ACT.Abs, bias=column("minus_one")).then_inc(tent_ready, 1)
                        act.wait_ge(tent_ready, 2)
                        S.activation(tent[0][:, :, :], pos[:, :, :], ACT.Relu, scale=-1.0, bias=column("one")).then_inc(tent_ready, 1)
                        S.activation(tent[1][:, :, :], base[:, :, :], ACT.Relu, scale=-1.0, bias=column("one")).then_inc(tent_ready, 1)
                        act.wait_ge(expo_in, 1)
                        S.activation(expo[:, :, :], expo[:, :, :], ACT.Exp).then_inc(expo_out, 1)

                    @block.tensor
                    def _(pe):
                        T = nc.tensor
                        m = T.matmul(ps[:, 7, 0:2], group[:, :], column("mv").rearrange("p (t k) -> p k t", k=2)[:, 0, :],
                                     start=True, stop=True).then_inc(mean1_out, 1)
                        pe.wait_ge(var1_in, 1)
                        T.matmul(ps[:, 7, 2:4], group[:, :], column("e"), start=True, stop=True).then_inc(var1_out, 1)
                        pe.wait_ge(wide_ready, 1 + CB)
                        pe.wait_ge(grid_landed, 32)
                        for kb in range(CB):
                            T.matmul(ps[:, 6, 0:NPROJ], nmr_wide[:, kb, :], wp[:, kb, :], start=kb == 0, stop=False)
                        T.matmul(ps[:, 6, 0:NPROJ], ones_row[0:1, :], bias_row[:, :], start=False, stop=True).then_inc(bias_out, 1)
                        pe.wait_ge(wps_ready, CB)
                        with pe.Fori(0, NT // SLOTS) as j:
                            for u in range(SLOTS):
                                pe.wait_ge(x_ready, j * SLOTS + (u + 1))
                                pe.wait_ge(proj_free, j * SLOTS + (u + 1))
                                for kb in range(CB):
                                    m = T.matmul(ps[:, u, 0:NPROJ], x_ring[u][:, kb, :], wps[:, kb, :], start=kb == 0, stop=kb == CB - 1)
                                m.then_inc(proj_ready, 1)

            with ExitStack() as c6:
                def sb6(name, shape, dt=F32):
                    return c6.enter_context(nc.sbuf_tensor(name, shape, dt))

                SLOTS = 3
                QUAD = 4 * C
                ON_DVE = [(k, q) for k in range(HEADS) for q in range(3 if k < 2 else 2)]
                ON_PE = [(k, q) for k in range(HEADS) for q in range(4) if (k, q) not in ON_DVE]
                ND, NP = len(ON_DVE), len(ON_PE)
                quad = [[sb6(f"quad{i}_{k}", [P, QUAD]) for k in range(HEADS)] for i in range(SLOTS)]
                idx = [sb6(f"idx{i}", [P, HEADS], U32) for i in range(SLOTS)]
                diag = [[sb6(f"diag{i}_{c}", [P, P]) for c in range(NP)] for i in range(SLOTS)]
                acc = [sb6(f"acc{i}", [P, 2, C]) for i in range(SLOTS)]
                ob = [sb6(f"ob{i}", [P, CB, P]) for i in range(SLOTS)]

                landed = [[sem(f"landed{i}_{k}") for k in range(HEADS)] for i in range(SLOTS)]
                idx_ready = sem("idx_ready")
                idx_seen = sem("idx_seen")
                added = sem("added")
                diag_ready = sem("diag_ready")
                out_psum = sem("out_psum")
                out_ready = sem("out_ready")
                written = [sem(f"written{i}") for i in range(SLOTS)]

                with nc.Block(no_gpsimd_drain=True) as block:
                    def tiles(eng, step):
                        for u in range(SLOTS):
                            step(0, u)
                        with eng.Fori(1, NT // SLOTS) as j:
                            for u in range(SLOTS):
                                step(j, u)

                    def later(j):
                        return not (isinstance(j, int) and j == 0)

                    @block.gpsimd
                    def _(pool):
                        G = nc.gpsimd

                        def step(j, u):
                            t = j * SLOTS + u
                            if later(j):
                                pool.wait_ge(out_psum, t + (1 - SLOTS))
                                pool.sem_inc(idx_seen, 1)
                            G.tensor_copy(idx[u][:, :], index[:, ds(t, 1), :].rearrange("p a k -> p (a k)")).then_inc(idx_ready, 1)
                            pool.wait_ge(idx_ready, t + 1)
                            pool.sem_inc(idx_seen, 1)
                            for k in range(HEADS):
                                G.indirect_dma_start(quad[u][k][:, :], None, table,
                                                     bass.IndirectOffsetOnAxis(ap=idx[u][:, k:k + 1], axis=0)) \
                                    .then_inc(landed[u][k], 16)

                        tiles(pool, step)

                    @block.vector
                    def _(dve):
                        V = nc.vector

                        def step(j, u):
                            t = j * SLOTS + u
                            sums = [ps[:, 6, i * C:(i + 1) * C] for i in range(2)]
                            for n, (k, q) in enumerate(ON_DVE):
                                if n == 0 or ON_DVE[n - 1][0] != k:
                                    dve.wait_ge(landed[u][k], j * 16 + 16)
                                src = quad[u][k][:, q * C:(q + 1) * C]
                                w = weights[:, ds(t, 1), k, q]
                                s = sums[n % 2]
                                o = acc[u][:, n % 2, :] if n >= ND - 2 else s
                                if not (isinstance(t, int) and t == 0 and n < 2):
                                    dve.wait_ge(added, t * ND + (n - 1))
                                if n == ND - 2 and later(j):
                                    dve.wait_ge(out_psum, t + (1 - SLOTS))
                                if n < 2:
                                    V.tensor_scalar(o, src, w, None, ALU.mult).then_inc(added, 1)
                                else:
                                    V.scalar_tensor_tensor(o, src, w, s, ALU.mult, ALU.add).then_inc(added, 1)

                        tiles(dve, step)

                    @block.scalar
                    def _(act):
                        S = nc.scalar

                        def diags(j, u):
                            t = j * SLOTS + u
                            if later(j):
                                act.wait_ge(out_psum, t + (1 - SLOTS))
                            for n, (k, q) in enumerate(ON_PE):
                                S.activation(diag[u][n][:, :], ident[:, :], ACT.Copy, scale=weights[:, ds(t, 1), k, q]) \
                                    .then_inc(diag_ready, 1)

                        def result(j, u):
                            t = j * SLOTS + u
                            act.wait_ge(out_psum, t + 1)
                            if later(j):
                                act.wait_ge(written[u], j * 16)
                            S.copy(ob[u][:, :, :], ps[:, 2 * u:2 * u + 2, 0:P]).then_inc(out_ready, 1)

                        diags(0, 0)
                        for u in range(SLOTS - 1):
                            diags(0, u + 1)
                            result(0, u)
                        diags(1, 0)
                        result(0, SLOTS - 1)
                        with act.Fori(1, NT // SLOTS - 1) as j:
                            for u in range(SLOTS - 1):
                                diags(j, u + 1)
                                result(j, u)
                            diags(j + 1, 0)
                            result(j, SLOTS - 1)
                        last = NT // SLOTS - 1
                        for u in range(SLOTS - 1):
                            diags(last, u + 1)
                            result(last, u)
                        result(last, SLOTS - 1)

                    @block.tensor
                    def _(pe):
                        T = nc.tensor

                        def step(j, u):
                            t = j * SLOTS + u
                            o = [ps[:, 2 * u + cb, 0:P] for cb in range(CB)]
                            if later(j):
                                pe.wait_ge(out_ready, t + (1 - SLOTS))
                            for cb in range(CB):
                                T.matmul(o[cb], ident[:, :], xs[:, cb, ds(t * P, P)], start=True, stop=False, skip_group_check=True)
                            for n, (k, q) in enumerate(ON_PE):
                                if n == 0 or ON_PE[n - 1][0] != k:
                                    pe.wait_ge(landed[u][k], j * 16 + 16)
                                pe.wait_ge(diag_ready, t * NP + (n + 1))
                                for cb in range(CB):
                                    T.matmul(o[cb], quad[u][k][:, q * C + cb * P:q * C + (cb + 1) * P], diag[u][n][:, :],
                                             start=False, stop=False, skip_group_check=True)
                            for i in range(2):
                                pe.wait_ge(added, t * ND + (ND - 1 + i))
                                for cb in range(CB):
                                    m = T.matmul(o[cb], acc[u][:, i, cb * P:(cb + 1) * P], ident[:, :],
                                                 start=False, stop=i == 1, skip_group_check=True)
                            m.then_inc(out_psum, 1)

                        tiles(pe, step)

                    @block.sync
                    def _(sp):
                        def step(j, u):
                            t = j * SLOTS + u
                            sp.wait_ge(out_ready, t + 1)
                            sp.dma_start(out_c[:, :, ds(t * P, P)], ob[u][:, :, :]).then_inc(written[u], 16)

                        tiles(sp, step)
                        for u in range(SLOTS):
                            sp.wait_ge(written[u], 16 * (NT // SLOTS))


def kernel(**inputs):
    import concourse.bacc as _bacc
    from concourse import mybir as _mybir
    from concourse.bass_utils import run_bass_kernel_spmd as _run

    g = {n: np.asarray(a) for n, a in inputs.items()}
    laid = {
        "x": g["x"],
        "WqT": g["L0_conv_Wq"].T, "bq": g["L0_conv_bq"],
        "WvT": g["L0_conv_Wv"].T, "bv": g["L0_conv_bv"].reshape(CB, P).T,
        "WpT": np.concatenate([g["L1_conv_Wc"], g["L1_conv_Woff"].reshape(2 * HEADS, C), g["L1_conv_Wwt"]]).T,
        "bp": np.concatenate([g["L1_conv_bc"], g["L1_conv_boff"].reshape(-1), g["L1_conv_bwt"]]),
    }
    nc = _bacc.Bacc("TRN2", target_bir_lowering=False, num_devices=1)
    arrays, args = {}, []
    for name, a in laid.items():
        a = np.ascontiguousarray(a)
        arrays[f"in_{name}_dram"] = a
        args.append(nc.dram_tensor(f"in_{name}_dram", a.shape, _mybir.dt.from_np(a.dtype), kind="ExternalInput").ap())
    args.append(nc.dram_tensor("out_0_dram", (1, C, H, W), _mybir.dt.from_np(np.dtype("float32")),
                               kind="ExternalOutput").ap())
    build(nc, *args)
    r = _run(nc, [arrays], core_ids=[0])
    return r.results[0]["out_0_dram"]
```

```python
from contextlib import ExitStack

import numpy as np

import concourse.bass as bass
from concourse import mybir

F32 = mybir.dt.float32
BF16 = mybir.dt.bfloat16
U32 = mybir.dt.uint32
ALU = mybir.AluOpType
ACT = mybir.ActivationFunctionType
AX_X = mybir.AxisListType.X
ds = bass.ds

P = 128
C, H, W = 256, 96, 96
HW = H * W
CB = C // P
NT = HW // P
GROUPS = 32
PER_GROUP = C // GROUPS
EPS = 1e-5
HEADS = 4
NFLOW = 3 * HEADS
NPROJ = C + NFLOW
LEVELS = 255.0
ROUND = 1.5 * 2.0 ** 23
CHUNK = 512
NCH = HW // CHUNK
QCH = 768
NQ = HW // QCH
QT = QCH // P
CUT = int(0.05 * (H // 2))
SPLITS = 3
ROWS = 32
STACK = SPLITS * ROWS
PAIRS = ((0, 0), (1, 0), (2, 0), (0, 1), (0, 2), (1, 1))
BLOCKS = 8
THIRD = HW // 3
THIRD_TILES = THIRD // P


def bf16_bits(a):
    u = np.ascontiguousarray(a, np.float32).view(np.uint32).astype(np.uint64)
    return ((u + 0x7FFF + ((u >> 16) & 1)) >> 16).astype(np.uint16)


def from_bits(b):
    return (b.astype(np.uint32) << 16).view(np.float32)


def split3(a):
    out = []
    for _ in range(SPLITS):
        out.append(bf16_bits(a.astype(np.float32)))
        a = a - from_bits(out[-1])
    return out


def shape_constants():
    freqs = range(-CUT, CUT)
    alone = [(a, b) for a in freqs for b in freqs if -CUT in (a, b)]
    pairs = [(a, b) for a in range(CUT) for b in range(-CUT + 1, CUT) if a > 0 or b > 0]
    yy, xx = np.divmod(np.arange(HW), W)
    n_a, n_p = len(alone), len(pairs)

    def phase(ab):
        return 2 * np.pi * ((ab[0] * yy + ab[1] * xx) % W) / W

    fns = [np.cos(phase(f)) for f in alone] + [np.sin(phase(f)) for f in alone]
    fns += [np.cos(phase(f)) for f in pairs] + [np.sin(phase(f)) for f in pairs] + [np.ones(HW)]
    n = len(fns)
    assert n <= ROWS
    basis = np.zeros((ROWS, HW))
    basis[:n] = fns
    b1, b2, b3 = split3(basis)
    ana = np.zeros((P, NT, P), np.uint16)
    ana[:, :, :STACK] = np.stack([b1, b2, b3], 0).reshape(STACK, NT, P).transpose(2, 1, 0)
    syn = np.stack([np.concatenate([b1, b1, b1]), np.concatenate([b2, b3, b2])], 1)
    m = 2 * n_a
    assert len(PAIRS) * m <= STACK
    syn_i = np.zeros((STACK, HW), np.uint16)
    which = np.zeros((STACK, SPLITS), np.float32)
    for i, (cs, bs) in enumerate(PAIRS):
        syn_i[i * m:(i + 1) * m] = (b1, b2, b3)[bs][:m]
        which[i * m:(i + 1) * m, cs] = 1.0
    syn = np.stack([syn[:, 0], syn[:, 1], syn_i], 1)
    sel = np.zeros((STACK, 2, STACK), np.float32)
    for s in range(SPLITS):
        for to in range(SPLITS):
            for j in range(n):
                sel[s * ROWS + j, 0, to * ROWS + j] = 2.0 if 2 * n_a <= j < 2 * n_a + 2 * n_p else 1.0
        for i in range(len(PAIRS)):
            for j in range(n_a):
                sel[s * ROWS + j, 1, i * m + n_a + j] = 1.0
                sel[s * ROWS + n_a + j, 1, i * m + j] = -1.0
    group = np.zeros((P, P), np.float32)
    for c in range(P):
        group[c, c // PER_GROUP * PER_GROUP:(c // PER_GROUP + 1) * PER_GROUP] = 1.0 / PER_GROUP
    pick = np.zeros((P, 3, C), np.float32)
    for s in range(SPLITS):
        for t in range(3):
            for c in range(C):
                pick[s * BLOCKS + 3 * (3 * c + t) % BLOCKS, t, c] = 1.0
    grid = np.zeros((P, NT, HEADS, 2), np.float32)
    gx, gy = xx.reshape(NT, P).T, yy.reshape(NT, P).T
    grid[..., 0] = (gx * (W / (W - 1.0)) - 0.5)[:, :, None]
    grid[..., 1] = (gy * (H / (H - 1.0)) - 0.5)[:, :, None]
    return {
        "ana": ana, "syn": np.ascontiguousarray(syn), "sel": sel, "group": group,
        "which": which, "pick": bf16_bits(pick), "grid": grid.reshape(P, NT, 2 * HEADS),
        "ident": np.eye(P, dtype=np.float32), "identb": bf16_bits(np.eye(P)),
    }


def build(nc, x, WqT, bq, WvT, bv, WpT, bp, out):
    const = shape_constants()
    k_ = {n: nc.inline_tensor(a, name="const_" + n).ap() for n, a in const.items()}
    x_c = x.rearrange("a (t p) h w -> t p (a h w)", p=P)
    out_c = out.rearrange("a (t p) h w -> p (a t) (h w)", p=P)
    table = nc.dram_tensor("table", (HW + W, 2 * C), F32, kind="Internal").ap()

    with ExitStack() as ctx:
        def sb(name, shape, dt=F32):
            return ctx.enter_context(nc.sbuf_tensor(name, shape, dt))

        def sem(name):
            return ctx.enter_context(nc.semaphore(name))

        ps = ctx.enter_context(nc.psum_tensor("ps", [P, 8, CHUNK], F32))
        xs = sb("xs", [P, CB, HW])
        ident = sb("ident", [P, P])
        identb = sb("identb", [P, P], BF16)
        group = sb("group", [P, P])
        small = sb("small", [P, 256])
        wp = sb("wp", [P, CB, NPROJ])
        link_sem = sem("link_sem")
        linked = [0]

        def link(eng, ins):
            linked[0] += 1
            ins.then_inc(link_sem, 1)
            eng.wait_ge(link_sem, linked[0])

        col = {}

        def column(name, n=1):
            if name not in col:
                col[name] = (sum(w for _, w in col.values()), n)
            a, w = col[name]
            return small[:, a:a + w]

        for nme in ("mean", "var", "rstd", "nmr", "mg", "mn", "sc", "bvp", "mean1", "var1", "rstd1", "nmr1"):
            column(nme, CB)
        for nme in ("d", "e", "mx_", "ptp", "rp"):
            column(nme, CB)
        column("mv", 2 * CB)
        column("minus_round", 1)
        column("minus_one", 1)
        column("one", 1)
        column("eye3", 3)

        with ExitStack() as c0:
            def sb0(name, shape, dt=F32):
                return c0.enter_context(nc.sbuf_tensor(name, shape, dt))

            v = sb0("v", [P, CB, HW])
            wq = sb0("wq", [P, CB, C])
            bq3 = sb0("bq3", [3, C])
            bqs = sb0("bqs", [P, C], BF16)
            ones = sb0("ones", [P, P], BF16)
            pick = sb0("pick", [P, 3, C], BF16)
            coef = sb0("coef", [STACK, CB * P])
            mask = sb0("mask", [P, THIRD], BF16)

            with ExitStack() as c1:
                def sb1(name, shape, dt=F32):
                    return c1.enter_context(nc.sbuf_tensor(name, shape, dt))

                ana = sb1("ana", [P, NT, P], BF16)
                wv = sb1("wv", [P, CB, C])
                wvs = sb1("wvs", [P, CB, C])
                stats = sb1("stats", [P, CB, NCH, 6])
                mxs = sb1("mxs", [P, CB, NQ])
                mns = sb1("mns", [P, CB, NQ])
                a_ring = [sb1(f"a_ring{i}", [P, QCH]) for i in range(2)]
                t_ring = [sb1(f"t_ring{i}", [P, QCH]) for i in range(2)]
                u_ring = [sb1(f"u_ring{i}", [P, QCH]) for i in range(2)]
                qt_ring = [sb1(f"qt_ring{i}", [P, QT, P], BF16) for i in range(2)]

                PIECES = 3
                x_landed = [[sem(f"x_landed{t}{i}") for i in range(PIECES)] for t in range(CB)]
                w_landed = sem("w_landed")
                ana_landed = sem("ana_landed")
                c_landed = sem("c_landed")
                bq_landed = sem("bq_landed")
                stats_done = sem("stats_done")
                mean_in = sem("mean_in")
                mean_out = sem("mean_out")
                var_in = sem("var_in")
                var_out = sem("var_out")
                std_in = sem("std_in")
                std_out = sem("std_out")
                norm_ready = sem("norm_ready")
                wvs_ready = sem("wvs_ready")
                bvp_out = sem("bvp_out")
                bvp_ready = sem("bvp_ready")
                abs_ready = sem("abs_ready")
                abs_free = sem("abs_free")
                minmax_done = sem("minmax_done")
                t_done = sem("t_done")
                u_ready = sem("u_ready")
                transposed = sem("transposed")
                qt_ready = sem("qt_ready")
                qt_free = sem("qt_free")
                v_psum = sem("v_psum")
                v_free = sem("v_free")
                cst_ready = sem("cst_ready")

                def q_psum(slot):
                    return ps[:, 2 * slot:2 * slot + 2, :].rearrange("p b n -> p (b n)")[:, 0:QCH]

                PRE = CB * NQ

                with nc.Block(no_gpsimd_drain=True) as block:
                    @block.sync
                    def _(sp):
                        n = HW // PIECES
                        for t in range(CB):
                            for i in range(PIECES):
                                sp.dma_start(xs[:, t, i * n:(i + 1) * n], x_c[t][:, i * n:(i + 1) * n]) \
                                    .then_inc(x_landed[t][i], 16)
                                if t == 0 and i == 0:
                                    sp.dma_start(group[:, :], k_["group"]).then_inc(c_landed, 16)
                                    sp.dma_start(ident[:, :], k_["ident"]).then_inc(c_landed, 16)
                        sp.dma_start(wv[:, :, :], WvT.rearrange("(t p) n -> p t n", p=P)).then_inc(w_landed, 16)
                        sp.dma_start(column("bvp"), bv).then_inc(w_landed, 16)
                        sp.dma_start(ana[:, :, :], k_["ana"].bitcast(BF16)).then_inc(ana_landed, 16)
                        sp.dma_start(identb[:, :], k_["identb"].bitcast(BF16)).then_inc(bq_landed, 16)
                        sp.dma_start(wq[:, :, :], WqT.rearrange("(t p) n -> p t n", p=P)).then_inc(bq_landed, 16)
                        sp.dma_start(wp[:, :, :], WpT.rearrange("(t p) n -> p t n", p=P)).then_inc(bq_landed, 16)
                        sp.dma_start(pick[:, :, :], k_["pick"].bitcast(BF16)).then_inc(bq_landed, 16)
                        for r in range(3):
                            sp.dma_start(bq3[r:r + 1, :], bq.rearrange("(a n) -> a n", a=1)).then_inc(bq_landed, 16)
                        sp.dma_start(column("eye3")[0:3, :], k_["ident"][0:3, 0:3]).then_inc(bq_landed, 16)
                        sp.wait_ge(bq_landed, 16 * 8)
                        sp.wait_ge(ana_landed, 16)

                    @block.vector
                    def _(dve):
                        V = nc.vector
                        V.memset(column("minus_round"), -ROUND).then_inc(cst_ready, 1)
                        V.memset(column("minus_one"), -1.0).then_inc(cst_ready, 1)
                        V.memset(column("one"), 1.0).then_inc(cst_ready, 1)
                        V.memset(ones[:, :], 1.0).then_inc(cst_ready, 1)
                        V.memset(bqs[:, :], 0.0).then_inc(cst_ready, 1)
                        V.memset(mask[:, :], 0.0).then_inc(cst_ready, 1)
                        for t in range(CB):
                            per = NCH // PIECES
                            for i in range(PIECES):
                                dve.wait_ge(x_landed[t][i], 16)
                                with dve.Fori(0, per) as j:
                                    V.bn_stats(stats[:, t, ds(j + i * per, 1), :],
                                               xs[:, t, ds(j * CHUNK + i * per * CHUNK, CHUNK)]).then_inc(stats_done, 1)
                            dve.wait_ge(stats_done, NCH * (t + 1))
                            mean, var = column("mv")[:, 2 * t:2 * t + 1], column("mv")[:, 2 * t + 1:2 * t + 2]
                            V.bn_aggr(column("mv")[:, 2 * t:2 * t + 2],
                                      stats[:, t, :, :].rearrange("p a b -> p (a b)")).then_inc(mean_in, 1)
                            dve.wait_ge(mean_in, t + 1)
                            dve.wait_ge(mean_out, t + 1)
                            link(dve, V.tensor_copy(column("mg")[:, t:t + 1], ps[:, 7, 0:1]))
                            link(dve, V.tensor_tensor(column("d")[:, t:t + 1], mean, column("mg")[:, t:t + 1], ALU.subtract))
                            link(dve, V.tensor_tensor(column("d")[:, t:t + 1], column("d")[:, t:t + 1],
                                                      column("d")[:, t:t + 1], ALU.mult))
                            V.tensor_tensor(column("e")[:, t:t + 1], column("d")[:, t:t + 1], var, ALU.add).then_inc(var_in, 1)
                            dve.wait_ge(var_out, t + 1)
                            V.tensor_scalar(column("var")[:, t:t + 1], ps[:, 7, 1:2], EPS, None, ALU.add).then_inc(std_in, 1)
                            dve.wait_ge(std_out, t + 1)
                            link(dve, V.reciprocal(column("rstd")[:, t:t + 1], column("e")[:, t:t + 1]))
                            V.scalar_tensor_tensor(column("nmr")[:, t:t + 1], column("mg")[:, t:t + 1], -1.0,
                                                   column("rstd")[:, t:t + 1], ALU.mult, ALU.mult).then_inc(norm_ready, 1)
                        dve.wait_ge(w_landed, 32)
                        for t in range(CB):
                            V.tensor_scalar(wvs[:, t, :], wv[:, t, :], column("rstd")[:, t:t + 1], None,
                                            ALU.mult).then_inc(wvs_ready, 1)
                        dve.wait_ge(norm_ready, CB)
                        dve.wait_ge(bvp_out, 1)
                        V.tensor_tensor(column("bvp"), column("bvp"), ps[:, 7, 2:4], ALU.add).then_inc(bvp_ready, 1)
                        for t in range(CB):
                            with dve.Fori(0, NQ // 2) as j:
                                for u in range(2):
                                    dve.wait_ge(abs_ready, j * 2 + (t * NQ + u + 1))
                                    V.tensor_reduce(mxs[:, t, ds(j * 2 + u, 1)], a_ring[u][:, :], AX_X, ALU.max).then_inc(minmax_done, 1)
                                    V.tensor_reduce(mns[:, t, ds(j * 2 + u, 1)], a_ring[u][:, :], AX_X, ALU.min).then_inc(abs_free, 1)
                            dve.wait_ge(minmax_done, NQ * (t + 1))
                            dve.wait_ge(abs_free, NQ * (t + 1))
                            one = slice(t, t + 1)
                            link(dve, V.tensor_reduce(column("mx_")[:, one], mxs[:, t, :], AX_X, ALU.max))
                            link(dve, V.tensor_reduce(column("mn")[:, one], mns[:, t, :], AX_X, ALU.min))
                            link(dve, V.tensor_tensor(column("ptp")[:, one], column("mx_")[:, one], column("mn")[:, one],
                                                      ALU.subtract))
                            link(dve, V.reciprocal(column("rp")[:, one], column("ptp")[:, one]))
                            link(dve, V.tensor_scalar(column("sc")[:, one], column("rp")[:, one],
                                                      LEVELS * (1 + 2.0 ** -22), None, ALU.mult))
                        for t in range(CB):
                            with dve.Fori(0, NQ // 2) as j:
                                for u in range(2):
                                    n = j * 2 + (t * NQ + u + 1)
                                    dve.wait_ge(abs_ready, n + CB * NQ)
                                    dve.wait_ge(transposed, n)
                                    V.tensor_scalar(t_ring[u][:, :], a_ring[u][:, :], column("mn")[:, t:t + 1],
                                                    column("sc")[:, t:t + 1], ALU.subtract, ALU.mult).then_inc(abs_free, 1)
                                    dve.wait_ge(abs_free, n + CB * NQ)
                                    V.tensor_scalar(u_ring[u][:, :], t_ring[u][:, :], -0.5 + 2.0 ** -16, ROUND,
                                                    ALU.add, ALU.add).then_inc(u_ready, 1)

                    @block.scalar
                    def _(act):
                        S = nc.scalar
                        for t in range(CB):
                            act.wait_ge(std_in, t + 1)
                            S.activation(column("e")[:, t:t + 1], column("var")[:, t:t + 1], ACT.Sqrt).then_inc(std_out, 1)

                        def absolute(t, j, u):
                            S.activation(a_ring[u][:, :], xs[:, t, ds(j * (2 * QCH) + u * QCH, QCH)], ACT.Abs,
                                         scale=column("rstd")[:, t:t + 1], bias=column("nmr")[:, t:t + 1]).then_inc(abs_ready, 1)

                        def v_out(n, chunk, ob, slot):
                            act.wait_ge(v_psum, n + 1)
                            S.activation(v[:, ob, ds(chunk * CHUNK, CHUNK)], ps[:, 4 + slot, :], ACT.Identity,
                                         bias=column("bvp")[:, ob:ob + 1]).then_inc(v_free, 1)

                        half = NQ // 2
                        act.wait_ge(norm_ready, 1)
                        absolute(0, 0, 0)
                        absolute(0, 0, 1)
                        act.wait_ge(norm_ready, CB)
                        act.wait_ge(bvp_ready, 1)
                        for t in range(CB):
                            with act.Fori(0, half - 1) as j:
                                for u in range(2):
                                    n = j * 2 + (t * NQ + u)
                                    act.wait_ge(abs_free, n + 1)
                                    absolute(t, j + 1, u)
                                    v_out(n, j + t * half, u, u)
                            for u in range(2):
                                n = (t + 1) * NQ - 2 + u
                                act.wait_ge(abs_free, n + 1)
                                absolute((t + 1) % CB, 0, u)
                                v_out(n, n // 2, u, u)
                        act.wait_ge(cst_ready, 4)

                        def q_out(t, j, u, nxt):
                            n = j * 2 + (t * NQ + u)
                            if nxt is not None:
                                act.wait_ge(abs_free, n + (CB * NQ + 1))
                                absolute(nxt[0], nxt[1], u)
                            act.wait_ge(transposed, n + 3)
                            act.wait_ge(qt_free, n + 1)
                            S.activation(qt_ring[u][:, :, :].rearrange("p a b -> p (a b)"), q_psum(u), ACT.Identity,
                                         bias=column("minus_round")).then_inc(qt_ready, 1)
                            before = isinstance(j, int) and (t, j, u) == (0, 0, 0)
                            after = isinstance(j, int) and (t, j, u) > (1, 0, 0) or t > 0 and not isinstance(j, int)
                            if not before and not after:
                                v_out(n + (PRE - 1), j + ((PRE + t * NQ) // 2 + u - 1), 1 - u, 1 - u)

                        for t in range(CB):
                            for u in range(2):
                                q_out(t, 0, u, (t, 1))
                            with act.Fori(1, half - 1) as j:
                                for u in range(2):
                                    q_out(t, j, u, (t, j + 1))
                            for u in range(2):
                                q_out(t, half - 1, u, (t + 1, 0) if t + 1 < CB else None)

                    @block.tensor
                    def _(pe):
                        T = nc.tensor
                        pe.wait_ge(c_landed, 32)
                        for t in range(CB):
                            pe.wait_ge(mean_in, t + 1)
                            T.matmul(ps[:, 7, 0:1], group[:, :], column("mv")[:, 2 * t:2 * t + 1],
                                     start=True, stop=True).then_inc(mean_out, 1)
                            pe.wait_ge(var_in, t + 1)
                            T.matmul(ps[:, 7, 1:2], group[:, :], column("e")[:, t:t + 1],
                                     start=True, stop=True).then_inc(var_out, 1)
                        pe.wait_ge(norm_ready, CB)
                        pe.wait_ge(w_landed, 32)
                        for ob in range(CB):
                            for kb in range(CB):
                                m = T.matmul(ps[:, 7, 2 + ob:3 + ob], wv[:, kb, ob * P:(ob + 1) * P],
                                             column("nmr")[:, kb:kb + 1], start=kb == 0, stop=kb == CB - 1)
                        m.then_inc(bvp_out, 1)
                        pe.wait_ge(wvs_ready, CB)
                        pe.sem_inc(v_free, 2)
                        pe.sem_inc(transposed, 2)
                        pe.sem_inc(qt_free, 2)

                        def v_unit(n, chunk, ob):
                            pe.wait_ge(v_free, n + 1)
                            for kb in range(CB):
                                m = T.matmul(ps[:, 4 + ob, :], wvs[:, kb, ob * P:(ob + 1) * P],
                                             xs[:, kb, ds(chunk * CHUNK, CHUNK)], start=kb == 0, stop=kb == CB - 1)
                            m.then_inc(v_psum, 1)

                        with pe.Fori(0, PRE // 2) as j:
                            for u in range(2):
                                v_unit(j * 2 + u, j, u)
                        pe.wait_ge(ana_landed, 16)

                        def turn(n, u):
                            pe.wait_ge(u_ready, n + 1)
                            for i in range(QT):
                                m = T.transpose(q_psum(u)[:, i * P:(i + 1) * P], u_ring[u][:, i * P:(i + 1) * P], ident[:, :])
                            m.then_inc(transposed, 1)

                        def q_step(t, j, first=False, last=False):
                            for u in range(2):
                                n = j * 2 + (t * NQ + u)
                                if not (last and u == 1 and t == CB - 1):
                                    turn(n + 1, 1 - u)
                                if t == 0:
                                    v_unit(n + PRE, j + PRE // 2, u)
                                pe.wait_ge(qt_ready, n + 1)
                                for i in range(QT):
                                    m = T.matmul(ps[:, 6, t * P:(t + 1) * P],
                                                 ana[:, ds(j * (2 * QT) + (u * QT + i), 1), :].rearrange("p a n -> p (a n)"),
                                                 qt_ring[u][:, i, :], start=first and u == 0 and i == 0,
                                                 stop=last and u == 1 and i == QT - 1, skip_group_check=True)
                                m.then_inc(qt_free, 1)

                        turn(0, 0)
                        for t in range(CB):
                            q_step(t, 0, first=True)
                            with pe.Fori(1, NQ // 2 - 1) as j:
                                q_step(t, j)
                            q_step(t, NQ // 2 - 1, last=True)

            with ExitStack() as c2:
                def sb2(name, shape, dt=F32):
                    return c2.enter_context(nc.sbuf_tensor(name, shape, dt))

                sel = sb2("sel", [STACK, 2, STACK])
                rest = sb2("rest", [STACK, 2, C])
                part = [sb2(f"part{i}", [STACK, 2, C], BF16) for i in range(SPLITS)]
                stack_a = sb2("stack_a", [STACK, C], BF16)
                stack_b = sb2("stack_b", [STACK, C], BF16)
                stack_i = sb2("stack_i", [STACK, C], BF16)
                sum_i = [sb2(f"sum_i{i}", [STACK, C]) for i in range(2)]
                which = sb2("which", [STACK, SPLITS])
                syn_ring = [sb2(f"syn_ring{i}", [STACK, 3, CHUNK], BF16) for i in range(2)]
                sq_ring = [sb2(f"sq_ring{i}", [P, 2, CHUNK]) for i in range(2)]
                s2_ring = [sb2(f"s2_ring{i}", [P, CHUNK]) for i in range(2)]
                fq_ring = [sb2(f"fq_ring{i}", [P, CB, CHUNK]) for i in range(2)]
                bqf = [sb2(f"bqf{i}", [3, C]) for i in range(2)]
                bqp = [sb2(f"bqp{i}", [3, C], BF16) for i in range(3)]
                bqm = [sb2(f"bqm{i}", [3, C]) for i in range(2)]
                row_max = sb2("row_max", [P, NT, BLOCKS])
                m_f = sb2("m_f", [P, THIRD_TILES, BLOCKS])
                m_r = sb2("m_r", [P, THIRD_TILES, BLOCKS])
                m_p = sb2("m_p", [P, THIRD_TILES, SPLITS, BLOCKS], BF16)

                TPC = CHUNK // P
                sel_landed = sem("sel_landed")
                syn_landed = [sem(f"syn_landed{i}") for i in range(2)]
                ri_ready = sem("ri_ready")
                sq_ready = sem("sq_ready")
                s2_ready = sem("s2_ready")
                fq_ready = sem("fq_ready")
                q_ready = sem("q_ready")
                q_free = sem("q_free")
                coef_ready = sem("coef_ready")
                summed = sem("summed")
                stacks_ready = sem("stacks_ready")
                bias_ready = sem("bias_ready")
                m_ready = sem("m_ready")
                m_turned = sem("m_turned")

                with nc.Block(no_gpsimd_drain=True) as block:
                    @block.sync
                    def _(sp):
                        sp.dma_start(sel[:, :, :], k_["sel"]).then_inc(sel_landed, 16)
                        sp.dma_start(which[:, :], k_["which"]).then_inc(sel_landed, 16)

                        def load(j, u):
                            sp.dma_start(syn_ring[u][:, :, :], k_["syn"].bitcast(BF16)[:, :, ds(j * (2 * CHUNK) + u * CHUNK, CHUNK)]) \
                                .then_inc(syn_landed[u], 16)

                        load(0, 0)
                        load(0, 1)
                        with sp.Fori(1, NCH // 2) as j:
                            for u in range(2):
                                sp.wait_ge(ri_ready, j * 4 + (2 * u - 2))
                                load(j, u)

                    @block.vector
                    def _(dve):
                        V = nc.vector
                        V.tensor_copy(coef[:, :], ps[0:STACK, 6, 0:CB * P]).then_inc(coef_ready, 1)
                        dve.wait_ge(summed, 1)
                        sums = ps[0:STACK, 4, :].rearrange("p (a n) -> p a n", a=2)
                        link(dve, V.tensor_copy(part[0][:, :, :], sums))
                        link(dve, V.tensor_tensor(rest[:, :, :], sums, part[0][:, :, :], ALU.subtract))
                        link(dve, V.tensor_copy(part[1][:, :, :], rest[:, :, :]))
                        link(dve, V.tensor_tensor(rest[:, :, :], rest[:, :, :], part[1][:, :, :], ALU.subtract))
                        V.tensor_scalar(sum_i[0][:, :], part[0][:, 1, :], which[:, 0:1], None, ALU.mult)
                        link(dve, V.tensor_copy(part[2][:, :, :], rest[:, :, :]))
                        for s, (a, b) in enumerate(((0, 0), (1, 0), (2, 1))):
                            r = slice(s * ROWS, (s + 1) * ROWS)
                            V.tensor_copy(stack_a[r, :], part[a][r, 0, :]).then_inc(stacks_ready, 1)
                            V.tensor_copy(stack_b[r, :], part[b][r, 0, :]).then_inc(stacks_ready, 1)
                        link(dve, V.scalar_tensor_tensor(sum_i[1][:, :], part[1][:, 1, :], which[:, 1:2], sum_i[0][:, :],
                                                         ALU.mult, ALU.add))
                        V.scalar_tensor_tensor(stack_i[:, :], part[2][:, 1, :], which[:, 2:3], sum_i[1][:, :],
                                               ALU.mult, ALU.add).then_inc(stacks_ready, 1)
                        link(dve, V.tensor_copy(bqp[0][:, :], bq3[:, :]))
                        link(dve, V.tensor_tensor(bqf[0][:, :], bq3[:, :], bqp[0][:, :], ALU.subtract))
                        link(dve, V.tensor_copy(bqp[1][:, :], bqf[0][:, :]))
                        link(dve, V.tensor_tensor(bqf[1][:, :], bqf[0][:, :], bqp[1][:, :], ALU.subtract))
                        link(dve, V.tensor_copy(bqp[2][:, :], bqf[1][:, :]))
                        eye = column("eye3")
                        link(dve, V.tensor_scalar(bqm[0][:, :], bqp[0][:, :], eye[0:3, 0:1], None, ALU.mult))
                        link(dve, V.scalar_tensor_tensor(bqm[1][:, :], bqp[1][:, :], eye[0:3, 1:2], bqm[0][:, :],
                                                         ALU.mult, ALU.add))
                        V.scalar_tensor_tensor(bqs[0:3, :], bqp[2][:, :], eye[0:3, 2:3], bqm[1][:, :],
                                               ALU.mult, ALU.add).then_inc(bias_ready, 1)
                        dve.sem_inc(q_free, 2)

                        def squares(j, u):
                            for cb in range(CB):
                                n = j * 4 + (2 * u + cb)
                                dve.wait_ge(sq_ready, n + 3)
                                dve.wait_ge(fq_ready, n + 1)
                                V.tensor_tensor(s2_ring[cb][:, :], sq_ring[cb][:, 0, :], sq_ring[cb][:, 1, :],
                                                ALU.add).then_inc(s2_ready, 1)

                        def maxima(j, u):
                            dve.wait_ge(q_ready, j * 2 + (u + 3))
                            V.tensor_reduce(row_max[:, ds(j * (2 * TPC) + u * TPC, TPC), :],
                                            ps[:, 4 + 2 * u:6 + 2 * u, :].rearrange(
                                                "p b (t g r) -> p (b t) r g", t=2, r=BLOCKS), AX_X, ALU.max).then_inc(q_free, 1)

                        last = NCH // 2 - 1
                        squares(0, 0)
                        with dve.Fori(0, last) as j:
                            squares(j, 1)
                            maxima(j, 0)
                            squares(j + 1, 0)
                            maxima(j, 1)
                        squares(last, 1)
                        maxima(last, 0)
                        maxima(last, 1)
                        dve.wait_ge(q_free, NCH + 2)
                        third = [row_max[:, t * THIRD_TILES:(t + 1) * THIRD_TILES, :] for t in range(3)]
                        for t in range(1, 3):
                            so_far = third[0] if t == 1 else m_f[:, :, :]
                            cut = 3 * t % BLOCKS
                            V.tensor_tensor(m_f[:, :, cut:BLOCKS], so_far[:, :, cut:BLOCKS], third[t][:, :, 0:BLOCKS - cut],
                                            ALU.max)
                            link(dve, V.tensor_tensor(m_f[:, :, 0:cut], so_far[:, :, 0:cut], third[t][:, :, BLOCKS - cut:BLOCKS],
                                                      ALU.max))
                        link(dve, V.tensor_copy(m_p[:, :, 0, :], m_f[:, :, :]))
                        link(dve, V.tensor_tensor(m_r[:, :, :], m_f[:, :, :], m_p[:, :, 0, :], ALU.subtract))
                        link(dve, V.tensor_copy(m_p[:, :, 1, :], m_r[:, :, :]))
                        link(dve, V.tensor_tensor(m_f[:, :, :], m_r[:, :, :], m_p[:, :, 1, :], ALU.subtract))
                        V.tensor_copy(m_p[:, :, 2, :], m_f[:, :, :]).then_inc(m_ready, 1)
                        dve.wait_ge(m_turned, 1)
                        V.tensor_copy(mask[0:SPLITS * BLOCKS, :], ps[0:SPLITS * BLOCKS, 0:3, :].rearrange("p b n -> p (b n)")
                                      .bitcast(BF16)[:, 0:THIRD])

                    @block.scalar
                    def _(act):
                        S = nc.scalar
                        act.sem_inc(sq_ready, 2)
                        act.sem_inc(fq_ready, 2)
                        with act.Fori(0, NCH // 2) as j:
                            for u in range(2):
                                for cb in range(CB):
                                    n = j * 4 + (2 * u + cb)
                                    act.wait_ge(ri_ready, n + 1)
                                    S.activation(sq_ring[cb][:, :, :], ps[:, 2 * cb:2 * cb + 2, :], ACT.Square,
                                                 scale=1.0 / HW).then_inc(sq_ready, 1)
                                for cb in range(CB):
                                    n = j * 4 + (2 * u + cb)
                                    act.wait_ge(s2_ready, n + 1)
                                    if cb == 0:
                                        act.wait_ge(q_ready, j * 2 + (u + 1))
                                    S.activation(fq_ring[u][:, cb, :], s2_ring[cb][:, :], ACT.Sqrt).then_inc(fq_ready, 1)

                    @block.tensor
                    def _(pe):
                        T = nc.tensor
                        pe.wait_ge(sel_landed, 32)
                        pe.wait_ge(coef_ready, 1)
                        for i in range(2):
                            m = T.matmul(ps[0:STACK, 4, i * C:(i + 1) * C], sel[:, i, :], coef[:, :], start=True, stop=True)
                        m.then_inc(summed, 1)
                        pe.wait_ge(stacks_ready, 7)
                        pe.sem_inc(q_ready, 2)

                        def parts(j, u):
                            pe.wait_ge(syn_landed[u], j * 16 + 16)
                            for cb in range(CB):
                                n = j * 4 + (2 * u + cb)
                                pe.wait_ge(sq_ready, n + 1)
                                c = slice(cb * P, (cb + 1) * P)
                                T.matmul(ps[:, 2 * cb, :], stack_a[:, c], syn_ring[u][:, 0, :], start=True, stop=False)
                                T.matmul(ps[:, 2 * cb, :], stack_b[:, c], syn_ring[u][:, 1, :], start=False, stop=True)
                                m = T.matmul(ps[:, 2 * cb + 1, :], stack_i[:, c], syn_ring[u][:, 2, :], start=True, stop=True)
                                m.then_inc(ri_ready, 1)

                        def queries(j, u):
                            pe.wait_ge(fq_ready, j * 4 + (2 * u + 4))
                            pe.wait_ge(q_free, j * 2 + (u + 1))
                            for i in range(TPC):
                                o = ps[:, 4 + 2 * u + i // 2, (i % 2) * C:(i % 2 + 1) * C]
                                T.matmul(o, ones[:, :], bqs[:, :], start=True, stop=False)
                                for kb in range(CB):
                                    m = T.matmul(o, fq_ring[u][:, kb, i * P:(i + 1) * P], wq[:, kb, :],
                                                 start=False, stop=kb == CB - 1)
                                    if i == TPC - 1 and kb == CB - 1:
                                        m.then_inc(q_ready, 1)

                        parts(0, 0)
                        pe.wait_ge(bias_ready, 1)
                        with pe.Fori(0, NCH // 2 - 1) as j:
                            parts(j, 1)
                            queries(j, 0)
                            parts(j + 1, 0)
                            queries(j, 1)
                        last = NCH // 2 - 1
                        parts(last, 1)
                        queries(last, 0)
                        queries(last, 1)
                        pe.wait_ge(m_ready, 1)
                        for i in range(THIRD_TILES):
                            o = ps[0:SPLITS * BLOCKS, i * P // (2 * CHUNK), :].bitcast(BF16)
                            a = i * P % (2 * CHUNK)
                            m = T.transpose(o[:, a:a + P], m_p[:, i, :, :].rearrange("p s b -> p (s b)"), identb[:, :])
                        m.then_inc(m_turned, 1)

            with ExitStack() as c3:
                def sb3(name, shape, dt=F32):
                    return c3.enter_context(nc.sbuf_tensor(name, shape, dt))

                SLOTS = 3
                x1_ring = [sb3(f"x1_ring{i}", [P, CB, CHUNK]) for i in range(SLOTS)]
                stage = [[sb3(f"stage{i}{h}", [P, 2, C]) for h in range(2)] for i in range(SLOTS)]
                zeros = sb3("zeros", [W, C])
                stats = sb3("stats1", [P, CB, NCH, 6])
                mask_psum = sem("mask_psum")
                y_ready = sem("y_ready")
                y_seen = sem("y_seen")
                x1_ready = sem("x1_ready")
                stats1_done = sem("stats1_done")
                x1_turned = sem("x1_turned")
                x1_kept = sem("x1_kept")
                stage_ready = sem("stage_ready")
                zeros_ready = sem("zeros_ready")
                stored = [sem(f"stored{i}") for i in range(SLOTS)]
                edges_stored = sem("edges_stored")
                X_ROUNDS = NCH // SLOTS

                ROUNDS = NT // SLOTS
                AHEAD = 3
                MOST = (AHEAD - 1) * SLOTS
                QUAD = 4 * C
                FLOWS, LOGITS = slice(C, C + 2 * HEADS), slice(C + 2 * HEADS, NPROJ)
                SKIP = float(2 ** 20)
                ON_DVE = [(k, q) for k in range(HEADS) for q in range(3 if k < 2 else 2)]
                ON_PE = [(k, q) for k in range(HEADS) for q in range(4) if (k, q) not in ON_DVE]
                ND, NP = len(ON_DVE), len(ON_PE)

                weights = sb3("weights", [P, NT, HEADS, 4])
                wsum = sb3("wsum", [P, NT])
                index = sb3("index", [P, NT, HEADS])
                wps = sb3("wps", [P, CB, NPROJ])
                nmr_wide = sb3("nmr_wide", [P, CB, P])
                ones_row = sb3("ones_row", [P, P])
                bias_row = sb3("bias_row", [1, NPROJ])
                bias = sb3("bias", [P, NPROJ])
                grid = sb3("grid", [P, NT, 2 * HEADS])
                x_group = sb3("x_group", [P, CB, SLOTS * P])
                logit = sb3("logit", [P, MOST, HEADS])
                pos = sb3("pos", [P, MOST, 2 * HEADS])
                low = sb3("low", [P, MOST, 2 * HEADS])
                base = sb3("base", [P, MOST, 2 * HEADS])
                off = sb3("off", [P, MOST, 2 * HEADS])
                far = sb3("far", [P, MOST, 2 * HEADS])
                tent = [sb3(f"tent{i}", [P, MOST, 2 * HEADS]) for i in range(2)]
                row = sb3("row", [P, MOST, HEADS])
                top = sb3("top", [P, MOST])
                expo = sb3("expo", [P, MOST, HEADS])
                total = sb3("total", [P, MOST])
                share = sb3("share", [P, MOST])
                wy = [sb3(f"wy{i}", [P, MOST, HEADS]) for i in range(2)]
                used = [0]

                def from_v(*shape):
                    n = int(np.prod(shape))
                    a = v[:, :, :].rearrange("p c n -> p (c n)")[:, used[0]:used[0] + n]
                    used[0] += n
                    assert used[0] <= CB * HW
                    return a if len(shape) == 1 else a.rearrange("p (a n) -> p a n", n=shape[1])

                quad = [[from_v(QUAD) for _ in range(HEADS)] for _ in range(SLOTS)]
                idx = [sb3(f"idx{i}", [P, HEADS], U32) for i in range(SLOTS)]
                diag = [[from_v(P) for _ in range(NP)] for _ in range(SLOTS)]
                diag_sum = [from_v(P) for _ in range(SLOTS)]
                acc = [from_v(2, C) for _ in range(SLOTS)]
                sample = [from_v(CB, P) for _ in range(SLOTS)]
                ob = [from_v(CB, P) for _ in range(SLOTS)]

                grid_landed = sem("grid_landed")
                quads_clear = sem("quads_clear")
                mean1_in = sem("mean1_in")
                mean1_out = sem("mean1_out")
                var1_in = sem("var1_in")
                var1_out = sem("var1_out")
                std1_in = sem("std1_in")
                std1_out = sem("std1_out")
                wide_ready = sem("wide_ready")
                wps_ready = sem("wps_ready")
                bias_out = sem("bias_out")
                bias_ready = sem("bias_ready1")
                x_ready = sem("x_ready")
                flow_psum = sem("flow_psum")
                flow_ready = sem("flow_ready")
                flow_step = sem("flow_step")
                pool_step = sem("pool_step")
                off_ready = sem("off_ready")
                dist_ready = sem("dist_ready")
                tent_ready = sem("tent_ready")
                expo_in = sem("expo_in")
                expo_out = sem("expo_out")
                weights_ready = sem("weights_ready")
                landed = [[sem(f"landed{i}_{k}") for k in range(HEADS)] for i in range(SLOTS)]
                idx_ready = sem("idx_ready")
                idx_seen = sem("idx_seen")
                added = sem("added")
                diag_ready = sem("diag_ready")
                combined = sem("combined")
                sample_ready = sem("sample_ready")
                projected = sem("projected")
                out_ready = sem("out_ready")
                written = [sem(f"written{i}") for i in range(SLOTS)]

                def rounds(eng, step):
                    step(0, True, True)
                    step(1, True, True)
                    with eng.Fori(2, ROUNDS - AHEAD) as j:
                        step(j, True, True)
                    step(ROUNDS - AHEAD, False, True)
                    for j in range(ROUNDS - AHEAD + 1, ROUNDS):
                        step(j, False, False)

                def first(g):
                    return isinstance(g, int) and g == 0

                def flow_bank(g):
                    return (1, 3)[g] if isinstance(g, int) and g < 2 else 7

                def later(t):
                    return not (isinstance(t, int) and t < SLOTS)

                def group_tiles(g):
                    if isinstance(g, int) and g < 2:
                        return ((0, SLOTS), (SLOTS, MOST))[g]
                    return g * SLOTS + SLOTS, SLOTS

 
                with nc.Block(no_gpsimd_drain=True) as block:
                    @block.sync
                    def _(sp):
                        sp.dma_start(bias_row[:, :], bp.rearrange("(a n) -> a n", a=1)).then_inc(grid_landed, 16)
                        sp.dma_start(grid[:, :, :], k_["grid"]).then_inc(grid_landed, 16)
                        sp.wait_ge(zeros_ready, 1)
                        sp.dma_start(table[0:W, 0:C], zeros[:, :]).then_inc(edges_stored, 16)
                        sp.dma_start(table[HW:HW + W, C:2 * C], zeros[:, :]).then_inc(edges_stored, 16)
                        with sp.Fori(0, X_ROUNDS) as j:
                            for u in range(SLOTS):
                                for h in range(2):
                                    sp.wait_ge(stage_ready, j * (2 * SLOTS) + (2 * u + h + 3))
                                    r = j * (SLOTS * CHUNK) + (u * CHUNK + h * 2 * P)
                                    sp.dma_start(table[ds(r + W, 2 * P), 0:C].rearrange("(a p) c -> p a c", p=P),
                                                 stage[u][h][:, :, :]).then_inc(stored[u], 16)
                                    sp.dma_start(table[ds(r, 2 * P), C:2 * C].rearrange("(a p) c -> p a c", p=P),
                                                 stage[u][h][:, :, :]).then_inc(stored[u], 16)

                        with sp.Fori(0, ROUNDS) as j:
                            for u in range(SLOTS):
                                sp.wait_ge(out_ready, j * SLOTS + (u + 1))
                                sp.dma_start(out_c[:, :, ds(j * (SLOTS * P) + u * P, P)], ob[u][:, :, :]).then_inc(written[u], 16)
                        for u in range(SLOTS):
                            sp.wait_ge(written[u], 16 * ROUNDS)

                    @block.gpsimd
                    def _(pool):
                        nc.gpsimd.memset(zeros[:, :], 0.0).then_inc(zeros_ready, 1)
                        with pool.Fori(0, X_ROUNDS) as j:
                            for u in range(SLOTS):
                                pool.wait_ge(y_ready, j * SLOTS + (u + 1))
                                pool.sem_inc(y_seen, 1)
                                nc.gpsimd.tensor_tensor(x1_ring[u][:, :, :], xs[:, :, ds(j * (SLOTS * CHUNK) + u * CHUNK, CHUNK)],
                                                        x1_ring[u][:, :, :], ALU.add).then_inc(x1_ready, 1)

                        G = nc.gpsimd
                        for u in range(SLOTS - 1):
                            for k in range(HEADS):
                                G.memset(quad[u][k], 0.0).then_inc(quads_clear, 1)
                        STEPS = 11

                        def find(g):
                            t0, n = group_tiles(g)
                            r = slice(0, n)
                            done = [0]

                            def chain(ins):
                                done[0] += 1
                                ins.then_inc(pool_step, 1)
                                pool.wait_ge(pool_step, g * STEPS + done[0])
                                pool.sem_inc(idx_seen, 1)

                            def c(x, i):
                                return x[:, r, :].rearrange("p t (k c) -> p (t k) c", c=2)[:, :, i]

                            pool.wait_ge(flow_ready, g + 1)
                            pool.sem_inc(idx_seen, 1)
                            chain(G.tensor_scalar(low[:, r, :], pos[:, r, :], -0.5, 0.0, ALU.add, ALU.max))
                            chain(G.tensor_scalar(base[:, r, :], low[:, r, :], W - 2.0, ROUND, ALU.min, ALU.add))
                            chain(G.tensor_scalar(low[:, r, :], base[:, r, :], 1.0, -ROUND, ALU.mult, ALU.add))
                            if not first(g):
                                pool.wait_ge(dist_ready, g * 2)
                                pool.sem_inc(idx_seen, 1)
                            chain(G.tensor_tensor(off[:, r, :], low[:, r, :], pos[:, r, :], ALU.subtract))
                            pool.sem_inc(off_ready, 1)
                            chain(G.tensor_scalar(base[:, r, :], off[:, r, :], 1.0, 1.0, ALU.mult, ALU.add))
                            chain(G.tensor_tensor(far[:, r, :], off[:, r, :], base[:, r, :], ALU.mult))
                            rows = row[:, r, :].rearrange("p t k -> p (t k)")
                            chain(G.tensor_scalar(rows, c(low, 1), float(W), float(W), ALU.mult, ALU.add))
                            chain(G.tensor_tensor(rows, rows, c(low, 0), ALU.add))
                            chain(G.tensor_scalar(far[:, r, :], far[:, r, :], 2.0, SKIP, ALU.is_gt, ALU.mult))
                            chain(G.tensor_tensor(rows, rows, c(far, 0), ALU.add))
                            chain(G.tensor_tensor(index[:, ds(t0, n), :].rearrange("p t k -> p (t k)"), rows, c(far, 1), ALU.add))
                            assert done[0] == STEPS

                        def gather(t, u):
                            if later(t):
                                pool.wait_ge(combined, t + (1 - SLOTS))
                                pool.sem_inc(idx_seen, 1)
                            G.tensor_copy(idx[u][:, :], index[:, ds(t, 1), :].rearrange("p a k -> p (a k)")).then_inc(idx_ready, 1)
                            pool.wait_ge(idx_ready, t + 1)
                            pool.sem_inc(idx_seen, 1)
                            for k in range(HEADS):
                                G.indirect_dma_start(quad[u][k][:, :], None, table,
                                                     bass.IndirectOffsetOnAxis(ap=idx[u][:, k:k + 1], axis=0),
                                                     bounds_check=HW + W - 1, oob_is_err=False) \
                                    .then_inc(landed[u][k], 16)

                        def step(j, begin, finish):
                            for u in range(SLOTS):
                                gather(j * SLOTS + u, u)
                            if finish:
                                find(j + 1)

                        find(0)
                        for u in range(len(stored)):
                            pool.wait_ge(stored[u], 64 * (NCH // len(stored)))
                        pool.wait_ge(edges_stored, 32)
                        pool.wait_ge(quads_clear, SLOTS * HEADS)
                        rounds(pool, step)

                    @block.vector
                    def _(dve):
                        V = nc.vector

                        def stat(i, u):
                            dve.wait_ge(x1_ready, i + 1)
                            for cb in range(CB):
                                V.bn_stats(stats[:, cb, ds(i, 1), :], x1_ring[u][:, cb, :]).then_inc(stats1_done, 1)

                        def product(i, u):
                            dve.wait_ge(mask_psum, i + 1)
                            if not isinstance(i, int):
                                dve.wait_ge(stats1_done, i * 2 + 2 * (1 - SLOTS))
                                dve.wait_ge(x1_turned, i * 2 + 2 * (1 - SLOTS))
                                dve.wait_ge(x1_kept, i + (1 - SLOTS))
                            V.scalar_tensor_tensor(x1_ring[u][:, :, :], ps[:, 2 * u:2 * u + 2, :], 1.0,
                                                   v[:, :, ds(i * CHUNK, CHUNK)], ALU.add, ALU.mult).then_inc(y_ready, 1)

                        for u in range(SLOTS):
                            product(u, u)
                        with dve.Fori(1, X_ROUNDS) as j:
                            for u in range(SLOTS):
                                stat(j * SLOTS + (u - SLOTS), u)
                                product(j * SLOTS + u, u)
                        for u in range(SLOTS):
                            stat(NCH - SLOTS + u, u)
                        dve.wait_ge(stats1_done, 2 * NCH)
                        for t in range(CB):
                            V.bn_aggr(column("mv")[:, 2 * t:2 * t + 2], stats[:, t, :, :].rearrange("p a b -> p (a b)")) \
                                .then_inc(mean1_in, 1)

                        V = nc.vector
                        V.memset(ones_row[:, :], 1.0).then_inc(wide_ready, 1)
                        dve.wait_ge(mean1_out, 1)
                        dve.wait_ge(mean1_in, CB)
                        mv = column("mv").rearrange("p (t k) -> p k t", k=2)
                        link(dve, V.tensor_copy(column("mg"), ps[:, 0, 0:2]))
                        link(dve, V.tensor_tensor(column("d"), mv[:, 0, :], column("mg"), ALU.subtract))
                        link(dve, V.tensor_tensor(column("mean"), column("d"), column("d"), ALU.mult))
                        V.tensor_tensor(column("e"), column("mean"), mv[:, 1, :], ALU.add).then_inc(var1_in, 1)
                        dve.wait_ge(var1_out, 1)
                        V.tensor_scalar(column("var1"), ps[:, 0, 2:4], EPS, None, ALU.add).then_inc(std1_in, 1)
                        dve.wait_ge(std1_out, 1)
                        link(dve, V.reciprocal(column("rstd1"), column("mean1")))
                        for t in range(CB):
                            V.tensor_scalar(wps[:, t, FLOWS], wp[:, t, FLOWS], column("rstd1")[:, t:t + 1], W / (W - 1.0),
                                            ALU.mult, ALU.mult).then_inc(wps_ready, 1)
                        for cols in (LOGITS, slice(0, C)):
                            for t in range(CB):
                                V.tensor_scalar(wps[:, t, cols], wp[:, t, cols], column("rstd1")[:, t:t + 1], None,
                                                ALU.mult).then_inc(wps_ready, 1)
                        link(dve, V.scalar_tensor_tensor(column("nmr1"), column("mg"), -1.0, column("rstd1"), ALU.mult, ALU.mult))
                        dve.wait_ge(wide_ready, 1)
                        for t in range(CB):
                            V.tensor_scalar(nmr_wide[:, t, :], ones_row[:, :], column("nmr1")[:, t:t + 1], None,
                                            ALU.mult).then_inc(wide_ready, 1)
                        dve.wait_ge(bias_out, 1)
                        link(dve, V.tensor_copy(bias[:, C:NPROJ], ps[:, 2, C:NPROJ]))
                        dve.wait_ge(grid_landed, 32)
                        link(dve, V.scalar_tensor_tensor(grid[:, :, :], bias[:, None, FLOWS].broadcast_to([P, NT, 2 * HEADS]),
                                                         W / (W - 1.0), grid[:, :, :], ALU.mult, ALU.add))
                        STEPS = 14

                        def chain(g, i, ins):
                            ins.then_inc(flow_step, 1)
                            dve.wait_ge(flow_step, g * STEPS + (i + 1))

                        def begin_group(g):
                            t0, n = group_tiles(g)
                            r = slice(0, n)
                            dve.wait_ge(flow_psum, g + 1)
                            both = ps[:, flow_bank(g), 0:n * NFLOW].rearrange("p (t f) -> p t f", f=NFLOW)
                            chain(g, 0, V.tensor_tensor(pos[:, r, :], both[:, :, 0:2 * HEADS], grid[:, ds(t0, n), :], ALU.add))
                            chain(g, 1, V.tensor_tensor(logit[:, r, :], both[:, :, 2 * HEADS:NFLOW],
                                                        bias[:, None, LOGITS].broadcast_to([P, n, HEADS]), ALU.add))
                            dve.sem_inc(flow_ready, 1)
                            chain(g, 2, V.tensor_reduce(top[:, r], logit[:, r, :], AX_X, ALU.max))
                            chain(g, 3, V.tensor_tensor(expo[:, r, :], logit[:, r, :], top[:, r, None].broadcast_to([P, n, HEADS]),
                                                        ALU.subtract))
                            dve.sem_inc(expo_in, 1)

                        def finish_group(g):
                            t0, n = group_tiles(g)
                            r = slice(0, n)
                            dve.wait_ge(expo_out, g + 1)
                            chain(g, 4, V.tensor_reduce(total[:, r], expo[:, r, :], AX_X, ALU.add))
                            chain(g, 5, V.reciprocal(share[:, r], total[:, r]))
                            chain(g, 6, V.tensor_tensor(expo[:, r, :], expo[:, r, :], share[:, r, None].broadcast_to([P, n, HEADS]),
                                                        ALU.mult))
                            dve.wait_ge(tent_ready, g * 2 + 2)
                            side = [tent[i][:, r, :].rearrange("p t (k c) -> p (t k) c", c=2) for i in range(2)]
                            for i in range(2):
                                chain(g, 7 + i, V.tensor_tensor(wy[i][:, r, :].rearrange("p t k -> p (t k)"), side[i][:, :, 1],
                                                                expo[:, r, :].rearrange("p t k -> p (t k)"), ALU.mult))
                            here = weights[:, ds(t0, n), :, :]
                            w4 = here.rearrange("p t k q -> p (t k) q")
                            for i in range(2):
                                for k in range(2):
                                    chain(g, 9 + 2 * i + k, V.tensor_tensor(w4[:, :, 2 * i + k], side[i][:, :, 0],
                                                                            wy[k][:, r, :].rearrange("p t k -> p (t k)"), ALU.mult))
                            chain(g, 13, V.tensor_reduce(wsum[:, ds(t0, n)], here.rearrange("p t k q -> p t (k q)"), AX_X, ALU.add))
                            dve.sem_inc(weights_ready, 1)

                        def add(j, u):
                            t = j * SLOTS + u
                            sums = [ps[:, 6, i * C:(i + 1) * C] for i in range(2)]
                            for n, (k, q) in enumerate(ON_DVE):
                                if n == 0 or ON_DVE[n - 1][0] != k:
                                    dve.wait_ge(landed[u][k], j * 16 + 16)
                                src = quad[u][k][:, q * C:(q + 1) * C]
                                w = weights[:, ds(t, 1), k, q]
                                s = sums[n % 2]
                                o = acc[u][:, n % 2, :] if n >= ND - 2 else s
                                if not (isinstance(t, int) and t == 0 and n < 2):
                                    dve.wait_ge(added, t * ND + (n - 1))
                                if n == ND - 2 and later(t):
                                    dve.wait_ge(combined, t + (1 - SLOTS))
                                if n < 2:
                                    V.tensor_scalar(o, src, w, None, ALU.mult).then_inc(added, 1)
                                else:
                                    V.scalar_tensor_tensor(o, src, w, s, ALU.mult, ALU.add).then_inc(added, 1)

                        def step(j, begin, finish):
                            for u in range(SLOTS):
                                add(j, u)
                            if finish:
                                finish_group(j + 1)
                            if begin:
                                begin_group(j + 2)

                        begin_group(0)
                        for k in range(HEADS):
                            V.memset(quad[SLOTS - 1][k], 0.0).then_inc(quads_clear, 1)
                        dve.wait_ge(bias_out, 2)
                        V.tensor_copy(bias[:, 0:C], ps[:, 4, 0:C]).then_inc(bias_ready, 1)
                        finish_group(0)
                        begin_group(1)
                        rounds(dve, step)

                    @block.scalar
                    def _(act):
                        S = nc.scalar

                        def leave(j, u):
                            i = j * SLOTS + u
                            act.wait_ge(x1_ready, i + 1)
                            S.copy(xs[:, :, ds(i * CHUNK, CHUNK)], x1_ring[u][:, :, :]).then_inc(x1_kept, 1)
                            if isinstance(i, int) and i == NCH - 1:
                                act.wait_ge(std1_in, 1)
                                S.activation(column("mean1"), column("var1"), ACT.Sqrt).then_inc(std1_out, 1)
                            for h in range(2):
                                act.wait_ge(x1_turned, i * 2 + (h + 1))
                                if h == 0 and not (isinstance(j, int) and j == 0):
                                    act.wait_ge(stored[u], j * 64)
                                S.copy(stage[u][h][:, :, :].rearrange("p a c -> p (a c)"), ps[:, 6 + h, :]) \
                                    .then_inc(stage_ready, 1)

                        for u in range(SLOTS):
                            leave(0, u)
                        with act.Fori(1, X_ROUNDS - 1) as j:
                            for u in range(SLOTS):
                                leave(j, u)
                        for u in range(SLOTS):
                            leave(X_ROUNDS - 1, u)

                        S = nc.scalar

                        def tents(g):
                            _, n = group_tiles(g)
                            r = slice(0, n)
                            act.wait_ge(off_ready, g + 1)
                            if not first(g):
                                act.wait_ge(weights_ready, g)
                            S.activation(tent[0][:, r, :], off[:, r, :], ACT.Abs).then_inc(dist_ready, 1)
                            S.activation(tent[1][:, r, :], off[:, r, :], ACT.Abs, bias=column("one")).then_inc(dist_ready, 1)
                            act.wait_ge(dist_ready, g * 2 + 2)
                            for i in range(2):
                                S.activation(tent[i][:, r, :], tent[i][:, r, :], ACT.Relu, scale=-1.0, bias=column("one")) \
                                    .then_inc(tent_ready, 1)
                            act.wait_ge(expo_in, g + 1)
                            S.activation(expo[:, r, :], expo[:, r, :], ACT.Exp).then_inc(expo_out, 1)

                        def copy_group(g):
                            t0, n = group_tiles(g)
                            act.wait_ge(flow_psum, g)
                            S.copy(x_group[:, :, :], xs[:, :, ds(t0 * P, n * P)]).then_inc(x_ready, 1)

                        def diags(t, u):
                            if later(t):
                                act.wait_ge(combined, t + (1 - SLOTS))
                            for n, (k, q) in enumerate(ON_PE):
                                S.activation(diag[u][n][:, :], ident[:, :], ACT.Copy, scale=weights[:, ds(t, 1), k, q]) \
                                    .then_inc(diag_ready, 1)
                            if later(t):
                                act.wait_ge(projected, t + (1 - SLOTS))
                            S.activation(diag_sum[u][:, :], ident[:, :], ACT.Copy, scale=wsum[:, ds(t, 1)]).then_inc(diag_ready, 1)

                        def keep(t, u):
                            act.wait_ge(combined, t + 1)
                            S.copy(sample[u][:, :, :], ps[:, 2 * u:2 * u + 2, 0:P]).then_inc(sample_ready, 1)

                        def result(j, t, u):
                            act.wait_ge(projected, t + 1)
                            if later(t):
                                act.wait_ge(written[u], j * 16)
                            S.copy(ob[u][:, :, :], ps[:, 2 * u:2 * u + 2, P:2 * P]).then_inc(out_ready, 1)

                        def step(j, begin, finish):
                            for u in range(SLOTS):
                                t = j * SLOTS + u
                                if isinstance(t, int) and t == SLOTS - 1:
                                    act.wait_ge(weights_ready, 2)
                                if isinstance(t, int) and t == (ROUNDS - 1) * SLOTS - 1:
                                    act.wait_ge(weights_ready, ROUNDS - AHEAD + 2)
                                if not (isinstance(t, int) and t == NT - 1):
                                    diags(t + 1, (u + 1) % SLOTS)
                                keep(t, u)
                                if not (isinstance(t, int) and t == 0):
                                    result(j + (-1 if u == 0 else 0), t + -1, (u - 1) % SLOTS)
                                if u == 0 and begin:
                                    copy_group(j + 2)
                                if u == 1 and finish:
                                    tents(j + 1)

                        tents(0)
                        act.wait_ge(weights_ready, 1)
                        diags(0, 0)
                        rounds(act, step)
                        result(ROUNDS - 1, NT - 1, SLOTS - 1)

                    @block.tensor
                    def _(pe):
                        T = nc.tensor

                        def spread(t, j, u):
                            for cb in range(CB):
                                m = T.matmul(ps[:, 2 * u + cb, :], pick[:, ds(t, 1), cb * P:(cb + 1) * P].rearrange("p a n -> p (a n)"),
                                             mask[:, ds(j * (SLOTS * CHUNK) + u * CHUNK, CHUNK)], start=True, stop=True)
                            m.then_inc(mask_psum, 1)

                        def turn(i, u):
                            pe.wait_ge(x1_ready, i + 1)
                            for h in range(2):
                                pe.wait_ge(stage_ready, i * 2 + (h + 1))
                                for a in range(2):
                                    for cb in range(CB):
                                        n = (2 * h + a) * P
                                        m = T.transpose(ps[:, 6 + h, a * C + cb * P:a * C + (cb + 1) * P],
                                                        x1_ring[u][:, cb, n:n + P], ident[:, :])
                                m.then_inc(x1_turned, 1)

                        pe.sem_inc(stage_ready, 2)
                        per = X_ROUNDS // 3

                        def third(t, last):
                            for r in range(per):
                                for u in range(SLOTS):
                                    turn(t * (per * SLOTS) + (r * SLOTS + u), u)
                                    if r < per - 1:
                                        spread(t, r + 1, u)
                                    elif not last:
                                        spread(t + 1, 0, u)

                        for u in range(SLOTS):
                            spread(0, 0, u)
                        with pe.Fori(0, 2) as t:
                            third(t, False)
                        third(2, True)

                        T = nc.tensor
                        pe.wait_ge(mean1_in, CB)
                        T.matmul(ps[:, 0, 0:2], group[:, :], column("mv").rearrange("p (t k) -> p k t", k=2)[:, 0, :],
                                 start=True, stop=True).then_inc(mean1_out, 1)
                        pe.wait_ge(var1_in, 1)
                        T.matmul(ps[:, 0, 2:4], group[:, :], column("e"), start=True, stop=True).then_inc(var1_out, 1)

                        def flows(g, source):
                            t0, n = group_tiles(g)
                            if source is x_group:
                                t0 = 0
                            for t in range(n):
                                for kb in range(CB):
                                    m = T.matmul(ps[:, flow_bank(g), t * NFLOW:(t + 1) * NFLOW], source[:, kb, (t0 + t) * P:(t0 + t + 1) * P],
                                                 wps[:, kb, C:NPROJ], start=kb == 0, stop=kb == CB - 1)
                            m.then_inc(flow_psum, 1)

                        pe.wait_ge(wps_ready, 2 * CB)
                        pe.wait_ge(x1_kept, NCH)
                        flows(0, xs)

                        def broadcast_bias(cols, bank):
                            o = ps[:, bank, cols]
                            for kb in range(CB):
                                T.matmul(o, nmr_wide[:, kb, :], wp[:, kb, cols], start=kb == 0, stop=False)
                            T.matmul(o, ones_row[0:1, :], bias_row[:, cols], start=False, stop=True).then_inc(bias_out, 1)

                        pe.wait_ge(wide_ready, 1 + CB)
                        pe.wait_ge(grid_landed, 32)
                        broadcast_bias(slice(C, NPROJ), 2)
                        flows(1, xs)
                        broadcast_bias(slice(0, C), 4)
                        pe.wait_ge(bias_ready, 1)
                        pe.wait_ge(wps_ready, 3 * CB)

                        def combine(j, u):
                            t = j * SLOTS + u
                            if later(t):
                                pe.wait_ge(out_ready, t + (1 - SLOTS))
                            o = [ps[:, 2 * u + cb, 0:P] for cb in range(CB)]
                            for n, (k, q) in enumerate(ON_PE):
                                if n == 0 or ON_PE[n - 1][0] != k:
                                    pe.wait_ge(landed[u][k], j * 16 + 16)
                                pe.wait_ge(diag_ready, t * (NP + 1) + (n + 1))
                                for cb in range(CB):
                                    T.matmul(o[cb], quad[u][k][:, q * C + cb * P:q * C + (cb + 1) * P], diag[u][n][:, :],
                                             start=n == 0, stop=False)
                            for i in range(2):
                                pe.wait_ge(added, t * ND + (ND - 1 + i))
                                for cb in range(CB):
                                    m = T.matmul(o[cb], acc[u][:, i, cb * P:(cb + 1) * P], ident[:, :],
                                                 start=False, stop=i == 1)
                            m.then_inc(combined, 1)

                        def project(t, u):
                            o = [ps[:, 2 * u + cb, P:2 * P] for cb in range(CB)]
                            pe.wait_ge(sample_ready, t + 1)
                            for cb in range(CB):
                                T.matmul(o[cb], ident[:, :], xs[:, cb, ds(t * P, P)], start=True, stop=False)
                            pe.wait_ge(diag_ready, t * (NP + 1) + (NP + 1))
                            for cb in range(CB):
                                T.matmul(o[cb], bias[:, cb * P:(cb + 1) * P], diag_sum[u][:, :], start=False, stop=False)
                            for cb in range(CB):
                                for kb in range(CB):
                                    m = T.matmul(o[cb], wps[:, kb, cb * P:(cb + 1) * P], sample[u][:, kb, :],
                                                 start=False, stop=kb == CB - 1)
                            m.then_inc(projected, 1)

                        def step(j, begin, finish):
                            for u in range(SLOTS):
                                t = j * SLOTS + u
                                combine(j, u)
                                if not (isinstance(t, int) and t == 0):
                                    project(t + -1, (u - 1) % SLOTS)
                                if u == 1 and begin:
                                    pe.wait_ge(x_ready, j + 1)
                                    pe.wait_ge(flow_ready, j + 2)
                                    flows(j + 2, x_group)

                        rounds(pe, step)
                        project(NT - 1, SLOTS - 1)


def kernel(**inputs):
    import concourse.bacc as _bacc
    from concourse import mybir as _mybir
    from concourse.bass_utils import run_bass_kernel_spmd as _run

    g = {n: np.asarray(a) for n, a in inputs.items()}
    laid = {
        "x": g["x"],
        "WqT": g["L0_conv_Wq"].T, "bq": g["L0_conv_bq"],
        "WvT": g["L0_conv_Wv"].T, "bv": g["L0_conv_bv"].reshape(CB, P).T,
        "WpT": np.concatenate([g["L1_conv_Wc"], g["L1_conv_Woff"].reshape(2 * HEADS, C), g["L1_conv_Wwt"]]).T,
        "bp": np.concatenate([g["L1_conv_bc"], g["L1_conv_boff"].reshape(-1), g["L1_conv_bwt"]]),
    }
    nc = _bacc.Bacc("TRN2", target_bir_lowering=False, num_devices=1)
    arrays, args = {}, []
    for name, a in laid.items():
        a = np.ascontiguousarray(a)
        arrays[f"in_{name}_dram"] = a
        args.append(nc.dram_tensor(f"in_{name}_dram", a.shape, _mybir.dt.from_np(a.dtype), kind="ExternalInput").ap())
    args.append(nc.dram_tensor("out_0_dram", (1, C, H, W), _mybir.dt.from_np(np.dtype("float32")),
                               kind="ExternalOutput").ap())
    build(nc, *args)
    r = _run(nc, [arrays], core_ids=[0])
    return r.results[0]["out_0_dram"]
```

```python
from contextlib import ExitStack

import numpy as np

import concourse.bass as bass
from concourse import mybir

F32 = mybir.dt.float32
BF16 = mybir.dt.bfloat16
F32R = mybir.dt.float32r
U32 = mybir.dt.uint32
ALU = mybir.AluOpType
ACT = mybir.ActivationFunctionType
AX_X = mybir.AxisListType.X
ds = bass.ds

P = 128
C, H, W = 256, 96, 96
HW = H * W
CB = C // P
NT = HW // P
GROUPS = 32
PER_GROUP = C // GROUPS
EPS = 1e-5
HEADS = 4
NFLOW = 3 * HEADS
NPROJ = C + NFLOW
LEVELS = 255.0
ROUND = 1.5 * 2.0 ** 23
CHUNK = 512
NCH = HW // CHUNK
QCH = 768
NQ = HW // QCH
QT = QCH // P
CUT = int(0.05 * (H // 2))
SPLITS = 3
ROWS = 32
STACK = SPLITS * ROWS
BLOCKS = 8
THIRD = HW // 3
THIRD_TILES = THIRD // P


def bf16_bits(a):
    u = np.ascontiguousarray(a, np.float32).view(np.uint32).astype(np.uint64)
    return ((u + 0x7FFF + ((u >> 16) & 1)) >> 16).astype(np.uint16)


def from_bits(b):
    return (b.astype(np.uint32) << 16).view(np.float32)


def split3(a):
    out = []
    for _ in range(SPLITS):
        out.append(bf16_bits(a.astype(np.float32)))
        a = a - from_bits(out[-1])
    return out


def high_bits(a):
    u = a.astype(np.float32).view(np.uint32).astype(np.uint64)
    return (((u + 0x7FF + ((u >> 12) & 1)) >> 12) << 12).astype(np.uint32).view(np.float32)


def shape_constants():
    freqs = range(-CUT, CUT)
    alone = [(a, b) for a in freqs for b in freqs if -CUT in (a, b)]
    pairs = [(a, b) for a in range(CUT) for b in range(-CUT + 1, CUT) if a > 0 or b > 0]
    yy, xx = np.divmod(np.arange(HW), W)
    n_a, n_p = len(alone), len(pairs)

    def phase(ab):
        return 2 * np.pi * ((ab[0] * yy + ab[1] * xx) % W) / W

    fns = [np.cos(phase(f)) for f in alone] + [np.sin(phase(f)) for f in alone]
    fns += [np.cos(phase(f)) for f in pairs] + [np.sin(phase(f)) for f in pairs] + [np.ones(HW)]
    n = len(fns)
    assert n <= ROWS
    basis = np.zeros((ROWS, HW))
    basis[:n] = fns
    b1, b2, b3 = split3(basis)
    ana = np.zeros((P, NT, P), np.uint16)
    ana[:, :, :STACK] = np.stack([b1, b2, b3], 0).reshape(STACK, NT, P).transpose(2, 1, 0)
    high = high_bits(basis)
    syn = np.concatenate([high, (basis - high).astype(np.float32), high])
    sel = np.zeros((STACK, 2, STACK), np.float32)
    for s in range(SPLITS):
        for to in range(3):
            for j in range(n):
                sel[s * ROWS + j, 0, to * ROWS + j] = 2.0 if 2 * n_a <= j < 2 * n_a + 2 * n_p else 1.0
            for j in range(n_a):
                sel[s * ROWS + j, 1, to * ROWS + n_a + j] = 1.0
                sel[s * ROWS + n_a + j, 1, to * ROWS + j] = -1.0
    group = np.zeros((P, P), np.float32)
    for c in range(P):
        group[c, c // PER_GROUP * PER_GROUP:(c // PER_GROUP + 1) * PER_GROUP] = 1.0 / PER_GROUP
    pick = np.zeros((P, 3, C), np.float32)
    for s in range(SPLITS):
        for t in range(3):
            for c in range(C):
                pick[s * BLOCKS + 3 * (3 * c + t) % BLOCKS, t, c] = 1.0
    grid = np.zeros((P, NT, HEADS, 2), np.float32)
    gx, gy = xx.reshape(NT, P).T, yy.reshape(NT, P).T
    grid[..., 0] = (gx * (W / (W - 1.0)) - 0.5)[:, :, None]
    grid[..., 1] = (gy * (H / (H - 1.0)) - 0.5)[:, :, None]
    return {
        "ana": ana, "syn": syn, "sel": sel, "group": group,
        "pick": bf16_bits(pick), "grid": grid.reshape(P, NT, 2 * HEADS),
        "ident": np.eye(P, dtype=np.float32), "identb": bf16_bits(np.eye(P)),
    }


def build(nc, x, WqT, bq, WvT, bv, WpT, bp, out):
    const = shape_constants()
    k_ = {n: nc.inline_tensor(a, name="const_" + n).ap() for n, a in const.items()}
    x_c = x.rearrange("a (t p) h w -> t p (a h w)", p=P)
    out_c = out.rearrange("a (t p) h w -> p (a t) (h w)", p=P)
    table = nc.dram_tensor("table", (HW + W, 2 * C), F32, kind="Internal").ap()

    with ExitStack() as ctx:
        def sb(name, shape, dt=F32):
            return ctx.enter_context(nc.sbuf_tensor(name, shape, dt))

        def sem(name):
            return ctx.enter_context(nc.semaphore(name))

        ps = ctx.enter_context(nc.psum_tensor("ps", [P, 8, CHUNK], F32))
        xs = sb("xs", [P, CB, HW])
        ident = sb("ident", [P, P])
        identb = sb("identb", [P, P], BF16)
        group = sb("group", [P, P])
        small = sb("small", [P, 256])
        wp = sb("wp", [P, CB, NPROJ])
        link_sem = sem("link_sem")
        linked = [0]

        def link(eng, ins):
            linked[0] += 1
            ins.then_inc(link_sem, 1)
            eng.wait_ge(link_sem, linked[0])

        col = {}

        def column(name, n=1):
            if name not in col:
                col[name] = (sum(w for _, w in col.values()), n)
            a, w = col[name]
            return small[:, a:a + w]

        for nme in ("mean", "var", "rstd", "nmr", "mg", "mn", "sc", "bvp", "mean1", "var1", "rstd1", "nmr1"):
            column(nme, CB)
        for nme in ("d", "e", "std", "mx_", "ptp", "rp", "less_mn"):
            column(nme, CB)
        column("mv", 2 * CB)
        column("one", 1)
        column("eye3", 3)

        with ExitStack() as c0:
            def sb0(name, shape, dt=F32):
                return c0.enter_context(nc.sbuf_tensor(name, shape, dt))

            v = sb0("v", [P, CB, HW])
            wq = sb0("wq", [P, 2, CB, C], F32R)
            wvs = sb0("wvs", [P, CB, C])
            bq3 = sb0("bq3", [3, C])
            bqs = sb0("bqs", [P, C], BF16)
            ones = sb0("ones", [P, P], BF16)
            pick = sb0("pick", [P, 3, C], BF16)
            mask = sb0("mask", [P, THIRD], BF16)

            with ExitStack() as c1:
                def sb1(name, shape, dt=F32):
                    return c1.enter_context(nc.sbuf_tensor(name, shape, dt))

                ana = sb1("ana", [P, NT, P], BF16)
                wv = sb1("wv", [P, CB, C])
                stats = sb1("stats", [P, CB, NCH, 6])
                mxs = sb1("mxs", [P, CB, NQ])
                mns = sb1("mns", [P, CB, NQ])
                a_ring = [sb1(f"a_ring{i}", [P, QCH]) for i in range(2)]
                t_ring = [sb1(f"t_ring{i}", [P, QCH]) for i in range(2)]
                u_ring = [sb1(f"u_ring{i}", [P, QCH]) for i in range(2)]
                wq_in = t_ring[0][:, 0:CB * C].rearrange("p (t n) -> p t n", t=CB)
                bq_rest, bq_sum, bq_row = (t_ring[1][0:3, i * C:(i + 1) * C] for i in range(3))
                bqp = [u_ring[1][0:3, i * P:(i + 1) * P].bitcast(BF16) for i in range(3)]
                qt_ring = [sb1(f"qt_ring{i}", [P, QT, P], BF16) for i in range(2)]

                PIECES = 6
                x_landed = [[sem(f"x_landed{t}{i}") for i in range(PIECES)] for t in range(CB)]
                w_landed = sem("w_landed")
                ana_landed = sem("ana_landed")
                c_landed = sem("c_landed")
                bq_landed = sem("bq_landed")
                stats_done = sem("stats_done")
                mean_in = sem("mean_in")
                mean_out = sem("mean_out")
                var_in = sem("var_in")
                var_out = sem("var_out")
                std_in = sem("std_in")
                std_out = sem("std_out")
                norm_ready = sem("norm_ready")
                wvs_ready = sem("wvs_ready")
                bvp_out = sem("bvp_out")
                bvp_ready = sem("bvp_ready")
                abs_ready = sem("abs_ready")
                abs_free = sem("abs_free")
                minmax_done = sem("minmax_done")
                scale_ready = sem("scale_ready")
                a_seen = sem("a_seen")
                bias_step = sem("bias_step")
                u_ready = sem("u_ready")
                transposed = sem("transposed")
                qt_ready = sem("qt_ready")
                qt_free = sem("qt_free")
                v_psum = sem("v_psum")
                v_free = sem("v_free")
                cst_ready = sem("cst_ready")

                def q_psum(slot):
                    return ps[:, 2 * slot:2 * slot + 2, :].rearrange("p b n -> p (b n)")[:, 0:QCH]

                PRE_CHUNKS = NQ
                PRE = CB * PRE_CHUNKS
                FOURS = NQ // 4
                assert NCH - PRE_CHUNKS == CB * FOURS

                with nc.Block(no_gpsimd_drain=True) as block:
                    @block.sync
                    def _(sp):
                        n = HW // PIECES
                        for t in range(CB):
                            for i in range(PIECES):
                                sp.dma_start(xs[:, t, i * n:(i + 1) * n], x_c[t][:, i * n:(i + 1) * n]) \
                                    .then_inc(x_landed[t][i], 16)
                                if t == 0 and i == 0:
                                    sp.dma_start(group[:, :], k_["group"]).then_inc(c_landed, 16)
                                    sp.dma_start(ident[:, :], k_["ident"]).then_inc(c_landed, 16)
                        sp.dma_start(wv[:, :, :], WvT.rearrange("(t p) n -> p t n", p=P)).then_inc(w_landed, 16)
                        sp.dma_start(column("bvp"), bv).then_inc(w_landed, 16)
                        sp.dma_start(ana[:, :, :], k_["ana"].bitcast(BF16)).then_inc(ana_landed, 16)
                        sp.dma_start(identb[:, :], k_["identb"].bitcast(BF16)).then_inc(bq_landed, 16)
                        sp.dma_start(wq_in, WqT.rearrange("(t p) n -> p t n", p=P)).then_inc(bq_landed, 16)
                        sp.dma_start(wp[:, :, :], WpT.rearrange("(t p) n -> p t n", p=P)).then_inc(bq_landed, 16)
                        sp.dma_start(pick[:, :, :], k_["pick"].bitcast(BF16)).then_inc(bq_landed, 16)
                        for r in range(3):
                            sp.dma_start(bq3[r:r + 1, :], bq.rearrange("(a n) -> a n", a=1)).then_inc(bq_landed, 16)
                        sp.dma_start(column("eye3")[0:3, :], k_["ident"][0:3, 0:3]).then_inc(bq_landed, 16)
                        sp.wait_ge(bq_landed, 16 * 8)
                        sp.wait_ge(ana_landed, 16)

                    @block.vector
                    def _(dve):
                        V = nc.vector
                        V.memset(column("one"), 1.0).then_inc(cst_ready, 1)
                        V.memset(ones[:, :], 1.0).then_inc(cst_ready, 1)
                        V.memset(bqs[:, :], 0.0).then_inc(cst_ready, 1)
                        V.memset(mask[:, :], 0.0).then_inc(cst_ready, 1)
                        per = NCH // PIECES
                        for t in range(CB):
                            for i in range(PIECES):
                                dve.wait_ge(x_landed[t][i], 16)
                                for j in range(i * per, (i + 1) * per):
                                    V.bn_stats(stats[:, t, j, :], xs[:, t, j * CHUNK:(j + 1) * CHUNK]).then_inc(stats_done, 1)
                        dve.wait_ge(stats_done, NCH * CB)
                        for t in range(CB):
                            V.bn_aggr(column("mv")[:, 2 * t:2 * t + 2],
                                      stats[:, t, :, :].rearrange("p a b -> p (a b)")).then_inc(mean_in, 1)
                        dve.wait_ge(mean_in, CB)
                        dve.wait_ge(mean_out, 1)
                        mv = column("mv").rearrange("p (t k) -> p k t", k=2)
                        link(dve, V.tensor_copy(column("mg"), ps[:, 7, 0:2]))
                        link(dve, V.tensor_tensor(column("d"), mv[:, 0, :], column("mg"), ALU.subtract))
                        link(dve, V.tensor_tensor(column("mean"), column("d"), column("d"), ALU.mult))
                        V.tensor_tensor(column("e"), column("mean"), mv[:, 1, :], ALU.add).then_inc(var_in, 1)
                        dve.wait_ge(var_out, 1)
                        V.tensor_scalar(column("var"), ps[:, 7, 2:4], EPS, None, ALU.add).then_inc(std_in, 1)
                        dve.wait_ge(std_out, 1)
                        link(dve, V.reciprocal(column("rstd"), column("std")))
                        V.scalar_tensor_tensor(column("nmr"), column("mg"), -1.0, column("rstd"), ALU.mult, ALU.mult) \
                            .then_inc(norm_ready, 1)
                        dve.wait_ge(w_landed, 32)
                        for t in range(CB):
                            V.tensor_scalar(wvs[:, t, :], wv[:, t, :], column("rstd")[:, t:t + 1], None,
                                            ALU.mult).then_inc(wvs_ready, 1)
                        dve.wait_ge(norm_ready, 1)
                        dve.wait_ge(bvp_out, 1)
                        V.tensor_tensor(column("bvp"), column("bvp"), ps[:, 7, 4:6], ALU.add).then_inc(bvp_ready, 1)
                        for t in range(CB):
                            with dve.Fori(0, NQ // 2) as j:
                                for u in range(2):
                                    dve.wait_ge(abs_ready, j * 2 + (t * NQ + u + 1))
                                    V.tensor_reduce(mxs[:, t, ds(j * 2 + u, 1)], a_ring[u][:, :], AX_X, ALU.max) \
                                        .then_inc(minmax_done, 1)
                                    V.tensor_reduce(mns[:, t, ds(j * 2 + u, 1)], a_ring[u][:, :], AX_X, ALU.min) \
                                        .then_inc(abs_free, 1)
                            if t == 0:
                                dve.wait_ge(bq_landed, 16 * 8)
                                link(dve, V.tensor_copy(wq[:, 0, :, :], wq_in))
                                link(dve, V.tensor_tensor(wq[:, 1, :, :], wq_in, wq[:, 0, :, :].bitcast(F32), ALU.subtract))
                            dve.wait_ge(minmax_done, NQ * (t + 1))
                            dve.wait_ge(abs_free, NQ * (t + 1))
                            one = slice(t, t + 1)
                            link(dve, V.tensor_reduce(column("mx_")[:, one], mxs[:, t, :], AX_X, ALU.max))
                            link(dve, V.tensor_reduce(column("mn")[:, one], mns[:, t, :], AX_X, ALU.min))
                            link(dve, V.tensor_tensor(column("ptp")[:, one], column("mx_")[:, one], column("mn")[:, one],
                                                      ALU.subtract))
                            link(dve, V.reciprocal(column("rp")[:, one], column("ptp")[:, one]))
                            link(dve, V.tensor_scalar(column("sc")[:, one], column("rp")[:, one],
                                                      LEVELS * (1 + 2.0 ** -22), None, ALU.mult))
                            link(dve, V.tensor_scalar(column("less_mn")[:, one], column("mn")[:, one], -1.0, None, ALU.mult))
                            dve.sem_inc(scale_ready, 1)
                        dve.sem_inc(u_ready, 2)

                        def rounded(n, u):
                            dve.wait_ge(abs_free, n + (CB * NQ + 1))
                            dve.wait_ge(transposed, n + 1)
                            V.tensor_scalar(u_ring[u][:, :], t_ring[u][:, :], -0.5 + 2.0 ** -16, ROUND,
                                            ALU.add, ALU.add).then_inc(u_ready, 1)

                        def q_out(n, u):
                            dve.wait_ge(transposed, n + 3)
                            dve.wait_ge(qt_free, n + 1)
                            V.tensor_scalar(qt_ring[u][:, :, :].rearrange("p a b -> p (a b)"), q_psum(u), -ROUND, None,
                                            ALU.add).then_inc(qt_ready, 1)

                        rounded(0, 0)
                        rounded(1, 1)
                        with dve.Fori(1, CB * NQ // 2) as j:
                            for u in range(2):
                                q_out(j * 2 + (u - 2), u)
                                rounded(j * 2 + u, u)
                        for u in range(2):
                            q_out(CB * NQ - 2 + u, u)

                    @block.gpsimd
                    def _(pool):
                        G = nc.gpsimd
                        done = [0]

                        def chain(ins):
                            done[0] += 1
                            ins.then_inc(bias_step, 1)
                            pool.wait_ge(bias_step, done[0])

                        pool.wait_ge(bq_landed, 16 * 8)
                        pool.wait_ge(cst_ready, 4)
                        chain(G.tensor_copy(bqp[0], bq3[:, :]))
                        chain(G.tensor_tensor(bq_rest, bq3[:, :], bqp[0], ALU.subtract))
                        chain(G.tensor_copy(bqp[1], bq_rest))
                        chain(G.tensor_tensor(bq_rest, bq_rest, bqp[1], ALU.subtract))
                        chain(G.tensor_copy(bqp[2], bq_rest))
                        for i in range(3):
                            o = bq_row if i else bq_sum
                            chain(G.tensor_scalar(o, bqp[i], column("eye3")[0:3, i:i + 1], 0.0, ALU.mult, ALU.add))
                            if i:
                                chain(G.tensor_tensor(bq_sum if i == 1 else bqs[0:3, :], bq_sum, bq_row, ALU.add))
                        for t in range(CB):
                            pool.wait_ge(scale_ready, t + 1)
                            with pool.Fori(0, NQ // 2) as j:
                                for u in range(2):
                                    n = j * 2 + (t * NQ + u)
                                    pool.wait_ge(abs_ready, n + (CB * NQ + 1))
                                    pool.wait_ge(u_ready, n + 1)
                                    pool.sem_inc(a_seen, 1)
                                    nc.gpsimd.tensor_scalar(t_ring[u][:, :], a_ring[u][:, :], column("less_mn")[:, t:t + 1],
                                                            column("sc")[:, t:t + 1], ALU.add, ALU.mult).then_inc(abs_free, 1)

                    @block.scalar
                    def _(act):
                        S = nc.scalar
                        act.wait_ge(std_in, 1)
                        S.activation(column("std"), column("var"), ACT.Sqrt).then_inc(std_out, 1)

                        def absolute(t, j, u):
                            S.activation(a_ring[u][:, :], xs[:, t, ds(j * (2 * QCH) + u * QCH, QCH)], ACT.Abs,
                                         scale=column("rstd")[:, t:t + 1], bias=column("nmr")[:, t:t + 1]).then_inc(abs_ready, 1)

                        def v_out(n, chunk, ob, slot):
                            act.wait_ge(v_psum, n + 1)
                            S.activation(v[:, ob, ds(chunk * CHUNK, CHUNK)], ps[:, 4 + slot, :], ACT.Identity,
                                         bias=column("bvp")[:, ob:ob + 1]).then_inc(v_free, 1)

                        half = NQ // 2
                        act.wait_ge(norm_ready, 1)
                        absolute(0, 0, 0)
                        absolute(0, 0, 1)
                        act.wait_ge(bvp_ready, 1)
                        for t in range(CB):
                            with act.Fori(0, half - 1) as j:
                                for u in range(2):
                                    n = j * 2 + (t * NQ + u)
                                    act.wait_ge(abs_free, n + 1)
                                    absolute(t, j + 1, u)
                                    v_out(n, j + t * half, u, u)
                            for u in range(2):
                                n = (t + 1) * NQ - 2 + u
                                act.wait_ge(abs_free, n + 1)
                                absolute((t + 1) % CB, 0, u)
                                v_out(n, n // 2, u, u)
                        def two_steps(t, pair):
                            nxt = (t, pair + 1) if pair + 1 < half else (t + 1, 0)
                            for u in range(2):
                                act.wait_ge(abs_free, t * NQ + 2 * pair + u + CB * NQ + 1)
                                absolute(nxt[0], nxt[1], u)

                        for i in range(CB * FOURS):
                            t, j = i // FOURS, i % FOURS
                            two_steps(t, 2 * j)
                            if i > 0:
                                v_out(PRE + i - 1, PRE_CHUNKS + i - 1, 0, 0)
                            if i < CB * FOURS - 1:
                                two_steps(t, 2 * j + 1)
                        v_out(PRE + CB * FOURS - 1, NCH - 1, 0, 0)

                    @block.tensor
                    def _(pe):
                        T = nc.tensor
                        pe.wait_ge(c_landed, 32)
                        pe.wait_ge(mean_in, CB)
                        T.matmul(ps[:, 7, 0:2], group[:, :], column("mv").rearrange("p (t k) -> p k t", k=2)[:, 0, :],
                                 start=True, stop=True).then_inc(mean_out, 1)
                        pe.wait_ge(var_in, 1)
                        T.matmul(ps[:, 7, 2:4], group[:, :], column("e"), start=True, stop=True).then_inc(var_out, 1)
                        pe.wait_ge(norm_ready, 1)
                        pe.wait_ge(w_landed, 32)
                        for ob in range(CB):
                            for kb in range(CB):
                                m = T.matmul(ps[:, 7, 4 + ob:5 + ob], wv[:, kb, ob * P:(ob + 1) * P],
                                             column("nmr")[:, kb:kb + 1], start=kb == 0, stop=kb == CB - 1)
                        m.then_inc(bvp_out, 1)
                        pe.wait_ge(wvs_ready, CB)
                        pe.sem_inc(v_free, 2)
                        pe.sem_inc(transposed, 2)
                        pe.sem_inc(qt_free, 2)

                        def v_unit(n, chunk, ob):
                            pe.wait_ge(v_free, n + 1)
                            for kb in range(CB):
                                m = T.matmul(ps[:, 4 + ob, :], wvs[:, kb, ob * P:(ob + 1) * P],
                                             xs[:, kb, ds(chunk * CHUNK, CHUNK)], start=kb == 0, stop=kb == CB - 1)
                            m.then_inc(v_psum, 1)

                        with pe.Fori(0, PRE // 2) as j:
                            for u in range(2):
                                v_unit(j * 2 + u, j, u)
                        pe.wait_ge(ana_landed, 16)

                        def turn(n, u):
                            pe.wait_ge(u_ready, n + 3)
                            for i in range(QT):
                                m = T.transpose(q_psum(u)[:, i * P:(i + 1) * P], u_ring[u][:, i * P:(i + 1) * P], ident[:, :])
                            m.then_inc(transposed, 1)

                        def v_quarter(n, chunk, i):
                            if i == 0:
                                pe.wait_ge(v_free, n + 2)
                            h, kb = i // 2, i % 2
                            m = T.matmul(ps[:, 4, h * (CHUNK // 2):(h + 1) * (CHUNK // 2)], wvs[:, kb, 0:P],
                                         xs[:, kb, ds(chunk * CHUNK + h * (CHUNK // 2), CHUNK // 2)], start=kb == 0, stop=kb == 1)
                            if i == 3:
                                m.then_inc(v_psum, 1)

                        def four_steps(t, j, last=False):
                            for i in range(4):
                                u = i % 2
                                n = j * 4 + (t * NQ + i)
                                if not (last and i == 3):
                                    turn(n + 1, 1 - u)
                                v_quarter(j + (PRE + t * FOURS), j + (PRE_CHUNKS + t * FOURS), i)
                                pe.wait_ge(qt_ready, n + 1)
                                for k in range(QT):
                                    m = T.matmul(coef_psum(t), ana[:, ds(j * (4 * QT) + (i * QT + k), 1), :]
                                                 .rearrange("p a n -> p (a n)"),
                                                 qt_ring[u][:, k, :], start=False, stop=False, skip_group_check=True)
                                m.then_inc(qt_free, 1)

                        def coef_psum(t):
                            return ps[:, 6, t * P:(t + 1) * P]

                        def nothing(t, start):
                            T.matmul(coef_psum(t), mask[:, 0:P], mask[:, 0:P], start=start, stop=not start, skip_group_check=True)

                        pe.wait_ge(cst_ready, 4)
                        turn(0, 0)
                        for t in range(CB):
                            nothing(t, True)
                            with pe.Fori(0, FOURS - (t == CB - 1)) as j:
                                four_steps(t, j)
                            if t == CB - 1:
                                four_steps(t, FOURS - 1, last=True)
                            nothing(t, False)

            with ExitStack() as c2:
                def sb2(name, shape, dt=F32):
                    return c2.enter_context(nc.sbuf_tensor(name, shape, dt))

                sel = sb2("sel", [STACK, 2, STACK])
                stack = sb2("stack", [STACK, 2, C], F32R)
                syn_ring = [sb2(f"syn_ring{i}", [STACK, CHUNK], F32R) for i in range(2)]
                sq_ring = [sb2(f"sq_ring{i}", [P, 2, CHUNK]) for i in range(2)]
                s2_ring = [[sb2(f"s2_ring{i}{c}", [P, CHUNK]) for c in range(CB)] for i in range(2)]
                high = [sb2(f"high{i}", [P, CB, CHUNK], F32R) for i in range(2)]
                lows = [sb2(f"lows{i}", [P, CB, CHUNK], F32R) for i in range(2)]
                coef = sq_ring[1][0:STACK, 1, 0:C]
                row_max = sb2("row_max", [P, NT, BLOCKS])
                m_f, m_r = (sq_ring[0][:, i, 0:THIRD_TILES * BLOCKS].rearrange("p (t b) -> p t b", b=BLOCKS) for i in range(2))
                m_p = sq_ring[1][:, 0, 0:THIRD_TILES * SPLITS * BLOCKS // 2].bitcast(BF16) \
                    .rearrange("p (t s b) -> p t s b", s=SPLITS, b=BLOCKS)

                TPC = CHUNK // P
                PASSES = ((0, 0), (0, 1), (1, 0))
                sel_landed = sem("sel_landed")
                syn_landed = [sem(f"syn_landed{i}") for i in range(2)]
                ri_ready = sem("ri_ready")
                sq_ready = sem("sq_ready")
                s2_ready = sem("s2_ready")
                root_ready = sem("root_ready")
                high_ready = sem("high_ready")
                high_seen = sem("high_seen")
                low_ready = [sem(f"low_ready{i}") for i in range(CB)]
                q_ready = sem("q_ready")
                q_free = sem("q_free")
                coef_ready = sem("coef_ready")
                late_v_psum = sem("late_v_psum")
                late_v_out = sem("late_v_out")
                summed = sem("summed")
                stack_ready = sem("stack_ready")
                syn_seen = sem("syn_seen")
                m_ready = sem("m_ready")
                m_turned = sem("m_turned")
                EARLY_V = [(12, 5), (13, 7), (14, 5), (15, 7)]
                LATE_V = [(16, 3), (17, 4)]
                MASK_BANKS = THIRD // (2 * CHUNK)

                def mask_out(eng, copy, bank):
                    eng.wait_ge(m_turned, bank + 1)
                    copy(mask[0:SPLITS * BLOCKS, bank * 2 * CHUNK:(bank + 1) * 2 * CHUNK],
                         ps[0:SPLITS * BLOCKS, bank, :].bitcast(BF16))

                def v_out(act, i, chunk, bank):
                    act.wait_ge(late_v_psum, i + 1)
                    nc.scalar.activation(v[:, 1, chunk * CHUNK:(chunk + 1) * CHUNK], ps[:, bank, :], ACT.Identity,
                                         bias=column("bvp")[:, 1:2]).then_inc(late_v_out, 1)

                with nc.Block(no_gpsimd_drain=True) as block:
                    @block.sync
                    def _(sp):
                        sp.dma_start(sel[:, :, :], k_["sel"]).then_inc(sel_landed, 16)

                    @block.vector
                    def _(dve):
                        V = nc.vector
                        V.tensor_copy(coef, ps[0:STACK, 6, 0:CB * P]).then_inc(coef_ready, 1)
                        dve.wait_ge(summed, 1)
                        sums = ps[0:STACK, 4, :].rearrange("p (a n) -> p a n", a=2)
                        link(dve, V.tensor_copy(stack[:, :, :], sums))
                        r = slice(2 * ROWS, STACK)
                        V.tensor_tensor(stack[r, :, :], sums[r, :, :], stack[r, :, :].bitcast(F32), ALU.subtract) \
                            .then_inc(stack_ready, 1)
                        dve.sem_inc(q_free, 2)

                        def add(j, u, cb):
                            n = j * 4 + (2 * u + cb)
                            dve.wait_ge(sq_ready, n + 3)
                            dve.wait_ge(low_ready[cb], j * 2 + (u + 1))
                            V.tensor_tensor(s2_ring[u][cb][:, :], sq_ring[cb][:, 0, :], sq_ring[cb][:, 1, :],
                                            ALU.add).then_inc(s2_ready, 1)

                        def split(j, u, cb):
                            dve.wait_ge(root_ready, j * 4 + (2 * u + cb + 1))
                            if cb == 0:
                                dve.wait_ge(q_ready, j * 2 + (u + 1))
                            V.tensor_copy(high[u][:, cb, :], s2_ring[u][cb][:, :]).then_inc(high_ready, 1)
                            if cb == 1:
                                dve.wait_ge(high_ready, j * 4 + (2 * u + 2))
                                V.tensor_tensor(lows[u][:, cb, :], s2_ring[u][cb][:, :], high[u][:, cb, :].bitcast(F32),
                                                ALU.subtract).then_inc(low_ready[cb], 1)

                        def maxima(j, u):
                            dve.wait_ge(q_ready, j * 2 + (u + 3))
                            V.tensor_reduce(row_max[:, ds(j * (2 * TPC) + u * TPC, TPC), :],
                                            ps[:, 4 + 2 * u:6 + 2 * u, :].rearrange(
                                                "p b (t g r) -> p (b t) r g", t=2, r=BLOCKS), AX_X, ALU.max).then_inc(q_free, 1)

                        last = NCH // 2 - 1

                        def step(j, u, next_chunk=True, last_maxima=True):
                            for cb in range(CB):
                                if next_chunk:
                                    add(j if u == 0 else j + 1, 1 - u, cb)
                                split(j, u, cb)
                            if last_maxima:
                                maxima(j if u == 1 else j + -1, 1 - u)

                        for cb in range(CB):
                            add(0, 0, cb)
                        step(0, 0, last_maxima=False)
                        step(0, 1)
                        with dve.Fori(1, last) as j:
                            step(j, 0)
                            step(j, 1)
                        step(last, 0)
                        step(last, 1, next_chunk=False)
                        maxima(last, 1)
                        dve.wait_ge(q_free, NCH + 2)
                        third = [row_max[:, t * THIRD_TILES:(t + 1) * THIRD_TILES, :] for t in range(3)]
                        for t in range(1, 3):
                            so_far = third[0] if t == 1 else m_f[:, :, :]
                            cut = 3 * t % BLOCKS
                            V.tensor_tensor(m_f[:, :, cut:BLOCKS], so_far[:, :, cut:BLOCKS], third[t][:, :, 0:BLOCKS - cut],
                                            ALU.max)
                            link(dve, V.tensor_tensor(m_f[:, :, 0:cut], so_far[:, :, 0:cut], third[t][:, :, BLOCKS - cut:BLOCKS],
                                                      ALU.max))
                        link(dve, V.tensor_copy(m_p[:, :, 0, :], m_f[:, :, :]))
                        link(dve, V.tensor_tensor(m_r[:, :, :], m_f[:, :, :], m_p[:, :, 0, :], ALU.subtract))
                        link(dve, V.tensor_copy(m_p[:, :, 1, :], m_r[:, :, :]))
                        link(dve, V.tensor_tensor(m_f[:, :, :], m_r[:, :, :], m_p[:, :, 1, :], ALU.subtract))
                        V.tensor_copy(m_p[:, :, 2, :], m_f[:, :, :]).then_inc(m_ready, 1)
                        mask_out(dve, V.tensor_copy, 0)
                        mask_out(dve, V.tensor_copy, 2)

                    @block.scalar
                    def _(act):
                        S = nc.scalar
                        act.sem_inc(sq_ready, 2)
                        for cb in range(CB):
                            act.sem_inc(low_ready[cb], 2)
                        act.sem_inc(s2_ready, 2)

                        def square(j, u, cb):
                            n = j * 4 + (2 * u + cb)
                            act.wait_ge(ri_ready, n + 1)
                            act.wait_ge(s2_ready, n + 1)
                            S.activation(sq_ring[cb][:, :, :], ps[:, 2 * cb:2 * cb + 2, :], ACT.Square,
                                         scale=1.0 / HW).then_inc(sq_ready, 1)

                        def step(j, u, next_chunk=True):
                            for cb in range(CB):
                                if next_chunk:
                                    square(j if u == 0 else j + 1, 1 - u, cb)
                                act.wait_ge(s2_ready, j * 4 + (2 * u + cb + 3))
                                S.activation(s2_ring[u][cb][:, :], s2_ring[u][cb][:, :], ACT.Sqrt).then_inc(root_ready, 1)

                        for i, (chunk, bank) in enumerate(EARLY_V):
                            v_out(act, i, chunk, bank)
                        for cb in range(CB):
                            square(0, 0, cb)
                        with act.Fori(0, NCH // 2 - 1) as j:
                            step(j, 0)
                            step(j, 1)
                        step(NCH // 2 - 1, 0)
                        step(NCH // 2 - 1, 1, next_chunk=False)
                        for i, (chunk, bank) in enumerate(LATE_V):
                            v_out(act, len(EARLY_V) + i, chunk, bank)
                        mask_out(act, S.copy, 1)

                    @block.gpsimd
                    def _(pool):
                        def load(j, u):
                            nc.gpsimd.dma_start(syn_ring[u][:, :], k_["syn"][:, ds(j * (2 * CHUNK) + u * CHUNK, CHUNK)]) \
                                .then_inc(syn_landed[u], 16)

                        load(0, 0)
                        load(0, 1)

                        def step(j, u, ahead=True):
                            if ahead:
                                pool.wait_ge(ri_ready, j * 4 + (2 * u + 2))
                                pool.sem_inc(syn_seen, 1)
                                load(j + 1, u)
                            pool.wait_ge(high_ready, j * 4 + (2 * u + 1))
                            pool.sem_inc(high_seen, 1)
                            nc.gpsimd.tensor_tensor(lows[u][:, 0, :], s2_ring[u][0][:, :], high[u][:, 0, :].bitcast(F32),
                                                    ALU.subtract).then_inc(low_ready[0], 1)

                        with pool.Fori(0, NCH // 2 - 1) as j:
                            for u in range(2):
                                step(j, u)
                        for u in range(2):
                            step(NCH // 2 - 1, u, ahead=False)

                    @block.tensor
                    def _(pe):
                        T = nc.tensor
                        def v_unit(i, chunk, bank, before):
                            if before:
                                pe.wait_ge(late_v_out, before)
                            for kb in range(CB):
                                m = T.matmul(ps[:, bank, :], wvs[:, kb, P:2 * P], xs[:, kb, chunk * CHUNK:(chunk + 1) * CHUNK],
                                             start=kb == 0, stop=kb == CB - 1)
                            m.then_inc(late_v_psum, 1)

                        for i, (chunk, bank) in enumerate(EARLY_V):
                            v_unit(i, chunk, bank, i - 1 if i > 1 else 0)
                            if i == 0:
                                pe.wait_ge(sel_landed, 16)
                                pe.wait_ge(coef_ready, 1)
                                for i in range(2):
                                    m = T.matmul(ps[0:STACK, 4, i * C:(i + 1) * C], sel[:, i, :], coef, start=True, stop=True)
                                m.then_inc(summed, 1)

                        pe.wait_ge(stack_ready, 1)
                        pe.sem_inc(q_ready, 2)

                        def parts(j, u):
                            pe.wait_ge(syn_landed[u], j * 16 + 16)
                            for cb in range(CB):
                                n = j * 4 + (2 * u + cb)
                                pe.wait_ge(sq_ready, n + 1)
                                c = slice(cb * P, (cb + 1) * P)
                                for i in range(2):
                                    m = T.matmul(ps[:, 2 * cb + i, :], stack[:, i, c], syn_ring[u][:, :], start=True, stop=True)
                                m.then_inc(ri_ready, 1)

                        def queries(j, u):
                            for cb in range(CB):
                                pe.wait_ge(low_ready[cb], j * 2 + (u + 3))
                            pe.wait_ge(q_free, j * 2 + (u + 1))
                            for i in range(TPC):
                                o = ps[:, 4 + 2 * u + i // 2, (i % 2) * C:(i % 2 + 1) * C]
                                T.matmul(o, ones[:, :], bqs[:, :], start=True, stop=False)
                                for kb in range(CB):
                                    for f, w in PASSES:
                                        m = T.matmul(o, (high, lows)[f][u][:, kb, i * P:(i + 1) * P],
                                                     wq[:, w, kb, :], start=False,
                                                     stop=kb == CB - 1 and (f, w) == PASSES[-1])
                            m.then_inc(q_ready, 1)

                        parts(0, 0)
                        parts(0, 1)
                        pe.wait_ge(late_v_out, len(EARLY_V))
                        with pe.Fori(0, NCH // 2 - 1) as j:
                            for u in range(2):
                                parts(j + 1, u)
                                queries(j, u)
                        for u in range(2):
                            queries(NCH // 2 - 1, u)
                        pe.wait_ge(sq_ready, 2 * NCH + 2)
                        pe.wait_ge(q_free, 2 + NCH - 1)
                        for i, (chunk, bank) in enumerate(LATE_V):
                            v_unit(len(EARLY_V) + i, chunk, bank, 0)
                        pe.wait_ge(m_ready, 1)
                        for i in range(THIRD_TILES):
                            o = ps[0:SPLITS * BLOCKS, i * P // (2 * CHUNK), :].bitcast(BF16)
                            a = i * P % (2 * CHUNK)
                            m = T.transpose(o[:, a:a + P], m_p[:, i, :, :].rearrange("p s b -> p (s b)"), identb[:, :])
                            if (i + 1) % (THIRD_TILES // MASK_BANKS) == 0:
                                m.then_inc(m_turned, 1)

            with ExitStack() as c3:
                def sb3(name, shape, dt=F32):
                    return c3.enter_context(nc.sbuf_tensor(name, shape, dt))

                SLOTS = 3
                x1_ring = [sb3(f"x1_ring{i}", [P, CB, CHUNK]) for i in range(SLOTS)]
                stage = [[sb3(f"stage{i}{h}", [P, 2, C]) for h in range(2)] for i in range(SLOTS)]
                stats = sb3("stats1", [P, CB, NCH, 6])
                mask_psum = sem("mask_psum")
                y_ready = sem("y_ready")
                y_seen = sem("y_seen")
                x1_ready = sem("x1_ready")
                stats1_done = sem("stats1_done")
                x1_turned = sem("x1_turned")
                x1_kept = sem("x1_kept")
                stage_ready = sem("stage_ready")
                zeros_ready = sem("zeros_ready")
                stored = [sem(f"stored{i}") for i in range(SLOTS)]
                edges_stored = sem("edges_stored")
                X_ROUNDS = NCH // SLOTS

                ROUNDS = NT // SLOTS
                AHEAD = 3
                MOST = (AHEAD - 1) * SLOTS
                QUAD = 4 * C
                FLOWS, LOGITS = slice(C, C + 2 * HEADS), slice(C + 2 * HEADS, NPROJ)
                SKIP = float(2 ** 20)
                ON_DVE = [(k, q) for k in range(HEADS) for q in range(3 if k < 2 else 2)]
                ON_PE = [(k, q) for k in range(HEADS) for q in range(4) if (k, q) not in ON_DVE]
                ND, NP = len(ON_DVE), len(ON_PE)

                weights = sb3("weights", [P, NT, HEADS, 4])
                wsum = sb3("wsum", [P, NT])
                index = sb3("index", [P, NT, HEADS])
                wps = sb3("wps", [P, CB, NPROJ])
                nmr_wide = sb3("nmr_wide", [P, CB, P])
                ones_row = sb3("ones_row", [P, P])
                bias_row = sb3("bias_row", [1, NPROJ])
                bias = sb3("bias", [P, NPROJ])
                grid = sb3("grid", [P, NT, 2 * HEADS])
                x_group = sb3("x_group", [P, CB, SLOTS * P])
                zeros = x_group[0:W, 0, 0:C]
                logit = sb3("logit", [P, MOST, HEADS])
                pos = sb3("pos", [P, MOST, 2 * HEADS])
                low = sb3("low", [P, MOST, 2 * HEADS])
                base = sb3("base", [P, MOST, 2 * HEADS])
                off = sb3("off", [P, MOST, 2 * HEADS])
                far = sb3("far", [P, MOST, 2 * HEADS])
                tent = [sb3(f"tent{i}", [P, MOST, 2 * HEADS]) for i in range(2)]
                row = sb3("row", [P, MOST, HEADS])
                top = sb3("top", [P, MOST])
                expo = sb3("expo", [P, MOST, HEADS])
                total = sb3("total", [P, MOST])
                share = sb3("share", [P, MOST])
                wy = [sb3(f"wy{i}", [P, MOST, HEADS]) for i in range(2)]
                used = [0]

                def from_v(*shape):
                    n = int(np.prod(shape))
                    a = v[:, :, :].rearrange("p c n -> p (c n)")[:, used[0]:used[0] + n]
                    used[0] += n
                    assert used[0] <= CB * HW
                    return a if len(shape) == 1 else a.rearrange("p (a n) -> p a n", n=shape[1])

                quad = [[from_v(QUAD) for _ in range(HEADS)] for _ in range(SLOTS)]
                idx = [sb3(f"idx{i}", [P, HEADS], U32) for i in range(SLOTS)]
                diag = [[from_v(P) for _ in range(NP)] for _ in range(SLOTS)]
                diag_sum = [from_v(P) for _ in range(SLOTS)]
                acc = [from_v(2, C) for _ in range(SLOTS)]
                sample = [from_v(CB, P) for _ in range(SLOTS)]
                ob = [from_v(CB, P) for _ in range(SLOTS)]

                grid_landed = sem("grid_landed")
                quads_clear = sem("quads_clear")
                mean1_in = sem("mean1_in")
                mean1_out = sem("mean1_out")
                var1_in = sem("var1_in")
                var1_out = sem("var1_out")
                std1_in = sem("std1_in")
                std1_out = sem("std1_out")
                wide_ready = sem("wide_ready")
                wps_ready = sem("wps_ready")
                bias_out = sem("bias_out")
                bias_ready = sem("bias_ready1")
                x_ready = sem("x_ready")
                flow_psum = sem("flow_psum")
                flow_ready = sem("flow_ready")
                flow_step = sem("flow_step")
                pool_step = sem("pool_step")
                off_ready = sem("off_ready")
                first_found = sem("first_found")
                dist_ready = sem("dist_ready")
                tent_ready = sem("tent_ready")
                expo_in = sem("expo_in")
                expo_out = sem("expo_out")
                weights_ready = sem("weights_ready")
                landed = [[sem(f"landed{i}_{k}") for k in range(HEADS)] for i in range(SLOTS)]
                idx_ready = sem("idx_ready")
                idx_seen = sem("idx_seen")
                added = sem("added")
                diag_ready = sem("diag_ready")
                combined = sem("combined")
                sample_ready = sem("sample_ready")
                projected = sem("projected")
                out_ready = sem("out_ready")
                written = [sem(f"written{i}") for i in range(SLOTS)]

                def rounds(eng, step):
                    step(0, True, True)
                    step(1, True, True)
                    with eng.Fori(2, ROUNDS - AHEAD) as j:
                        step(j, True, True)
                    step(ROUNDS - AHEAD, False, True)
                    for j in range(ROUNDS - AHEAD + 1, ROUNDS):
                        step(j, False, False)

                def corners(E, g, chain):
                    r = slice(0, group_tiles(g)[1])
                    chain(E.tensor_scalar(low[:, r, :], pos[:, r, :], -0.5, 0.0, ALU.add, ALU.max))
                    chain(E.tensor_scalar(base[:, r, :], low[:, r, :], W - 2.0, ROUND, ALU.min, ALU.add))
                    chain(E.tensor_scalar(low[:, r, :], base[:, r, :], 1.0, -ROUND, ALU.mult, ALU.add))

                def distances(E, g, chain):
                    r = slice(0, group_tiles(g)[1])
                    chain(E.tensor_tensor(off[:, r, :], low[:, r, :], pos[:, r, :], ALU.subtract))

                def indices(E, g, chain):
                    t0, n = group_tiles(g)
                    r = slice(0, n)

                    def c(x, i):
                        return x[:, r, :].rearrange("p t (k c) -> p (t k) c", c=2)[:, :, i]

                    chain(E.tensor_scalar(base[:, r, :], off[:, r, :], 1.0, 1.0, ALU.mult, ALU.add))
                    chain(E.tensor_tensor(far[:, r, :], off[:, r, :], base[:, r, :], ALU.mult))
                    rows = row[:, r, :].rearrange("p t k -> p (t k)")
                    chain(E.tensor_scalar(rows, c(low, 1), float(W), float(W), ALU.mult, ALU.add))
                    chain(E.tensor_tensor(rows, rows, c(low, 0), ALU.add))
                    chain(E.tensor_scalar(far[:, r, :], far[:, r, :], 2.0, SKIP, ALU.is_gt, ALU.mult))
                    chain(E.tensor_tensor(rows, rows, c(far, 0), ALU.add))
                    chain(E.tensor_tensor(index[:, ds(t0, n), :].rearrange("p t k -> p (t k)"), rows, c(far, 1), ALU.add))

                def flow_bank(g):
                    return (1, 3)[g] if isinstance(g, int) and g < 2 else 7

                def later(t):
                    return not (isinstance(t, int) and t < SLOTS)

                def group_tiles(g):
                    if isinstance(g, int) and g < 2:
                        return ((0, SLOTS), (SLOTS, MOST))[g]
                    return g * SLOTS + SLOTS, SLOTS

                with nc.Block(no_gpsimd_drain=True) as block:
                    @block.sync
                    def _(sp):
                        sp.dma_start(bias_row[:, :], bp.rearrange("(a n) -> a n", a=1)).then_inc(grid_landed, 16)
                        sp.dma_start(grid[:, :, :], k_["grid"]).then_inc(grid_landed, 16)
                        sp.wait_ge(zeros_ready, 1)
                        sp.dma_start(table[0:W, 0:C], zeros).then_inc(edges_stored, 16)
                        sp.dma_start(table[HW:HW + W, C:2 * C], zeros).then_inc(edges_stored, 16)
                        with sp.Fori(0, X_ROUNDS) as j:
                            for u in range(SLOTS):
                                for h in range(2):
                                    sp.wait_ge(stage_ready, j * (2 * SLOTS) + (2 * u + h + 3))
                                    r = j * (SLOTS * CHUNK) + (u * CHUNK + h * 2 * P)
                                    sp.dma_start(table[ds(r + W, 2 * P), 0:C].rearrange("(a p) c -> p a c", p=P),
                                                 stage[u][h][:, :, :]).then_inc(stored[u], 16)
                                    sp.dma_start(table[ds(r, 2 * P), C:2 * C].rearrange("(a p) c -> p a c", p=P),
                                                 stage[u][h][:, :, :]).then_inc(stored[u], 16)

                        with sp.Fori(0, ROUNDS) as j:
                            for u in range(SLOTS):
                                sp.wait_ge(out_ready, j * SLOTS + (u + 1))
                                sp.dma_start(out_c[:, :, ds(j * (SLOTS * P) + u * P, P)], ob[u][:, :, :]).then_inc(written[u], 16)
                        for u in range(SLOTS):
                            sp.wait_ge(written[u], 16 * ROUNDS)

                    @block.gpsimd
                    def _(pool):
                        nc.gpsimd.memset(zeros, 0.0).then_inc(zeros_ready, 1)
                        with pool.Fori(0, X_ROUNDS) as j:
                            for u in range(SLOTS):
                                pool.wait_ge(y_ready, j * SLOTS + (u + 1))
                                pool.sem_inc(y_seen, 1)
                                nc.gpsimd.tensor_tensor(x1_ring[u][:, :, :], xs[:, :, ds(j * (SLOTS * CHUNK) + u * CHUNK, CHUNK)],
                                                        x1_ring[u][:, :, :], ALU.add).then_inc(x1_ready, 1)

                        G = nc.gpsimd
                        for u in range(SLOTS):
                            for k in range(HEADS):
                                G.memset(quad[u][k], 0.0).then_inc(quads_clear, 1)
                        STEPS = 11

                        def find_group(g):
                            done = [0]

                            def settle():
                                pool.sem_inc(idx_seen, 1)

                            def chain(ins):
                                done[0] += 1
                                ins.then_inc(pool_step, 1)
                                pool.wait_ge(pool_step, g * STEPS + (done[0] - STEPS))
                                settle()

                            pool.wait_ge(flow_ready, g + 1)
                            settle()
                            corners(G, g, chain)
                            pool.wait_ge(dist_ready, g * 2)
                            settle()
                            distances(G, g, chain)
                            pool.sem_inc(off_ready, 1)
                            indices(G, g, chain)
                            assert done[0] == STEPS

                        def gather(t, u):
                            if later(t):
                                pool.wait_ge(combined, t + (1 - SLOTS))
                                pool.sem_inc(idx_seen, 1)
                            G.tensor_copy(idx[u][:, :], index[:, ds(t, 1), :].rearrange("p a k -> p (a k)")).then_inc(idx_ready, 1)
                            pool.wait_ge(idx_ready, t + 1)
                            pool.sem_inc(idx_seen, 1)
                            for k in range(HEADS):
                                G.indirect_dma_start(quad[u][k][:, :], None, table,
                                                     bass.IndirectOffsetOnAxis(ap=idx[u][:, k:k + 1], axis=0),
                                                     bounds_check=HW + W - 1, oob_is_err=False) \
                                    .then_inc(landed[u][k], 16)

                        def step(j, begin, finish):
                            for u in range(SLOTS):
                                gather(j * SLOTS + u, u)
                            if finish:
                                find_group(j + 1)

                        pool.wait_ge(first_found, 1)
                        for u in range(len(stored)):
                            pool.wait_ge(stored[u], 64 * (NCH // len(stored)))
                        pool.wait_ge(edges_stored, 32)
                        pool.wait_ge(quads_clear, SLOTS * HEADS)
                        rounds(pool, step)

                    @block.vector
                    def _(dve):
                        V = nc.vector

                        def stat(i, u):
                            dve.wait_ge(x1_ready, i + 1)
                            for cb in range(CB):
                                V.bn_stats(stats[:, cb, ds(i, 1), :], x1_ring[u][:, cb, :]).then_inc(stats1_done, 1)

                        def product(i, u):
                            dve.wait_ge(mask_psum, i + 1)
                            if not isinstance(i, int):
                                dve.wait_ge(stats1_done, i * 2 + 2 * (1 - SLOTS))
                                dve.wait_ge(x1_turned, i * 2 + 2 * (1 - SLOTS))
                                dve.wait_ge(x1_kept, i + (1 - SLOTS))
                            V.scalar_tensor_tensor(x1_ring[u][:, :, :], ps[:, 2 * u:2 * u + 2, :], 1.0,
                                                   v[:, :, ds(i * CHUNK, CHUNK)], ALU.add, ALU.mult).then_inc(y_ready, 1)

                        for u in range(SLOTS):
                            product(u, u)
                        with dve.Fori(1, X_ROUNDS) as j:
                            for u in range(SLOTS):
                                stat(j * SLOTS + (u - SLOTS), u)
                                product(j * SLOTS + u, u)
                        for u in range(SLOTS):
                            stat(NCH - SLOTS + u, u)
                        dve.wait_ge(stats1_done, 2 * NCH)
                        for t in range(CB):
                            V.bn_aggr(column("mv")[:, 2 * t:2 * t + 2], stats[:, t, :, :].rearrange("p a b -> p (a b)")) \
                                .then_inc(mean1_in, 1)

                        V.memset(ones_row[:, :], 1.0).then_inc(wide_ready, 1)
                        dve.wait_ge(mean1_out, 1)
                        dve.wait_ge(mean1_in, CB)
                        mv = column("mv").rearrange("p (t k) -> p k t", k=2)
                        link(dve, V.tensor_copy(column("mg"), ps[:, 0, 0:2]))
                        link(dve, V.tensor_tensor(column("d"), mv[:, 0, :], column("mg"), ALU.subtract))
                        link(dve, V.tensor_tensor(column("mean"), column("d"), column("d"), ALU.mult))
                        V.tensor_tensor(column("e"), column("mean"), mv[:, 1, :], ALU.add).then_inc(var1_in, 1)
                        dve.wait_ge(var1_out, 1)
                        V.tensor_scalar(column("var1"), ps[:, 0, 2:4], EPS, None, ALU.add).then_inc(std1_in, 1)
                        dve.wait_ge(std1_out, 1)
                        link(dve, V.reciprocal(column("rstd1"), column("mean1")))
                        for t in range(CB):
                            V.tensor_scalar(wps[:, t, FLOWS], wp[:, t, FLOWS], column("rstd1")[:, t:t + 1], W / (W - 1.0),
                                            ALU.mult, ALU.mult).then_inc(wps_ready, 1)
                        for cols in (LOGITS, slice(0, C)):
                            for t in range(CB):
                                V.tensor_scalar(wps[:, t, cols], wp[:, t, cols], column("rstd1")[:, t:t + 1], None,
                                                ALU.mult).then_inc(wps_ready, 1)
                        link(dve, V.scalar_tensor_tensor(column("nmr1"), column("mg"), -1.0, column("rstd1"), ALU.mult, ALU.mult))
                        dve.wait_ge(wide_ready, 1)
                        for t in range(CB):
                            V.tensor_scalar(nmr_wide[:, t, :], ones_row[:, :], column("nmr1")[:, t:t + 1], None,
                                            ALU.mult).then_inc(wide_ready, 1)
                        dve.wait_ge(bias_out, 1)
                        link(dve, V.tensor_copy(bias[:, C:NPROJ], ps[:, 2, C:NPROJ]))
                        dve.wait_ge(grid_landed, 32)
                        link(dve, V.scalar_tensor_tensor(grid[:, :, :], bias[:, None, FLOWS].broadcast_to([P, NT, 2 * HEADS]),
                                                         W / (W - 1.0), grid[:, :, :], ALU.mult, ALU.add))
                        STEPS = 14

                        def chain(g, i, ins):
                            ins.then_inc(flow_step, 1)
                            dve.wait_ge(flow_step, g * STEPS + (i + 1))

                        def begin_group(g):
                            t0, n = group_tiles(g)
                            r = slice(0, n)
                            dve.wait_ge(flow_psum, g + 1)
                            both = ps[:, flow_bank(g), 0:n * NFLOW].rearrange("p (t f) -> p t f", f=NFLOW)
                            chain(g, 0, V.tensor_tensor(pos[:, r, :], both[:, :, 0:2 * HEADS], grid[:, ds(t0, n), :], ALU.add))
                            chain(g, 1, V.tensor_tensor(logit[:, r, :], both[:, :, 2 * HEADS:NFLOW],
                                                        bias[:, None, LOGITS].broadcast_to([P, n, HEADS]), ALU.add))
                            dve.sem_inc(flow_ready, 1)
                            chain(g, 2, V.tensor_reduce(top[:, r], logit[:, r, :], AX_X, ALU.max))
                            chain(g, 3, V.tensor_tensor(expo[:, r, :], logit[:, r, :], top[:, r, None].broadcast_to([P, n, HEADS]),
                                                        ALU.subtract))
                            dve.sem_inc(expo_in, 1)

                        def finish_group(g):
                            t0, n = group_tiles(g)
                            r = slice(0, n)
                            dve.wait_ge(expo_out, g + 1)
                            chain(g, 4, V.tensor_reduce(total[:, r], expo[:, r, :], AX_X, ALU.add))
                            chain(g, 5, V.reciprocal(share[:, r], total[:, r]))
                            chain(g, 6, V.tensor_tensor(expo[:, r, :], expo[:, r, :], share[:, r, None].broadcast_to([P, n, HEADS]),
                                                        ALU.mult))
                            dve.wait_ge(tent_ready, g * 2 + 2)
                            side = [tent[i][:, r, :].rearrange("p t (k c) -> p (t k) c", c=2) for i in range(2)]
                            for i in range(2):
                                chain(g, 7 + i, V.tensor_tensor(wy[i][:, r, :].rearrange("p t k -> p (t k)"), side[i][:, :, 1],
                                                                expo[:, r, :].rearrange("p t k -> p (t k)"), ALU.mult))
                            here = weights[:, ds(t0, n), :, :]
                            w4 = here.rearrange("p t k q -> p (t k) q")
                            for i in range(2):
                                for k in range(2):
                                    chain(g, 9 + 2 * i + k, V.tensor_tensor(w4[:, :, 2 * i + k], side[i][:, :, 0],
                                                                            wy[k][:, r, :].rearrange("p t k -> p (t k)"), ALU.mult))
                            chain(g, 13, V.tensor_reduce(wsum[:, ds(t0, n)], here.rearrange("p t k q -> p t (k q)"), AX_X, ALU.add))
                            dve.sem_inc(weights_ready, 1)

                        def add(j, u):
                            t = j * SLOTS + u
                            sums = [ps[:, 6, i * C:(i + 1) * C] for i in range(2)]
                            for n, (k, q) in enumerate(ON_DVE):
                                if n == 0 or ON_DVE[n - 1][0] != k:
                                    dve.wait_ge(landed[u][k], j * 16 + 16)
                                src = quad[u][k][:, q * C:(q + 1) * C]
                                w = weights[:, ds(t, 1), k, q]
                                s = sums[n % 2]
                                o = acc[u][:, n % 2, :] if n >= ND - 2 else s
                                if not (isinstance(t, int) and t == 0 and n < 2):
                                    dve.wait_ge(added, t * ND + (n - 1))
                                if n == ND - 2 and later(t):
                                    dve.wait_ge(combined, t + (1 - SLOTS))
                                if n < 2:
                                    V.tensor_scalar(o, src, w, None, ALU.mult).then_inc(added, 1)
                                else:
                                    V.scalar_tensor_tensor(o, src, w, s, ALU.mult, ALU.add).then_inc(added, 1)

                        def step(j, begin, finish):
                            for u in range(SLOTS):
                                add(j, u)
                            if finish:
                                finish_group(j + 1)
                            if begin:
                                begin_group(j + 2)

                        begin_group(0)
                        corners(V, 0, lambda ins: link(dve, ins))
                        distances(V, 0, lambda ins: link(dve, ins))
                        dve.sem_inc(off_ready, 1)
                        indices(V, 0, lambda ins: link(dve, ins))
                        dve.sem_inc(first_found, 1)
                        dve.wait_ge(bias_out, 2)
                        V.tensor_copy(bias[:, 0:C], ps[:, 4, 0:C]).then_inc(bias_ready, 1)
                        finish_group(0)
                        begin_group(1)
                        rounds(dve, step)

                    @block.scalar
                    def _(act):
                        S = nc.scalar

                        def leave(j, u):
                            i = j * SLOTS + u
                            act.wait_ge(x1_ready, i + 1)
                            S.copy(xs[:, :, ds(i * CHUNK, CHUNK)], x1_ring[u][:, :, :]).then_inc(x1_kept, 1)
                            if isinstance(i, int) and i == NCH - 1:
                                act.wait_ge(std1_in, 1)
                                S.activation(column("mean1"), column("var1"), ACT.Sqrt).then_inc(std1_out, 1)
                            for h in range(2):
                                act.wait_ge(x1_turned, i * 2 + (h + 1))
                                if h == 0 and not (isinstance(j, int) and j == 0):
                                    act.wait_ge(stored[u], j * 64)
                                S.copy(stage[u][h][:, :, :].rearrange("p a c -> p (a c)"), ps[:, 6 + h, :]) \
                                    .then_inc(stage_ready, 1)

                        for u in range(SLOTS):
                            leave(0, u)
                        with act.Fori(1, X_ROUNDS - 1) as j:
                            for u in range(SLOTS):
                                leave(j, u)
                        for u in range(SLOTS):
                            leave(X_ROUNDS - 1, u)


                        def tents(g):
                            _, n = group_tiles(g)
                            r = slice(0, n)
                            act.wait_ge(off_ready, g + 1)
                            if not (isinstance(g, int) and g == 0):
                                act.wait_ge(weights_ready, g)
                            S.activation(tent[0][:, r, :], off[:, r, :], ACT.Abs).then_inc(dist_ready, 1)
                            S.activation(tent[1][:, r, :], off[:, r, :], ACT.Abs, bias=column("one")).then_inc(dist_ready, 1)
                            act.wait_ge(dist_ready, g * 2 + 2)
                            for i in range(2):
                                S.activation(tent[i][:, r, :], tent[i][:, r, :], ACT.Relu, scale=-1.0, bias=column("one")) \
                                    .then_inc(tent_ready, 1)
                            act.wait_ge(expo_in, g + 1)
                            S.activation(expo[:, r, :], expo[:, r, :], ACT.Exp).then_inc(expo_out, 1)

                        def copy_group(g):
                            t0, n = group_tiles(g)
                            act.wait_ge(flow_psum, g)
                            S.copy(x_group[:, :, :], xs[:, :, ds(t0 * P, n * P)]).then_inc(x_ready, 1)

                        def diags(t, u):
                            if later(t):
                                act.wait_ge(combined, t + (1 - SLOTS))
                            for n, (k, q) in enumerate(ON_PE):
                                S.activation(diag[u][n][:, :], ident[:, :], ACT.Copy, scale=weights[:, ds(t, 1), k, q]) \
                                    .then_inc(diag_ready, 1)
                            if later(t):
                                act.wait_ge(projected, t + (1 - SLOTS))
                            S.activation(diag_sum[u][:, :], ident[:, :], ACT.Copy, scale=wsum[:, ds(t, 1)]).then_inc(diag_ready, 1)

                        def keep(t, u):
                            act.wait_ge(combined, t + 1)
                            S.copy(sample[u][:, :, :], ps[:, 2 * u:2 * u + 2, 0:P]).then_inc(sample_ready, 1)

                        def result(j, t, u):
                            act.wait_ge(projected, t + 1)
                            if later(t):
                                act.wait_ge(written[u], j * 16)
                            S.copy(ob[u][:, :, :], ps[:, 2 * u:2 * u + 2, P:2 * P]).then_inc(out_ready, 1)

                        def step(j, begin, finish):
                            for u in range(SLOTS):
                                t = j * SLOTS + u
                                if isinstance(t, int) and t == SLOTS - 1:
                                    act.wait_ge(weights_ready, 2)
                                if isinstance(t, int) and t == (ROUNDS - 1) * SLOTS - 1:
                                    act.wait_ge(weights_ready, ROUNDS - AHEAD + 2)
                                if not (isinstance(t, int) and t == NT - 1):
                                    diags(t + 1, (u + 1) % SLOTS)
                                keep(t, u)
                                if not (isinstance(t, int) and t == 0):
                                    result(j + (-1 if u == 0 else 0), t + -1, (u - 1) % SLOTS)
                                if u == 0 and begin:
                                    copy_group(j + 2)
                                if u == 1 and finish:
                                    tents(j + 1)

                        tents(0)
                        act.wait_ge(weights_ready, 1)
                        diags(0, 0)
                        rounds(act, step)
                        result(ROUNDS - 1, NT - 1, SLOTS - 1)

                    @block.tensor
                    def _(pe):
                        T = nc.tensor

                        def spread(t, j, u):
                            for cb in range(CB):
                                m = T.matmul(ps[:, 2 * u + cb, :], pick[:, ds(t, 1), cb * P:(cb + 1) * P].rearrange("p a n -> p (a n)"),
                                             mask[:, ds(j * (SLOTS * CHUNK) + u * CHUNK, CHUNK)], start=True, stop=True)
                            m.then_inc(mask_psum, 1)

                        def turn(i, u):
                            pe.wait_ge(x1_ready, i + 1)
                            for h in range(2):
                                pe.wait_ge(stage_ready, i * 2 + (h + 1))
                                for a in range(2):
                                    for cb in range(CB):
                                        n = (2 * h + a) * P
                                        m = T.transpose(ps[:, 6 + h, a * C + cb * P:a * C + (cb + 1) * P],
                                                        x1_ring[u][:, cb, n:n + P], ident[:, :])
                                m.then_inc(x1_turned, 1)

                        pe.sem_inc(stage_ready, 2)
                        per = X_ROUNDS // 3

                        def group_means():
                            pe.wait_ge(mean1_in, CB)
                            T.matmul(ps[:, 0, 0:2], group[:, :], column("mv").rearrange("p (t k) -> p k t", k=2)[:, 0, :],
                                     start=True, stop=True).then_inc(mean1_out, 1)

                        def third(t, last):
                            for r in range(per):
                                for u in range(SLOTS):
                                    if last and r == per - 1 and u == SLOTS - 1:
                                        group_means()
                                    turn(t * (per * SLOTS) + (r * SLOTS + u), u)
                                    if r < per - 1:
                                        spread(t, r + 1, u)
                                    elif not last:
                                        spread(t + 1, 0, u)

                        for u in range(SLOTS):
                            spread(0, 0, u)
                        with pe.Fori(0, 2) as t:
                            third(t, False)
                        third(2, True)

                        pe.wait_ge(var1_in, 1)
                        T.matmul(ps[:, 0, 2:4], group[:, :], column("e"), start=True, stop=True).then_inc(var1_out, 1)

                        def flows(g, source):
                            t0, n = group_tiles(g)
                            if source is x_group:
                                t0 = 0
                            for t in range(n):
                                for kb in range(CB):
                                    m = T.matmul(ps[:, flow_bank(g), t * NFLOW:(t + 1) * NFLOW], source[:, kb, (t0 + t) * P:(t0 + t + 1) * P],
                                                 wps[:, kb, C:NPROJ], start=kb == 0, stop=kb == CB - 1)
                            m.then_inc(flow_psum, 1)

                        pe.wait_ge(wps_ready, 2 * CB)
                        pe.wait_ge(x1_kept, NCH)
                        flows(0, xs)

                        def broadcast_bias(cols, bank):
                            o = ps[:, bank, cols]
                            for kb in range(CB):
                                T.matmul(o, nmr_wide[:, kb, :], wp[:, kb, cols], start=kb == 0, stop=False)
                            T.matmul(o, ones_row[0:1, :], bias_row[:, cols], start=False, stop=True).then_inc(bias_out, 1)

                        pe.wait_ge(wide_ready, 1 + CB)
                        pe.wait_ge(grid_landed, 32)
                        broadcast_bias(slice(C, NPROJ), 2)
                        flows(1, xs)
                        broadcast_bias(slice(0, C), 4)
                        pe.wait_ge(bias_ready, 1)
                        pe.wait_ge(wps_ready, 3 * CB)

                        def combine(j, u):
                            t = j * SLOTS + u
                            if later(t):
                                pe.wait_ge(out_ready, t + (1 - SLOTS))
                            o = [ps[:, 2 * u + cb, 0:P] for cb in range(CB)]
                            for n, (k, q) in enumerate(ON_PE):
                                if n == 0 or ON_PE[n - 1][0] != k:
                                    pe.wait_ge(landed[u][k], j * 16 + 16)
                                pe.wait_ge(diag_ready, t * (NP + 1) + (n + 1))
                                for cb in range(CB):
                                    T.matmul(o[cb], quad[u][k][:, q * C + cb * P:q * C + (cb + 1) * P], diag[u][n][:, :],
                                             start=n == 0, stop=False)
                            for i in range(2):
                                pe.wait_ge(added, t * ND + (ND - 1 + i))
                                for cb in range(CB):
                                    m = T.matmul(o[cb], acc[u][:, i, cb * P:(cb + 1) * P], ident[:, :],
                                                 start=False, stop=i == 1)
                            m.then_inc(combined, 1)

                        def project(t, u):
                            o = [ps[:, 2 * u + cb, P:2 * P] for cb in range(CB)]
                            pe.wait_ge(sample_ready, t + 1)
                            for cb in range(CB):
                                T.matmul(o[cb], ident[:, :], xs[:, cb, ds(t * P, P)], start=True, stop=False)
                            pe.wait_ge(diag_ready, t * (NP + 1) + (NP + 1))
                            for cb in range(CB):
                                T.matmul(o[cb], bias[:, cb * P:(cb + 1) * P], diag_sum[u][:, :], start=False, stop=False)
                            for cb in range(CB):
                                for kb in range(CB):
                                    m = T.matmul(o[cb], wps[:, kb, cb * P:(cb + 1) * P], sample[u][:, kb, :],
                                                 start=False, stop=kb == CB - 1)
                            m.then_inc(projected, 1)

                        def step(j, begin, finish):
                            for u in range(SLOTS):
                                t = j * SLOTS + u
                                combine(j, u)
                                if not (isinstance(t, int) and t == 0):
                                    project(t + -1, (u - 1) % SLOTS)
                                if u == 1 and begin:
                                    pe.wait_ge(x_ready, j + 1)
                                    pe.wait_ge(flow_ready, j + 2)
                                    flows(j + 2, x_group)

                        rounds(pe, step)
                        project(NT - 1, SLOTS - 1)


def kernel(**inputs):
    import concourse.bacc as _bacc
    from concourse import mybir as _mybir
    from concourse.bass_utils import run_bass_kernel_spmd as _run

    g = {n: np.asarray(a) for n, a in inputs.items()}
    laid = {
        "x": g["x"],
        "WqT": g["L0_conv_Wq"].T, "bq": g["L0_conv_bq"],
        "WvT": g["L0_conv_Wv"].T, "bv": g["L0_conv_bv"].reshape(CB, P).T,
        "WpT": np.concatenate([g["L1_conv_Wc"], g["L1_conv_Woff"].reshape(2 * HEADS, C), g["L1_conv_Wwt"]]).T,
        "bp": np.concatenate([g["L1_conv_bc"], g["L1_conv_boff"].reshape(-1), g["L1_conv_bwt"]]),
    }
    nc = _bacc.Bacc("TRN2", target_bir_lowering=False, num_devices=1)
    arrays, args = {}, []
    for name, a in laid.items():
        a = np.ascontiguousarray(a)
        arrays[f"in_{name}_dram"] = a
        args.append(nc.dram_tensor(f"in_{name}_dram", a.shape, _mybir.dt.from_np(a.dtype), kind="ExternalInput").ap())
    args.append(nc.dram_tensor("out_0_dram", (1, C, H, W), _mybir.dt.from_np(np.dtype("float32")),
                               kind="ExternalOutput").ap())
    build(nc, *args)
    r = _run(nc, [arrays], core_ids=[0])
    return r.results[0]["out_0_dram"]
```
